# Optimizing a Trainium2 kernel written in Bass

```python
import numpy as np
import jax
import jax.numpy as jnp

def _softmax(x, axis=-1):
    return jax.nn.softmax(x, axis=axis)

def _gelu(x):
    return jax.nn.gelu(x, approximate=True)

def _silu(x):
    return jax.nn.silu(x)

def _sigmoid(x):
    return jax.nn.sigmoid(x)

def _layernorm(x, axis=-1, eps=1e-05):
    m = jnp.mean(x, axis=axis, keepdims=True)
    v = jnp.var(x, axis=axis, keepdims=True)
    return (x - m) / jnp.sqrt(v + eps)

def _scatter_add(tgt, idx, src, axis=0):
    return tgt.at[idx].add(src)

def _segment_sum(src, seg, n):
    return jax.ops.segment_sum(src, seg, n)
kernel_name = 'mk_xattn_ffn_d1_seqx_r4_355d5a'

def setup_inputs(seed: int=0):
    np.random.seed(seed)
    _w = jnp.asarray

    def _rec_inputs():
        import jax
        import jax.numpy as jnp
        _rk = jax.random.key(seed)
        x = -0.0002928 + 1 * jax.random.normal(jax.random.fold_in(_rk, 1), (32, 128, 256), jnp.float32)
        _lenS = 128 - jax.random.randint(jax.random.fold_in(_rk, 7), (32,), 0, max(1, 128 // 4) + 1, jnp.int32)
        _lenS2 = 128 - jax.random.randint(jax.random.fold_in(_rk, 8), (32,), 0, max(1, 128 // 4) + 1, jnp.int32)
        _ctx_1024P = jax.random.normal(jax.random.fold_in(_rk, 11), (32, 16, 256), jnp.float32)
        _ctx_1024c = jax.random.dirichlet(jax.random.fold_in(_rk, 511), 0.3 * jnp.ones((16,), jnp.float32), (32, 128))
        _ctx_1024t = jnp.einsum('bsk,bkd->bsd', _ctx_1024c, _ctx_1024P)
        _ctx_1024t = _ctx_1024t * jax.lax.rsqrt(jnp.mean(jnp.square(_ctx_1024t)) + 1e-12) * 0.953939
        ctx_1024 = -1.39393e-06 + 0.999914 * (_ctx_1024t + 0.3 * jax.random.normal(jax.random.fold_in(_rk, 611), (32, 128, 256), jnp.float32))
        return (x, ctx_1024)
    x, ctx_1024 = _rec_inputs()

    def _L0_xattn_setup():
        import jax, jax.numpy as jnp
        import numpy as np
        N_HEADS = 16
        D_MODEL = 256
        D_K = D_MODEL // N_HEADS
        B, T = (2, 512)
        key = jax.random.key(seed)
        ks = jax.random.split(key, 12)
        s = 1.0 / np.sqrt(D_MODEL)
        inp = {'q': jax.random.normal(ks[0], (B, T, D_MODEL), jnp.float32), 'k': jax.random.normal(ks[1], (B, T, D_MODEL), jnp.float32), 'v': jax.random.normal(ks[2], (B, T, D_MODEL), jnp.float32), 'Wq': jax.random.normal(ks[3], (D_MODEL, D_MODEL), jnp.float32) * s, 'bq': jax.random.normal(ks[4], (D_MODEL,), jnp.float32) * s, 'Wk': jax.random.normal(ks[5], (D_MODEL, D_MODEL), jnp.float32) * s, 'bk': jax.random.normal(ks[6], (D_MODEL,), jnp.float32) * s, 'Wv': jax.random.normal(ks[7], (D_MODEL, D_MODEL), jnp.float32) * s, 'bv': jax.random.normal(ks[8], (D_MODEL,), jnp.float32) * s, 'Wo': jax.random.normal(ks[9], (D_MODEL, D_MODEL), jnp.float32) * s, 'bo': jax.random.normal(ks[10], (D_MODEL,), jnp.float32) * s, 'alpha': jnp.ones((1, N_HEADS, 1, 1), jnp.float32) * 10.0}
        return inp
    _L0_xattn_all = _L0_xattn_setup()
    _L0_xattn_in = {k: v for k, v in _L0_xattn_all.items() if k in ('Wq', 'bq', 'Wk', 'bk', 'Wv', 'bv', 'Wo', 'bo', 'alpha')}
    del _L0_xattn_all

    def _L0_ffn_setup():
        import jax, jax.numpy as jnp
        import numpy as np
        B, T, D, H, E, K = (2, 1024, 256, 1024, 8, 2)
        key = jax.random.key(seed)
        ks = jax.random.split(key, 5)
        scale = 0.02
        x = jax.random.normal(ks[0], (B, T, D), dtype=jnp.float32)
        Wr = jax.random.normal(ks[1], (D, E), dtype=jnp.float32) * scale
        W1 = jax.random.normal(ks[2], (E, D, H), dtype=jnp.float32) * scale
        b1 = jnp.zeros((E, H), dtype=jnp.float32)
        W2 = jax.random.normal(ks[3], (E, H, D), dtype=jnp.float32) * scale
        b2 = jnp.zeros((E, D), dtype=jnp.float32)
        return {'x': x, 'Wr': Wr, 'W1': W1, 'b1': b1, 'W2': W2, 'b2': b2}
    _L0_ffn_all = _L0_ffn_setup()
    _L0_ffn_in = {k: v for k, v in _L0_ffn_all.items() if k in ('Wr', 'W1', 'b1', 'W2', 'b2')}
    del _L0_ffn_all
    return {'x': x, 'ctx_1024': ctx_1024, 'L0_xattn_Wq': _L0_xattn_in['Wq'], 'L0_xattn_bq': _L0_xattn_in['bq'], 'L0_xattn_Wk': _L0_xattn_in['Wk'], 'L0_xattn_bk': _L0_xattn_in['bk'], 'L0_xattn_Wv': _L0_xattn_in['Wv'], 'L0_xattn_bv': _L0_xattn_in['bv'], 'L0_xattn_Wo': _L0_xattn_in['Wo'], 'L0_xattn_bo': _L0_xattn_in['bo'], 'L0_xattn_alpha': _L0_xattn_in['alpha'], 'L0_ffn_Wr': _L0_ffn_in['Wr'], 'L0_ffn_W1': _L0_ffn_in['W1'], 'L0_ffn_b1': _L0_ffn_in['b1'], 'L0_ffn_W2': _L0_ffn_in['W2'], 'L0_ffn_b2': _L0_ffn_in['b2']}

def reference(x, ctx_1024, L0_xattn_Wq, L0_xattn_bq, L0_xattn_Wk, L0_xattn_bk, L0_xattn_Wv, L0_xattn_bv, L0_xattn_Wo, L0_xattn_bo, L0_xattn_alpha, L0_ffn_Wr, L0_ffn_W1, L0_ffn_b1, L0_ffn_W2, L0_ffn_b2):
    import jax
    import jax.numpy as jnp

    def _L0_xattn_ref(q, k, v, Wq, bq, Wk, bk, Wv, bv, Wo, bo, alpha):
        import jax, jax.numpy as jnp
        import numpy as np
        N_HEADS = 16
        D_MODEL = 256
        D_K = D_MODEL // N_HEADS
        B, T = (2, 512)
        Bsz, Tlen, _ = q.shape

        def proj(x, W, b):
            y = x @ W + b
            return y.reshape(Bsz, Tlen, N_HEADS, D_K).transpose(0, 2, 1, 3)
        qh = proj(q, Wq, bq)
        kh = proj(k, Wk, bk)
        vh = proj(v, Wv, bv)
        scores = jnp.einsum('bhqd,bhkd->bhqk', qh, kh)
        norm_q = jnp.linalg.norm(qh, axis=-1)
        norm_k = jnp.linalg.norm(kh, axis=-1)
        D_udps = (norm_q[..., :, None] + norm_k[..., None, :]) ** 2
        D_safe = jnp.where(D_udps == 0.0, jnp.inf, D_udps)
        scores = alpha * 4.0 * scores / D_safe
        attn = jax.nn.softmax(scores, axis=-1)
        out = jnp.einsum('bhqk,bhkd->bhqd', attn, vh)
        out = out.transpose(0, 2, 1, 3).reshape(Bsz, Tlen, D_MODEL)
        return out @ Wo + bo

    def _L0_ffn_ref(x, Wr, W1, b1, W2, b2):
        import jax, jax.numpy as jnp
        import numpy as np
        B, T, D, H, E, K = (2, 1024, 256, 1024, 8, 2)
        logits = jnp.einsum('btd,de->bte', x, Wr)
        probs = jax.nn.softmax(logits, axis=-1)
        w, idx = jax.lax.top_k(probs, K)
        w = w / jnp.sum(w, axis=-1, keepdims=True)
        dispatch = jnp.sum(jax.nn.one_hot(idx, E, dtype=x.dtype) * w[..., None], axis=-2)
        h = jax.nn.gelu(jnp.einsum('btd,edh->ebth', x, W1) + b1[:, None, None, :], approximate=False)
        y = jnp.einsum('ebth,ehd->ebtd', h, W2) + b2[:, None, None, :]
        out = jnp.einsum('ebtd,bte->btd', y, dispatch)
        return out
    x = x + _L0_xattn_ref(_layernorm(x, axis=-1), ctx_1024, ctx_1024, L0_xattn_Wq, L0_xattn_bq, L0_xattn_Wk, L0_xattn_bk, L0_xattn_Wv, L0_xattn_bv, L0_xattn_Wo, L0_xattn_bo, L0_xattn_alpha)
    x = x + _L0_ffn_ref(_layernorm(x, axis=-1), L0_ffn_Wr, L0_ffn_W1, L0_ffn_b1, L0_ffn_W2, L0_ffn_b2)
    return x

_drawn_inputs = setup_inputs


def setup_inputs(seed=0):
    import zlib

    import numpy as np

    out = dict(_drawn_inputs(seed))
    spreads = {'L0_xattn_alpha': (10.0, 0.2), 'L0_ffn_b1': (0.0, 0.362), 'L0_ffn_b2': (0.0, 0.1)}
    factors = {'L0_xattn_bk': 3.395}
    for name, (base, spread) in spreads.items():
        noise = np.random.default_rng([zlib.crc32(name.encode()), seed]).standard_normal(out[name].shape)
        drawn = base * np.exp(spread * noise) if base else spread * noise
        out[name] = jnp.asarray(drawn.astype(out[name].dtype))
    for name, factor in factors.items():
        out[name] = (out[name] * factor).astype(out[name].dtype)
    return out
```

```python
from contextlib import ExitStack

import numpy as np

import concourse.bass as bass
from concourse import mybir

F32, BF16, F16, I32 = mybir.dt.float32, mybir.dt.bfloat16, mybir.dt.float16, mybir.dt.int32
ALU, ACT, AX = mybir.AluOpType, mybir.ActivationFunctionType, mybir.AxisListType

P = 128
NB, D, NH, DK = 32, 256, 16, 16
NP = NB // 2
T = NB * P
DC = D // P
NE, H = 8, 1024
HC = H // P
EPS = 1e-5
NSLOT = 2 * T // P + NE - 1
REGION = T + P
REC = D + NE + 1
NSPLIT = 3
STRIP = 32
RROWS = NSPLIT * STRIP
QW = 4 * (P // 2 + 4)
VM = P // 2 + 4
X_SCALE = 2.0 ** 11
QK_SCALE = 2.0 ** 12
ONE = 1 << 23
LN2 = float(np.log(2.0))


def build(nc, ctx, io):
    (x, c, wq, bq, wk, bk, wv, bv, wo, bo, alpha, wr, w1, b1, w2, b2, out) = io

    sems = {}

    def sem(name):
        if name not in sems:
            sems[name] = ctx.enter_context(nc.semaphore(name))
        return sems[name]

    chains = {
        "dve_norms": ["mant", "ex", "exf", "ah", "sgq", "sgk", "p0", "r2", "p1", "r3", "parts", "y2", "n2y2", "nt",
                  "rn", "coef", "unit", "lo0", "lo1"],
        "dve_route": ["rmx", "rd", "rs", "rrs", "rp", "b_mx1", "b_eq1", "b_v1", "b_vm1", "b_oh1", "rq",
                  "b_mx2", "b_eq2", "b_v2", "b_vm2", "b_oh2", "rsm", "rrm", "rv1", "rv2", "rw1", "rw2", "rw",
                  "rtok", "rtk", "rhot", "ra0", "ra1", "racc", "rpos", "rm1", "rm2", "rp1", "rp2", "ridx"],
        "dve_split": ["wcl", "wexa", "wexb", "wex", "wsc", "wlo"],
    }
    halves = range(4)
    chains["pe_scores"] = [f"{s}{n}" for n in halves for s in ("u", "su")]
    chains["act_tanh"] = [f"{s}{n}" for n in halves for s in ("th", "t2")]
    chains["dve_max"] = [f"{s}{n}" for n in halves for s in ("tw", "tm")]
    chains["pool_less_max"] = [f"sb{n}" for n in halves]
    chains["pe_turn"] = [f"{s}{n}" for n in halves for s in ("ta", "tt")]
    chains["act_exp"] = [f"ex{n}{i}" for n in halves for i in range(2)]
    chains["pe_values"] = [f"pv{n}" for n in halves]
    for b_ in range(2):
        chains[f"pe_first{b_}"] = [f"xct{b_}", f"qk{b_}", f"v{b_}"]
        chains[f"pe_stack{b_}"] = [f"stq{b_}", f"stk{b_}"]
        chains[f"dve_first{b_}"] = [f"ln{b_}st", f"ln{b_}mv", f"ln{b_}ve", f"xn{b_}", f"qke{b_}", f"ve{b_}", f"n2{b_}"]
        chains[f"dve_second{b_}"] = [f"x1{b_}", f"lm{b_}st", f"lm{b_}mv", f"lm{b_}ve", f"lm{b_}rx", f"y{b_}",
                                 f"rh{b_}", f"rl{b_}"]
    owner = lambda chain: chain.split("_")[0]
    place = {name: (chain, i, len(names)) for chain, names in chains.items() for i, name in enumerate(names)}

    def done(ins, name):
        ins.then_inc(sem(place[name][0] if name in place else name), 1)

    def landed(ins, name):
        ins.then_inc(sem(name), 16)

    def need(eng, name, count):
        if isinstance(count, int) and count <= 0 or isinstance(eng, Rehearsal):
            return
        if name in place:
            name, i, m = place[name]
            count = count * m + i + 1
        eng.wait_ge(sem(name), count)
        if eng is nc.sync and not isinstance(count, int):
            settle(eng)

    def settle(eng):
        eng.sem_inc(sem("settled"), 1)

    def need_dma(eng, name, count):
        if isinstance(count, int) and count <= 0 or isinstance(eng, Rehearsal):
            return
        eng.wait_ge(sem(name), count * 16)
        if eng is nc.sync and not isinstance(count, int):
            settle(eng)

    xrec_d = nc.dram_tensor("xrec", [NE * REGION + P, REC], I32).ap()
    acc_d = nc.dram_tensor("acc", [T + P, D], F32).ap()
    w2s_d = nc.dram_tensor("w2s", [NE, P, 2 * HC * D], F16).ap()

    def alloc(stack, name, shape, dt):
        return stack.enter_context(nc.sbuf_tensor(name, shape, dt))

    def bank(name, shape, dt):
        return ctx.enter_context(nc.psum_tensor(name, shape, dt))

    w1s = alloc(ctx, "w1s", [P, NE, 2, DC, H], F16)
    id16 = alloc(ctx, "id16", [P, P], F16)
    ones_f = alloc(ctx, "ones_f", [P, P], F32)
    k1 = alloc(ctx, "k1", [P, NE], I32)
    k2 = alloc(ctx, "k2", [P, NE], I32)
    kb = alloc(ctx, "kb", [P, NE], I32)
    b1t = alloc(ctx, "b1t", [P, NE, HC], F32)
    acc_cnt = alloc(ctx, "acc_cnt", [P, NE], BF16)
    ebase = alloc(ctx, "ebase", [P, 2, NE], F32)
    cnt_keep = alloc(ctx, "cnt_keep", [P, NE], F32)
    ones_b = alloc(ctx, "ones_b", [P, P], BF16)

    s_ps = bank("s_ps", [P, 2, 512], F32)
    u_ps = bank("u_ps", [P, 1024], F32)
    pv_ps = bank("pv_ps", [P, 512], F32)
    gen = [bank(f"gen{i}", [P, 512], F32) for i in range(3)]

    class Turns:
        section, n, freed, given = 0, 0, [None] * 3, {}

    class Rehearsal:
        def __getattr__(self, _):
            return lambda *args, **kw: self

    def start_section(k, freed=(None,) * 3):
        Turns.section, Turns.n, Turns.freed = k, 0, list(freed)

    def turn(pe, what, name, count):
        i = Turns.n % 3
        Turns.n += 1
        if Turns.freed[i]:
            need(pe, *Turns.freed[i])
        Turns.freed[i] = (name, count)
        Turns.given[Turns.section, what] = gen[i]
        return gen[i]

    def given(what):
        return Turns.given[Turns.section, what]

    with ExitStack() as a:
        wq_sb = alloc(a, "wq_sb", [P, DC, D], F32)
        wk_sb = alloc(a, "wk_sb", [P, DC, D], F32)
        wv_sb = alloc(a, "wv_sb", [P, DC, D], F32)
        wo_sb = alloc(a, "wo_sb", [P, DC, D], F32)
        wr_sb = alloc(a, "wr_sb", [P, DC, NE], F32)
        bqk = alloc(a, "bqk", [P, 2 * D], F32)
        bv_sb = alloc(a, "bv_sb", [P, D], F32)
        bo_sb = alloc(a, "bo_sb", [P, D], F32)
        al = alloc(a, "al", [P, NH], F32)
        amax = alloc(a, "amax", [P, 1], F32)
        abig = alloc(a, "abig", [P, 1], I32)
        arec = alloc(a, "arec", [P, 1], I32)
        escale = alloc(a, "escale", [P, 1], F32)
        colscale = alloc(a, "colscale", [P, 2 * NH], F32)
        idf = alloc(a, "idf", [P, P], F32)
        idb = alloc(a, "idb", [P, P], BF16)
        lstrict = alloc(a, "lstrict", [P, P], BF16)
        rank8 = alloc(a, "rank8", [P, 2, NE], F32)
        padrec = alloc(a, "padrec", [P, REC], I32)
        zrow = alloc(a, "zrow", [P, D], F32)
        mhalf = alloc(a, "mhalf", [P, 1], F32)
        io8 = alloc(a, "io8", [P, 2, NE], I32)
        tok = alloc(a, "tok", [P, 1], I32)
        wl = alloc(a, "wl", [P, 2048], F32)
        wst = alloc(a, "wst", [P, 2, 2048], F16)
        wss = alloc(a, "wss", [P, 1], F32)
        wkk = alloc(a, "wkk", [P, 1], I32)
        wsc = alloc(a, "wsc", [P, 1], I32)
        wcl = alloc(a, "wcl", [P, 1], F32)
        pair = lambda name, shape, dt: [alloc(a, f"{name}{b}", shape, dt) for b in range(2)]
        xin, cin, xn = pair("xin", [P, D], F32), pair("cin", [P, D], F32), pair("xn", [P, D], F32)
        xct = pair("xct", [P, 2 * DC, P], F32)
        norm_bufs = {name: [[alloc(a, f"{name}{b}_{k}", [P, w], F32) for k, w in (("st6", 6), ("mv", 2), ("var", 1), ("rstd", 1))]
                            for b in range(2)] for name in ("ln", "lm")}
        qk = alloc(a, "qk", [P, 2, 2 * NH, DK], F32)
        qks = alloc(a, "qks", [P, 2, 2 * NH, DK], F32)
        vn = pair("vn", [P, D], F32)
        n2 = alloc(a, "n2", [P, 2, 2 * NH], F32)
        na = {k: alloc(a, f"na_{k}", [P, 2, 2 * NH], I32 if k in ("mant", "ex") else F32)
              for k in ("mant", "ex", "exf", "ln", "ah", "y", "y2", "n2y2", "nt", "rn", "coef", "r1", "r2")}
        ar = alloc(a, "ar", [P, 2, 2, RROWS], BF16)
        qks16 = pair("qks16", [P, 2 * NH, 4, DK], F16)
        qt, kt = pair("qt", [P, NH // 2, P], F16), pair("kt", [P, NH // 2, P], F16)
        aq = pair("aq", [RROWS + NSPLIT, P], BF16)
        kbr = pair("kbr", [RROWS, P], BF16)
        uk = pair("uk", [RROWS + NSPLIT, NH * P], BF16)
        vz = pair("vz", [P, 4, 4, VM + 16], F32)
        th, tw = pair("th", [P, 1024], F32), pair("tw", [P, 2, 4, P], F32)
        tm = pair("tm", [P, 8], F32)
        pt = pair("pt", [P, 2, 512], F32)
        osb = alloc(a, "osb", [VM, 512], F32)
        rz = alloc(a, "rz", [P, 4, 4], F32)
        on = alloc(a, "on", [P, D], F32)
        ot = alloc(a, "ot", [P, DC, P], F32)
        xres, xb = pair("xres", [P, D], F32), pair("xb", [P, D], F32)
        x1 = pair("x1", [P, D], F32)
        xn2 = pair("xn2", [P, D], F32)
        xn2t = alloc(a, "xn2t", [P, DC, P], F32)
        rec = alloc(a, "rec", [P, 2, REC], I32)
        r = {k: alloc(a, f"r_{k}", [P, 2, NE], F32)
             for k in ("l", "d", "e", "p", "q", "eq", "v", "oh1", "oh2", "w1", "w2", "pos", "m1", "m2")}
        rs = {k: alloc(a, f"rs_{k}", [P, 2], F32)
              for k in ("mx", "s", "rs", "p1", "vm", "p2", "sm", "rsm", "v1", "v2", "pos1", "pos2")}
        hot = alloc(a, "hot", [P, 2, NE], BF16)
        acc2 = alloc(a, "acc2", [P, 2, NE], BF16)
        idx = alloc(a, "idx", [P, 2, 2], I32)
        pad_idx = alloc(a, "pad_idx", [P, NE], I32)
        lane = alloc(a, "lane", [P, 1], F32)
        cnt_f = alloc(a, "cnt_f", [P, NE], F32)
        b1r = alloc(a, "b1r", [NE * HC, P], F32)
        b1q = alloc(a, "b1q", [P, NE, HC], F32)
        b1ss = alloc(a, "b1ss", [P, NE], F32)

        def load_stage(b):
            def go(e, eng, p):
                if e != "sp":
                    return
                row = (2 * p + b) * P
                need(eng, f"xn{b}", p)
                landed(eng.dma_start(xin[b][:, :], x[bass.ds(row, P), :]), f"ldx{b}")
                need(eng, f"xct{b}", p)
                landed(eng.dma_start(cin[b][:, :], c[bass.ds(row, P), :]), f"ldc{b}")
            return go

        def statistics(e, eng, src, b, name, count):
            st6, mv, var, rstd = norm_bufs[name][b]
            name = f"{name}{b}"
            if e == "dve":
                done(eng.bn_stats(st6[:, :], src), name + "st")
                need(eng, name + "st", count)
                settle(eng)
                done(eng.bn_aggr(mv[:, :], st6[:, :]), name + "mv")
                need(eng, name + "mv", count)
                done(eng.tensor_scalar(var[:, :], mv[:, 1:2], EPS, None, ALU.add), name + "ve")
            if e == "pool":
                need(eng, name + "ve", count)
                done(eng.tensor_tensor(rstd[:, :], var[:, :], mhalf[:, :], ALU.pow), name + "rs")

        def normalised(eng, src, b, name, count, dst, scale=1.0):
            _, mv, _, rstd = norm_bufs[name][b]
            name = f"{name}{b}"
            need(eng, name + "rs", count)
            if scale != 1.0:
                done(eng.tensor_scalar(rstd[:, :], rstd[:, :], scale, None, ALU.mult), name + "rx")
                need(eng, name + "rx", count)
            return eng.tensor_scalar(dst, src, mv[:, 0:1], rstd[:, :], ALU.subtract, ALU.mult)

        def means_in(b):
            def go(e, eng, p):
                if e == "dve":
                    need_dma(eng, f"ldx{b}", p + 1)
                    need(eng, f"xn{b}", p)
                statistics(e, eng, xin[b][:, :], b, "ln", p + 1)
            return go

        def norm_in(b):
            def go(e, eng, p):
                if e == "dve":
                    need(eng, f"xct{b}", p)
                    done(normalised(eng, xin[b][:, :], b, "ln", p + 1, xn[b][:, :]), f"xn{b}")
                if e == "pe":
                    g = turn(eng, f"xct{b}", f"xce{b}", p + 1)
                    need(eng, f"xn{b}", p + 1)
                    need_dma(eng, f"ldc{b}", p + 1)
                    for i, src in enumerate((xn[b], cin[b])):
                        for k in range(DC):
                            o = (DC * i + k) * P
                            ins = eng.transpose(g[:, o:o + P], src[:, k * P:(k + 1) * P], idf[:, :])
                    done(ins, f"xct{b}")
                if e == "act":
                    need(eng, f"xct{b}", p + 1)
                    need(eng, f"v{b}", p)
                    done(eng.activation(xct[b][:, :, :], given(f"xct{b}")[:, :].rearrange("p (a t) -> p a t", t=P),
                                        ACT.Copy), f"xce{b}")
            return go

        def project(b):
            def go(e, eng, p):
                if e == "pe":
                    need(eng, f"xce{b}", p + 1)
                    g = turn(eng, f"qk{b}", f"qke{b}", p + 1)
                    for i, w in ((0, wq_sb), (1, wk_sb)):
                        for k in range(DC):
                            ins = eng.matmul(g[:, i * D:(i + 1) * D], xct[b][:, DC * i + k, :], w[:, k, :],
                                             start=(k == 0), stop=(k == DC - 1))
                    done(ins, f"qk{b}")
                    g = turn(eng, f"v{b}", f"ve{b}", p + 1)
                    for k in range(DC):
                        ins = eng.matmul(g[:, 0:D], xct[b][:, DC + k, :], wv_sb[:, k, :],
                                         start=(k == 0), stop=(k == DC - 1))
                    done(ins, f"v{b}")
                if e == "dve":
                    need(eng, f"qk{b}", p + 1)
                    need(eng, "unit", p)
                    done(eng.tensor_tensor(qk[:, b, :, :].rearrange("p h d -> p (h d)"),
                                           given(f"qk{b}")[:, :], bqk[:, :], ALU.add), f"qke{b}")
                    need(eng, f"v{b}", p + 1)
                    need(eng, f"vz{b}", p)
                    done(eng.tensor_tensor(vn[b][:, :], given(f"v{b}")[:, 0:D], bv_sb[:, :], ALU.add), f"ve{b}")
            return go

        def squares(b):
            def go(e, eng, p):
                if e == "act":
                    need(eng, f"qke{b}", p + 1)
                    need(eng, "lo1", p)
                    done(eng.activation(qks[:, b, :, :], qk[:, b, :, :], ACT.Square), f"sq{b}")
                if e == "dve":
                    need(eng, f"sq{b}", p + 1)
                    need(eng, "n2y2", p)
                    done(eng.tensor_reduce(n2[:, b, :], qks[:, b, :, :], AX.X, ALU.add), f"n2{b}")
            return go

        def norms(piece):
            def go(e, eng, p):
                n = p + 1
                def step(ins, name):
                    done(ins, name)
                    need(eng, name, n)
                if piece == 1:
                    if e == "dve":
                        need(eng, "n20", n)
                        need(eng, "n21", n)
                        need(eng, "nln", p)
                        step(eng.tensor_scalar(na["mant"][:, :, :], n2[:, :, :].bitcast(I32), ONE - 1, 127 * ONE,
                                               ALU.bitwise_and, ALU.bitwise_or), "mant")
                        step(eng.tensor_scalar(na["ex"][:, :, :], n2[:, :, :].bitcast(I32), 23, None,
                                               ALU.logical_shift_right), "ex")
                        step(eng.tensor_scalar(na["exf"][:, :, :], na["ex"][:, :, :], -127.0, 0.5 * LN2,
                                               ALU.add, ALU.mult), "exf")
                    if e == "act":
                        need(eng, "mant", n)
                        done(eng.activation(na["ln"][:, :, :], na["mant"][:, :, :].bitcast(F32), ACT.Ln), "nln")
                if piece == 2:
                    if e == "dve":
                        need(eng, "nln", n)
                        need(eng, "ny", p)
                        step(eng.scalar_tensor_tensor(na["ah"][:, :, :], na["ln"][:, :, :], 0.5, na["exf"][:, :, :],
                                                      ALU.mult, ALU.add), "ah")
                    if e == "act":
                        need(eng, "ah", n)
                        need(eng, "nt", p)
                        need(eng, "rn", p)
                        done(eng.activation(na["y"][:, :, :], na["ah"][:, :, :], ACT.Exp, scale=-1.0), "ny")
                if piece == 3:
                    if e == "dve":
                        sgn = na["r1"]
                        need(eng, "rows_t", p)
                        step(eng.tensor_copy(sgn[:, :, 0:NH], na["ah"][:, :, 0:NH]), "sgq")
                        step(eng.tensor_scalar(sgn[:, :, NH:], na["ah"][:, :, NH:], -1.0, None, ALU.mult), "sgk")
                        part = lambda i: ar[:, :, :, i * STRIP:i * STRIP + NH]
                        v4 = lambda t: t[:, :, :].rearrange("p b (i h) -> p b i h", h=NH)
                        step(eng.tensor_copy(part(0), v4(sgn)), "p0")
                        step(eng.tensor_tensor(v4(na["r2"]), v4(sgn), part(0), ALU.subtract), "r2")
                        step(eng.tensor_copy(part(1), v4(na["r2"])), "p1")
                        step(eng.tensor_tensor(v4(sgn), v4(na["r2"]), part(1), ALU.subtract), "r3")
                        step(eng.tensor_copy(part(2), v4(sgn)), "parts")
                if piece == 4:
                    if e == "dve":
                        need(eng, "ny", n)
                        step(eng.tensor_tensor(na["y2"][:, :, :], na["y"][:, :, :], na["y"][:, :, :], ALU.mult), "y2")
                        step(eng.tensor_tensor(na["n2y2"][:, :, :], na["y2"][:, :, :], n2[:, :, :], ALU.mult), "n2y2")
                        step(eng.tensor_scalar(na["nt"][:, :, :], na["n2y2"][:, :, :], -0.5, 1.5, ALU.mult, ALU.add), "nt")
                        step(eng.tensor_tensor(na["rn"][:, :, :], na["y"][:, :, :], na["nt"][:, :, :], ALU.mult), "rn")
                        step(eng.tensor_tensor(na["coef"][:, :, :], na["rn"][:, :, :],
                                               colscale[:, :].unsqueeze(1).to_broadcast([P, 2, 2 * NH]), ALU.mult), "coef")
                        for b in range(2):
                            ins = eng.tensor_tensor(qks[:, b, :, :], qk[:, b, :, :],
                                                    na["coef"][:, b, :].unsqueeze(2).to_broadcast([P, 2 * NH, DK]), ALU.mult)
                        step(ins, "unit")
            return go

        def parts_of(b):
            def go(e, eng, p):
                n = p + 1
                part = lambda i, s0, ds: qks16[b][:, NH * i:NH * (i + 1), s0:s0 + ds + 1:ds, :]
                both = lambda t, i: t[:, NH * i:NH * (i + 1), :].unsqueeze(2).to_broadcast([P, NH, 2, DK])
                if e == "act":
                    need(eng, "unit", n)
                    need(eng, f"stk{b}", p)
                    eng.activation(part(0, 0, 1), both(qks[:, b, :, :], 0), ACT.Copy)
                    done(eng.activation(part(1, 0, 2), both(qks[:, b, :, :], 1), ACT.Copy), f"hi{b}")
                if e == "dve":
                    need(eng, f"hi{b}", n)
                    for i, s0, ds in ((0, 2, 1), (1, 1, 2)):
                        ins = eng.tensor_tensor(part(i, s0, ds), both(qks[:, b, :, :], i),
                                                both(qks16[b][:, :, 0, :], i), ALU.subtract)
                    done(ins, f"lo{b}")
            return go

        def rows(e, eng, p):
            n = p + 1
            if e == "pe":
                need(eng, "parts", n)
                g = turn(eng, "rows_t", "rowk1", n)
                gb = g[:, :].bitcast(BF16)
                for b in range(2):
                    for i in range(2):
                        o = (2 * b + i) * P
                        ins = eng.transpose(gb[0:RROWS, o:o + P], ar[:, b, i, :], idb[:, :])
                done(ins, "rows_t")
            if e == "dve":
                gb = given("rows_t")[:, :].bitcast(BF16)
                need(eng, "rows_t", n)
                for b in range(2):
                    need(eng, f"su{2 * b + 1}", p)
                    done(eng.tensor_copy(aq[b][0:RROWS, :], gb[0:RROWS, 2 * b * P:(2 * b + 1) * P]), f"rowq{b}")
                    need_dma(eng, f"flat{b}", 2 * NSPLIT * p)
                    done(eng.tensor_copy(kbr[b][:, :], gb[0:RROWS, (2 * b + 1) * P:(2 * b + 2) * P]), f"rowk{b}")
            if e == "sp":
                for b in range(2):
                    need(eng, f"rowk{b}", n)
                    need(eng, f"su{2 * b + 1}", p)
                    for s in range(NSPLIT):
                        for par in range(2):
                            dst = uk[b][RROWS + s:RROWS + s + 1, par * 1024:(par + 1) * 1024]
                            src = kbr[b][s * STRIP + par:s * STRIP + NH:2, :]
                            landed(eng.dma_start(dst.rearrange("o (j k) -> o j k", k=P), src), f"flat{b}")

        def stack(b):
            def go(e, eng, p):
                n = p + 1
                if e == "pe":
                    need(eng, f"lo{b}", n)
                    for i, to in ((0, "qte"), (1, "kte")):
                        g = turn(eng, f"{to}{b}", f"{to}{b}", n)
                        gh = g[:, :].bitcast(F16)
                        for j in range(NH // 2):
                            h = NH * i + 2 * j
                            src = qks16[b][:, h:h + 2, :, :].rearrange("p h s d -> p (h s d)")
                            ins = eng.transpose(gh[:, j * P:(j + 1) * P], src, id16[:, :])
                        done(ins, f"stk{b}" if i else f"stq{b}")
                if e == "act":
                    need(eng, f"stq{b}", n)
                    need(eng, f"su{2 * b + 1}", p)
                    done(eng.activation(qt[b][:, :, :], given(f"qte{b}")[:, :].bitcast(F16)
                                        .rearrange("p (j t) -> p j t", t=P), ACT.Copy), f"qte{b}")
                if e == "dve":
                    need(eng, f"stk{b}", n)
                    need(eng, f"su{2 * b + 1}", p)
                    done(eng.tensor_copy(kt[b][:, :, :], given(f"kte{b}")[:, :].bitcast(F16)
                                         .rearrange("p (j t) -> p j t", t=P)), f"kte{b}")
                if e == "pool":
                    need(eng, f"ve{b}", n)
                    need(eng, f"pv{2 * b + 1}", p)
                    settle(eng)
                    for h in range(2):
                        ins = eng.tensor_copy(
                            vz[b][:, 2 * h:2 * h + 2, :, 0:DK],
                            vn[b][:, h * P:(h + 1) * P].rearrange("p (j a d) -> p a j d", a=2, d=DK))
                    done(ins, f"vz{b}")
            return go

        def factors(n_):
            b, h = divmod(n_, 2)
            def go(e, eng, p):
                n = p + 1
                prev = (n_ - 1) % 4
                pc = n if n_ else p
                if e == "pe":
                    need(eng, f"rowq{b}", n)
                    need_dma(eng, f"flat{b}", 2 * NSPLIT * n)
                    need(eng, f"th{prev}", pc)
                    for i in range(2):
                        o = i * 1024 + h * 512
                        ins = eng.matmul(u_ps[:, i * 512:(i + 1) * 512], aq[b][:, :], uk[b][:, o:o + 512],
                                         start=True, stop=True)
                    done(ins, f"u{n_}")
                if e == "act":
                    need(eng, f"u{n_}", n)
                    need(eng, f"tw{n_ ^ 2}", n if n_ >= 2 else p)
                    done(eng.activation(th[h][:, :], u_ps[:, :], ACT.Tanh, scale=0.5), f"th{n_}")
                    need(eng, f"th{n_}", n)
                    done(eng.activation(th[h][:, :], th[h][:, :], ACT.Square), f"t2{n_}")
            return go

        def scores(n_):
            b, h = divmod(n_, 2)
            def go(e, eng, p):
                n = p + 1
                prev = (n_ - 1) % 4
                pc = n if n_ else p
                if e == "pe":
                    need(eng, f"qte{b}", n)
                    need(eng, f"kte{b}", n)
                    need(eng, f"tw{prev}", pc)
                    for j in range(4):
                        for i in range(2):
                            rws = slice(64 * i, 64 * i + 64)
                            ins = eng.matmul(s_ps[:, i, j * P:(j + 1) * P], qt[b][rws, 4 * h + j, :],
                                             kt[b][rws, 4 * h + j, :], start=True, stop=True)
                    done(ins, f"su{n_}")
                if e == "dve":
                    need(eng, f"t2{n_}", n)
                    need(eng, f"su{n_}", n)
                    need(eng, f"tt{n_ ^ 2}", n if n_ >= 2 else p)
                    twf = tw[h][:, :, :, :].rearrange("p i j k -> p (i j k)")
                    done(eng.scalar_tensor_tensor(twf, th[h][:, :], -1.0,
                                                  s_ps[:, :, :].rearrange("p i k -> p (i k)"),
                                                  ALU.add, ALU.mult), f"tw{n_}")
                    need(eng, f"tw{n_}", n)
                    need(eng, f"sb{n_ ^ 2}", n if n_ >= 2 else p)
                    done(eng.tensor_reduce(tm[h][:, :], tw[h][:, :, :, :].rearrange("p i j k -> p (i j) k"),
                                           AX.X, ALU.max), f"tm{n_}")
                if e == "pool":
                    need(eng, f"tm{n_}", n)
                    v = tw[h][:, :, :, :].rearrange("p i j k -> p (i j) k")
                    done(eng.tensor_tensor(v, v, tm[h][:, :].unsqueeze(2).to_broadcast([P, 8, P]),
                                           ALU.subtract), f"sb{n_}")
            return go

        def turned(n_, i):
            b, h = divmod(n_, 2)
            def go(e, eng, p):
                n = p + 1
                if e == "pe":
                    if i == 0:
                        need(eng, f"sb{n_}", n)
                    g = turn(eng, f"ex{n_}{i}", f"ex{n_}{i}", n)
                    for j in range(4):
                        ins = eng.transpose(g[:, j * P:(j + 1) * P], tw[h][:, i, j, :], idf[:, :])
                    done(ins, f"tt{n_}" if i else f"ta{n_}")
                if e == "act":
                    need(eng, f"tt{n_}" if i else f"ta{n_}", n)
                    need(eng, f"pv{n_ ^ 2}", n if n_ >= 2 else p)
                    done(eng.activation(pt[h][:, i, :], given(f"ex{n_}{i}")[:, :], ACT.Exp,
                                        scale=escale[:, :]), f"ex{n_}{i}")
            return go

        def values(n_):
            b, h = divmod(n_, 2)
            def go(e, eng, p):
                n = p + 1
                if e == "pe":
                    need(eng, f"vz{b}", n)
                    if h == 0:
                        need(eng, "osb", 2 * p + b)
                    for i in range(2):
                        need(eng, f"ex{n_}{i}", n)
                        q = 2 * h + i
                        for j in range(4):
                            vq = vz[b][:, q, :, :].rearrange("p j m -> p (j m)")
                            ins = eng.matmul(pv_ps[0:VM, q * P:(q + 1) * P], vq[:, j * VM:(j + 1) * VM],
                                             pt[h][:, i, j * P:(j + 1) * P], start=(j == 0), stop=(j == 3))
                    done(ins, f"pv{n_}")
            return go

        def back(b, part):
            def go(e, eng, p):
                n, m = p + 1, 2 * p + b + 1
                if part == 0:
                    if e == "sp":
                        need(eng, f"xb{b}", p)
                        landed(eng.dma_start(xres[b][:, :], x[bass.ds((2 * p + b) * P, P), :]), f"ldr{b}")
                    if e == "pool":
                        need_dma(eng, f"ldr{b}", n)
                        need(eng, f"x1{b}", p)
                        done(eng.tensor_tensor(xb[b][:, :], xres[b][:, :], bo_sb[:, :], ALU.add), f"xb{b}")
                if part == 1:
                    if e == "act":
                        need(eng, f"pv{2 * b + 1}", n)
                        need(eng, "ob", m - 1)
                        done(eng.activation(osb[:, :], pv_ps[0:VM, :], ACT.Copy), "osb")
                    if e == "pe":
                        g = turn(eng, f"ob{b}", "on", m)
                        need(eng, "osb", m)
                        for q in range(4):
                            ins = eng.transpose(g[:, q * P:q * P + VM], osb[:, q * P:(q + 1) * P],
                                                idf[0:VM, 0:VM])
                        done(ins, "ob")
                    if e == "dve":
                        g = given(f"ob{b}")[:, :].rearrange("p (q c) -> p q c", q=4)
                        need(eng, "ob", m)
                        done(eng.reciprocal(rz[:, :, :], g[:, :, 4 * DK:4 * DK + 4]), "rz")
                        need(eng, "rz", m)
                        need(eng, "oc", m - 1)
                        for h in range(2):
                            ins = eng.tensor_tensor(
                                on[:, h * P:(h + 1) * P].rearrange("p (j a d) -> p a j d", a=2, d=DK),
                                g[:, 2 * h:2 * h + 2, 0:4 * DK].rearrange("p a (j d) -> p a j d", d=DK),
                                rz[:, 2 * h:2 * h + 2, :].unsqueeze(3).to_broadcast([P, 2, 4, DK]), ALU.mult)
                        done(ins, "on")
                if part == 2:
                    if e == "pe":
                        g = turn(eng, f"oc{b}", "ote", m)
                        need(eng, "on", m)
                        for k in range(DC):
                            ins = eng.transpose(g[:, k * P:(k + 1) * P], on[:, k * P:(k + 1) * P], idf[:, :])
                        done(ins, "oc")
                    if e == "act":
                        need(eng, "oc", m)
                        need(eng, "wo", m - 1)
                        done(eng.activation(ot[:, :, :], given(f"oc{b}")[:, 0:D]
                                            .rearrange("p (k t) -> p k t", t=P), ACT.Copy), "ote")
                if part == 3:
                    if e == "pe":
                        g = turn(eng, f"wo{b}", f"x1{b}", n)
                        need(eng, "ote", m)
                        for k in range(DC):
                            ins = eng.matmul(g[:, 0:D], ot[:, k, :], wo_sb[:, k, :], start=(k == 0),
                                             stop=(k == DC - 1))
                        done(ins, "wo")
                    if e == "dve":
                        need(eng, "wo", m)
                        need(eng, f"xb{b}", n)
                        need_dma(eng, f"stx{b}", p)
                        done(eng.tensor_tensor(x1[b][:, :], given(f"wo{b}")[:, 0:D], xb[b][:, :], ALU.add), f"x1{b}")
                        need(eng, f"x1{b}", n)
                        need(eng, f"y{b}", p)
                    statistics(e, eng, x1[b][:, :], b, "lm", n)
                    if e == "sp":
                        need(eng, f"x1{b}", n)
                        landed(eng.dma_start(acc_d[bass.ds((2 * p + b) * P, P), :], x1[b][:, :]), f"stx{b}")
                if part == 4:
                    if e == "dve":
                        need(eng, f"xu{b}", p)
                        done(normalised(eng, x1[b][:, :], b, "lm", n, xn2[b][:, :], X_SCALE), f"y{b}")
                        need_dma(eng, "scat", 4 * p)
                        need(eng, f"y{b}", n)
                        done(eng.tensor_copy(rec[:, b, :].bitcast(F16)[:, 0:D], xn2[b][:, :]), f"rh{b}")
                        need(eng, f"rh{b}", n)
                        done(eng.tensor_tensor(rec[:, b, :].bitcast(F16)[:, D:2 * D], xn2[b][:, :],
                                               rec[:, b, :].bitcast(F16)[:, 0:D], ALU.subtract), f"rl{b}")
                    if e == "pe":
                        g = turn(eng, f"xu{b}", "xue", m)
                        need(eng, f"y{b}", n)
                        for k in range(DC):
                            ins = eng.transpose(g[:, k * P:(k + 1) * P], xn2[b][:, k * P:(k + 1) * P], idf[:, :])
                        done(ins, f"xu{b}")
                    if e == "act":
                        need(eng, f"xu{b}", n)
                        need(eng, "lg", m - 1)
                        done(eng.activation(xn2t[:, :, :], given(f"xu{b}")[:, 0:D]
                                            .rearrange("p (k t) -> p k t", t=P), ACT.Copy), "xue")
                if part == 5:
                    if e == "pe":
                        g = turn(eng, f"lg{b}", f"rl_{b}", n)
                        need(eng, "xue", m)
                        for k in range(DC):
                            ins = eng.matmul(g[:, 0:NE], xn2t[:, k, :], wr_sb[:, k, :], start=(k == 0),
                                             stop=(k == DC - 1))
                        done(ins, "lg")
                    if e == "dve":
                        need(eng, "lg", m)
                        need(eng, "rd", p)
                        done(eng.tensor_scalar(r["l"][:, b, :], given(f"lg{b}")[:, 0:NE], 1.0 / X_SCALE, None,
                                               ALU.mult), f"rl_{b}")
            return go

        def route(piece):
            def go(e, eng, p):
                n = p + 1
                wide = lambda t: rs[t][:, :].unsqueeze(2).to_broadcast([P, 2, NE])
                f = lambda t: r[t][:, :, :]
                def step(ins, name):
                    done(ins, name)
                    need(eng, name, n)

                def best(src, i):
                    top, oh = f"p{i}", f"oh{i}"
                    step(eng.tensor_reduce(rs[top][:, :], f(src), AX.X, ALU.max), f"b_mx{i}")
                    step(eng.tensor_tensor(f("eq"), f(src), wide(top), ALU.is_equal), f"b_eq{i}")
                    step(eng.tensor_tensor(f("v"), f("eq"), rank8[:, :, :], ALU.mult), f"b_v{i}")
                    step(eng.tensor_reduce(rs["vm"][:, :], f("v"), AX.X, ALU.max), f"b_vm{i}")
                    step(eng.tensor_tensor(f(oh), f("v"), wide("vm"), ALU.is_equal), f"b_oh{i}")

                if piece == 1:
                    if e == "dve":
                        need(eng, "rl_0", n)
                        need(eng, "rl_1", n)
                        step(eng.tensor_reduce(rs["mx"][:, :], f("l"), AX.X, ALU.max), "rmx")
                        need(eng, "re", p)
                        step(eng.tensor_tensor(f("d"), f("l"), wide("mx"), ALU.subtract), "rd")
                    if e == "act":
                        need(eng, "rd", n)
                        need(eng, "rp", p)
                        done(eng.activation(f("e"), f("d"), ACT.Exp), "re")
                if piece == 2:
                    if e == "dve":
                        need(eng, "re", n)
                        step(eng.tensor_reduce(rs["s"][:, :], f("e"), AX.X, ALU.add), "rs")
                        step(eng.reciprocal(rs["rs"][:, :], rs["s"][:, :]), "rrs")
                        step(eng.tensor_tensor(f("p"), f("e"), wide("rs"), ALU.mult), "rp")

                        best("p", 1)
                        step(eng.scalar_tensor_tensor(f("q"), f("oh1"), -2.0, f("p"), ALU.mult, ALU.add), "rq")
                        best("q", 2)
                if piece == 3:
                    if e == "dve":
                        step(eng.tensor_tensor(rs["sm"][:, :], rs["p1"][:, :], rs["p2"][:, :], ALU.add), "rsm")
                        step(eng.reciprocal(rs["rsm"][:, :], rs["sm"][:, :]), "rrm")
                        step(eng.tensor_tensor(rs["v1"][:, :], rs["p1"][:, :], rs["rsm"][:, :], ALU.mult), "rv1")
                        step(eng.tensor_tensor(rs["v2"][:, :], rs["p2"][:, :], rs["rsm"][:, :], ALU.mult), "rv2")
                        step(eng.tensor_tensor(f("w1"), f("oh1"), wide("v1"), ALU.mult), "rw1")
                        step(eng.tensor_tensor(f("w2"), f("oh2"), wide("v2"), ALU.mult), "rw2")
                if piece == 4:
                    if e == "dve":
                        recf = rec[:, :, :].bitcast(F32)
                        done(eng.tensor_tensor(recf[:, :, D:D + NE], f("w1"), f("w2"), ALU.add), "rw")
                        reci = rec[:, :, :]
                        for b in range(2):
                            ins = eng.tensor_scalar(reci[:, b, D + NE:D + NE + 1], tok[:, :], float(b * P), None, ALU.add)
                        step(ins, "rtok")
                        step(eng.tensor_scalar(tok[:, :], tok[:, :], float(2 * P), None, ALU.add), "rtk")
                        need(eng, "rank", p)
                        step(eng.tensor_tensor(hot[:, :, :], f("oh1"), f("oh2"), ALU.add), "rhot")
                        step(eng.tensor_copy(acc2[:, 0, :], acc_cnt[:, :]), "ra0")
                        step(eng.tensor_tensor(acc2[:, 1, :], acc_cnt[:, :], hot[:, 0, :], ALU.add), "ra1")
                        step(eng.tensor_tensor(acc_cnt[:, :], acc2[:, 1, :], hot[:, 1, :], ALU.add), "racc")
                    if e == "pe":
                        g = turn(eng, "rank", "rpos", n)
                        need(eng, "racc", n)
                        eng.matmul(g[:, 0:2 * NE], lstrict[:, :], hot[:, :, :].rearrange("p b e -> p (b e)"),
                                   start=True, stop=False)
                        done(eng.matmul(g[:, 0:2 * NE], ones_b[:, :], acc2[:, :, :].rearrange("p b e -> p (b e)"),
                                        start=False, stop=True), "rank")
                if piece == 5:
                    if e == "dve":
                        need(eng, "rank", n)
                        step(eng.tensor_tensor(f("pos"), given("rank")[:, 0:2 * NE].rearrange("p (b e) -> p b e", e=NE),
                                               ebase[:, :, :], ALU.add), "rpos")
                        step(eng.tensor_tensor(f("m1"), f("oh1"), f("pos"), ALU.mult), "rm1")
                        step(eng.tensor_tensor(f("m2"), f("oh2"), f("pos"), ALU.mult), "rm2")
                        step(eng.tensor_reduce(rs["pos1"][:, :], f("m1"), AX.X, ALU.add), "rp1")
                        step(eng.tensor_reduce(rs["pos2"][:, :], f("m2"), AX.X, ALU.add), "rp2")
                        need_dma(eng, "scat", 4 * p)
                        eng.tensor_copy(idx[:, 0, :], rs["pos1"][:, :])
                        done(eng.tensor_copy(idx[:, 1, :], rs["pos2"][:, :]), "ridx")
                    if e == "pool":
                        need(eng, "ridx", n)
                        need(eng, "rtok", n)
                        for b in range(2):
                            need(eng, f"rl{b}", n)
                            settle(eng)
                            for i in range(2):
                                landed(eng.indirect_dma_start(
                                    xrec_d[:, :], bass.IndirectOffsetOnAxis(ap=idx[:, i, b:b + 1], axis=0),
                                    rec[:, b, :], None), "scat")
            return go

        def weights(which, piece):
            def go(e, eng, p):
                n = p + 1
                ex = p if which == 1 else p - NE
                if piece == 1:
                    if e == "sp":
                        need(eng, "wlo", p)
                        src = (w1[bass.ds(ex, 1), :, :].rearrange("o (k q) h -> q (o k) h", q=P) if which == 1
                               else w2[bass.ds(ex, 1), :, :].rearrange("o (k q) h -> q (o k) h", q=P))
                        landed(eng.dma_start(wl[:, :].rearrange("q (k h) -> q k h", k=DC if which == 1 else HC), src), "ldw")
                    if e == "act":
                        need_dma(eng, "ldw", n)
                        if which == 2:
                            need_dma(eng, "stw", ex)
                        done(eng.activation(wst[:, 0, :], wl[:, :], ACT.Square, accum_out=wss[:, :]), "wss")
                    if e == "pe":
                        g = turn(eng, "wsum", "wcl", n)
                        need(eng, "wss", n)
                        done(eng.matmul(g[:, 0:1], ones_f[:, :], wss[:, :], start=True, stop=True), "wsum")
                    if e == "dve":
                        dst = (k1 if which == 1 else k2)
                        need(eng, "wsum", n)
                        done(eng.tensor_scalar(wcl[:, :], given("wsum")[:, 0:1], 2.0 ** -60, None, ALU.max), "wcl")
                        need(eng, "wcl", n)
                        exponent(eng, wcl[:, :], wkk[:, :], "wex", n)
                        eng.tensor_copy(dst[:, bass.ds(ex, 1)], wkk[:, :])
                        done(eng.tensor_scalar(wsc[:, :], wkk[:, :], -float(ONE), 268.0 * ONE, ALU.mult, ALU.add), "wsc")
                hi = (w1s[:, bass.ds(ex, 1), 0, :, :].rearrange("p o k h -> p (o k h)") if which == 1 else wst[:, 0, :])
                lo = (w1s[:, bass.ds(ex, 1), 1, :, :].rearrange("p o k h -> p (o k h)") if which == 1 else wst[:, 1, :])
                if piece == 2:
                    if e == "act":
                        need(eng, "wsc", n)
                        need(eng, "wss", n)
                        done(eng.activation(hi, wl[:, :], ACT.Identity, scale=wsc[:, :].bitcast(F32)), "whi")
                    if e == "dve":
                        need(eng, "wsc", n)
                        need(eng, "whi", n)
                        if which == 2:
                            need_dma(eng, "stw", ex)
                        done(eng.scalar_tensor_tensor(lo, wl[:, :], wsc[:, :].bitcast(F32), hi, ALU.mult,
                                                      ALU.subtract), "wlo")
                    if e == "sp" and which == 2:
                        need(eng, "wlo", n)
                        landed(eng.dma_start(w2s_d[bass.ds(ex, 1), :, :].rearrange("o q h -> q (o h)"),
                                             wst[:, :, :].rearrange("q s h -> q (s h)")), "stw")
            return go

        def exponent(eng, src, dst, name, count):
            done(eng.tensor_scalar(dst, src.bitcast(I32), 23, None, ALU.logical_shift_right), name + "a")
            need(eng, name + "a", count)
            done(eng.tensor_scalar(dst, dst, 129.0, None, ALU.add), name + "b")
            need(eng, name + "b", count)
            done(eng.tensor_scalar(dst, dst, 1, None, ALU.logical_shift_right), name)
            need(eng, name, count)

        def setup(e, eng, _):
            if e == "sp":
                for dst, src in ((wq_sb, wq), (wk_sb, wk), (wv_sb, wv), (wo_sb, wo), (wr_sb, wr)):
                    landed(eng.dma_start(dst[:, :, :], src.rearrange("(k q) n -> q k n", q=P)), "set_w")
                landed(eng.dma_start(b1r[:, :], b1.rearrange("e (m q) -> (e m) q", q=P)), "set_w")
            if e == "act":
                for dst, src in (((bqk[:, 0:D], bq), (bqk[:, D:2 * D], bk), (bv_sb[:, :], bv),
                                                (bo_sb[:, :], bo), (al[:, :], alpha))):
                    landed(eng.dma_start(dst, src.partition_broadcast(P)), "set_v")
            if e == "pe":
                need(eng, "set_pool", 2)
                need_dma(eng, "set_w", 6)
                done(eng.transpose(gen[0][:, 0:NE * HC], b1r[:, :], idf[0:NE * HC, 0:NE * HC]), "set_bt")
            if e == "dve":
                eng.memset(ones_f[:, :], 1.0)
                eng.memset(ones_b[:, :], 1.0)
                eng.memset(zrow[:, :], 0.0)
                eng.memset(acc_cnt[:, :], 0.0)
                eng.memset(mhalf[:, :], -0.5)
                eng.memset(ar[:, :, :, :], 0.0)
                eng.memset(padrec[:, :], 0)
                for b in range(2):
                    eng.memset(aq[b][RROWS:RROWS + NSPLIT, :], 1.0)
                    ins = eng.memset(vz[b][:, :, :, :], 0.0)
                done(ins, "set_dve")
                need(eng, "set_dve", 1)
                for b in range(2):
                    for j in range(4):
                        vq = vz[b][:, :, :, :].rearrange("p q j m -> p q (j m)")
                        ins = eng.memset(vq[:, :, j * VM + 4 * DK + j:j * VM + 4 * DK + j + 1], 1.0)
                done(ins, "set_dve")
                need_dma(eng, "set_v", 5)
                done(eng.tensor_reduce(amax[:, :], al[:, :], AX.X, ALU.max, apply_absolute_value=True), "set_a")
                need(eng, "set_a", 1)
                done(eng.tensor_scalar(amax[:, :], amax[:, :], 2.0 ** -60, None, ALU.max), "set_a")
                need(eng, "set_a", 2)
                done(eng.tensor_scalar(abig[:, :], amax[:, :].bitcast(I32), 255 * ONE, None, ALU.bitwise_and), "set_a")
                need(eng, "set_a", 3)
                done(eng.tensor_scalar(abig[:, :], abig[:, :], float(ONE), None, ALU.add), "set_a")
                need(eng, "set_a", 4)
                eng.tensor_scalar(arec[:, :], abig[:, :], -1.0, 254.0 * ONE, ALU.mult, ALU.add)
                done(eng.tensor_scalar(escale[:, :], abig[:, :].bitcast(F32), QK_SCALE ** -2, None, ALU.mult), "set_a")
                need(eng, "set_a", 5)
                eng.memset(colscale[:, NH:2 * NH], QK_SCALE)
                done(eng.tensor_scalar(colscale[:, 0:NH], al[:, :], arec[:, :].bitcast(F32), -QK_SCALE,
                                       ALU.mult, ALU.mult), "set_a")
                need(eng, "set_bt", 1)
                done(eng.tensor_copy(b1t[:, :, :].rearrange("p e m -> p (e m)"), gen[0][:, 0:NE * HC]), "set_b1t")
                need(eng, "set_b1t", 1)
                done(eng.tensor_tensor(b1q[:, :, :], b1t[:, :, :], b1t[:, :, :], ALU.mult), "set_b")
                need(eng, "set_b", 1)
                done(eng.tensor_reduce(b1ss[:, :], b1q[:, :, :], AX.X, ALU.add), "set_b")
                need(eng, "set_a", 6)
            if e == "pe":
                need(eng, "set_dve", 2)
                need(eng, "set_b", 2)
                done(eng.matmul(pv_ps[:, 0:NE], ones_f[:, :], b1ss[:, :], start=True, stop=True), "set_bs")
            if e == "dve":
                need(eng, "set_bs", 1)
                done(eng.tensor_scalar(b1ss[:, :], pv_ps[:, 0:NE], 2.0 ** -60, None, ALU.max), "set_b")
                need(eng, "set_b", 3)
                exponent(eng, b1ss[:, :], kb[:, :], "set_kb", 1)
            if e == "pool":
                for m in (idf, idb, id16, lstrict):
                    eng.memset(m[:, :], 0.0)
                for b in range(2):
                    eng.memset(uk[b][:, :], 0.0)
                eng.iota(io8[:, :, :], [[0, 2], [REGION, NE]], base=0, channel_multiplier=0)
                done(eng.iota(tok[:, :], [[0, 1]], base=T, channel_multiplier=1), "set_pool")
                need(eng, "set_pool", 1)
                made = 0

                def one(ins):
                    nonlocal made
                    made += 1
                    done(ins, "set_select")
                    need(eng, "set_select", made)
                for m in (idf, idb, id16):
                    one(eng.affine_select(out=m[:, :], in_=m[:, :], compare_op=ALU.not_equal, fill=1.0, base=0,
                                          pattern=[[-1, P]], channel_multiplier=1))
                one(eng.affine_select(out=lstrict[:, :], in_=lstrict[:, :], compare_op=ALU.is_ge, fill=1.0, base=0,
                                      pattern=[[-1, P]], channel_multiplier=1))
                for b in range(2):
                    for i in range(NSPLIT):
                        for par in range(2):
                            w = uk[b][i * STRIP:(i + 1) * STRIP, par * 1024:(par + 1) * 1024]\
                                .rearrange("r (j k) -> r j k", k=P)
                            one(eng.affine_select(out=w, in_=w, compare_op=ALU.not_equal, fill=1.0, base=-par,
                                                  pattern=[[-2, NH // 2], [0, P]], channel_multiplier=1))
                eng.sem_inc(sem("set_pool"), 1)
                need(eng, "set_pool", 2)
                need(eng, "set_dve", 1)
                done(eng.tensor_copy(padrec[:, D + NE:D + NE + 1], tok[:, :]), "set_pool")
                need(eng, "set_pool", 3)
                done(eng.iota(tok[:, :], [[0, 1]], base=0, channel_multiplier=1), "set_pool")
            if e == "dve":
                need(eng, "set_pool", 4)
                done(eng.tensor_copy(ebase[:, :, :], io8[:, :, :]), "set_e")
                for i in range(NE):
                    ins = eng.memset(rank8[:, :, i:i + 1], float(NE - i))
                done(ins, "set_e")
                need(eng, "set_e", 2)
            if e == "sp":
                need(eng, "set_pool", 4)
                landed(eng.dma_start(xrec_d[NE * REGION:NE * REGION + P, :], padrec[:, :]), "set_pad")
                need(eng, "set_dve", 1)
                landed(eng.dma_start(acc_d[T:T + P, :], zrow[:, :]), "set_pad")
            if e == "pe":
                need(eng, "set_pool", 2)
                need_dma(eng, "set_w", 6)
                need(eng, "set_b", 3)
            if e == "act":
                need(eng, "set_a", 6)
            if e == "pool":
                need_dma(eng, "set_v", 5)

        stages = {"rows": rows}
        for b_ in range(2):
            stages.update({f"load{b_}": load_stage(b_), f"means{b_}": means_in(b_), f"norm{b_}": norm_in(b_),
                           f"project{b_}": project(b_), f"squares{b_}": squares(b_), f"parts{b_}": parts_of(b_),
                           f"stack{b_}": stack(b_)})
            stages.update({f"back{b_}.{i}": back(b_, i) for i in range(6)})
        for n_ in halves:
            stages.update({f"factors{n_}": factors(n_), f"scores{n_}": scores(n_), f"values{n_}": values(n_)})
            stages.update({f"turned{n_}.{i}": turned(n_, i) for i in range(2)})
        stages.update({f"norms.{i}": norms(i) for i in range(1, 5)})
        stages.update({f"route.{i}": route(i) for i in range(1, 6)})

        order = {
            "pe": """
                values2- values3- back0.2- stack0 back1.1- factors0 back0.3- scores0 factors1 back1.2-
                scores1 factors2 stack1 norm1+ back1.3- project1+ turned0.0 norm0+ weights.1 scores2
                back0.4- turned0.1 factors3 project0+ back0.5- back1.4- back1.5- turned1.0 scores3
                turned1.1 turned2.0 values0 rows+ turned2.1 values1 turned3.0 back0.1 turned3.1
                route.4-""",
            "act": """
                parts1 back1.1- back0.2- stack0 factors0 factors1 stack1 back1.2- norm1+ factors2
                weights.1 turned0.0 norm0+ back0.4- factors3 squares1+ turned0.1 squares0+ back1.4-
                norms.1+ turned1.0 route.1- turned1.1 turned2.0 back0.1 turned2.1 norms.2+ turned3.0
                turned3.1 parts0+ weights.2""",
            "dve": """
                stack0 parts1 back1.1- scores0 means1+ back0.3- norm1+ means0+ stack1 scores1 norm0+
                back1.3- project1+ back0.4- weights.1 scores2 back1.4- project0+ squares1+ squares0+
                back0.5- back1.5- norms.1+ route.1- norms.2+ norms.3+ scores3 route.2- rows+ route.3-
                norms.4+ route.4- back0.1 route.5- parts0+ weights.2""",
            "pool": """
                means1+ scores0 means0+ stack0 stack1 back0.3- scores1 back1.3- scores2 back0.0
                scores3 back1.0 route.5-""",
            "sp": """
                load1+ back0.0 weights.1 load0+ back1.3- back0.3- back1.0 rows+ weights.2""",
        }
        deltas = {"+": 1, "-": -1}
        steps = {e: [(w.rstrip("+-"), deltas.get(w[-1], 0)) for w in text.split()] for e, text in order.items()}

        def finish_attention(e, eng, _):
            if e == "pe":
                g = turn(eng, "cnt", "cnt", 1)
                need(eng, "racc", NP)
                done(eng.matmul(g[:, 0:NE], ones_b[:, :], acc_cnt[:, :], start=True, stop=True), "cnt_ps")
            if e == "dve":
                need(eng, "cnt_ps", 1)
                done(eng.tensor_copy(cnt_f[:, :], given("cnt")[:, 0:NE]), "cnt")
                need(eng, "cnt", 1)
                done(eng.tensor_tensor(r["pos"][:, 0, :], cnt_f[:, :], ebase[:, 0, :], ALU.add), "pad_a")
                done(eng.tensor_copy(cnt_keep[:, :], cnt_f[:, :]), "pad_k")
                need(eng, "pad_a", 1)
                done(eng.tensor_scalar(pad_idx[:, :], r["pos"][:, 0, :], lane[:, :], None, ALU.add), "pad_i")
            if e == "pool":
                need(eng, "pad_i", 1)
                need_dma(eng, "scat", 4 * NP)
                for x_ in range(NE):
                    landed(eng.indirect_dma_start(
                        xrec_d[:, :], bass.IndirectOffsetOnAxis(ap=pad_idx[:, x_:x_ + 1], axis=0),
                        padrec[:, :], None), "pad")
                need_dma(eng, "pad", NE)
            if e == "sp":
                for b in range(2):
                    need_dma(eng, f"stx{b}", NP)
                need_dma(eng, "stw", NE)
                need_dma(eng, "set_pad", 2)

        def run(e, eng, k, p, which=1, kept=(-1, 0, 1), freed=(None,) * 3):
            start_section(k, freed)
            for name, d in steps[e]:
                if d in kept:
                    (weights(which, int(name[-1])) if name.startswith("weights") else stages[name])(e, eng, p + d)

        def readers(p):
            seen = []
            for q in range(2, 4):
                run("pe", Rehearsal(), None, q)
                seen.append(Turns.freed)
            return [(name, (n1 - n0) * (p - 2) + n0) for (name, n0), (_, n1) in zip(*seen)]

        def program(e, eng):
            for chain, names in chains.items():
                if e == owner(chain):
                    eng.sem_inc(sem(chain), len(names))
            setup(e, eng, 0)
            if e == "dve":
                done(eng.tensor_copy(lane[:, :], tok[:, :]), "lane")
                need(eng, "lane", 1)
            run(e, eng, 0, -1, kept=(1,))
            run(e, eng, 1, 0, kept=(0, 1), freed=Turns.freed)
            if e == "pe":
                for reader in Turns.freed:
                    need(eng, *reader)
            with eng.Fori(1, NE) as p:
                run(e, eng, 2, p, freed=readers(p - 1))
            with eng.Fori(0, NP - 1 - NE) as q:
                run(e, eng, 3, q + NE, which=2, freed=readers(q + (NE - 1)))
            run(e, eng, 4, NP - 1, which=2, kept=(-1, 0), freed=readers(NP - 2))
            run(e, eng, 5, NP, kept=(-1,), freed=Turns.freed)
            finish_attention(e, eng, 0)

        with nc.Block() as block:
            @block.tensor
            def _(eng): program("pe", eng)
            @block.scalar
            def _(eng): program("act", eng)
            @block.vector
            def _(eng): program("dve", eng)
            @block.gpsimd
            def _(eng): program("pool", eng)
            @block.sync
            def _(eng): program("sp", eng)

    U = 4
    AHEAD = 3
    SLOOP = (NSLOT - AHEAD - 1) // U * U
    with ExitStack() as f:
        w2s = alloc(f, "w2s_sb", [P, NE, 2, HC, D], F16)
        b2s = alloc(f, "b2s", [P, NE, D], F32)
        rb = [alloc(f, f"rb{i}", [P, REC], I32) for i in range(U)]
        xt = [alloc(f, f"xt{i}", [P, 2, DC, P], F16) for i in range(2)]
        h32 = [alloc(f, f"h32_{i}", [P, HC // 2, P], F32) for i in range(2)]
        hs = [alloc(f, f"hs{i}", [P, 2, HC, P], F16) for i in range(2)]
        yw = [alloc(f, f"yw{i}", [P, D], F32) for i in range(2)]
        yb = alloc(f, "yb", [P, D], F32)
        tiles_i = alloc(f, "tiles_i", [P, NE], I32)
        tiles = alloc(f, "tiles", [P, NE], F32)
        ends = alloc(f, "ends", [P, NE], F32)
        unit = alloc(f, "unit_row", [P, NE], F32)
        slot_n = alloc(f, "slot_n", [1, NSLOT, NE], I32)
        slot_f = alloc(f, "slot_f", [1, NSLOT, NE], F32)
        past = alloc(f, "past", [1, NSLOT, NE], F32)
        before = alloc(f, "before", [1, NSLOT, NE], F32)
        n_past = alloc(f, "n_past", [1, NSLOT], F32)
        start = alloc(f, "start", [1, NSLOT], F32)
        rowf = alloc(f, "rowf", [1, NSLOT], F32)
        slot_e = alloc(f, "slot_e", [1, NSLOT], I32)
        slot_row = alloc(f, "slot_row", [1, NSLOT], I32)
        mk = alloc(f, "mk", [P, NE], I32)
        hsc = alloc(f, "hsc", [P, NE], I32)
        inv1 = alloc(f, "inv1", [P, NE], I32)
        inv2 = alloc(f, "inv2", [P, NE], I32)
        hbank = [s_ps[:, 0, :], s_ps[:, 1, :], u_ps[:, 0:512], u_ps[:, 512:1024]]
        ybank = [pv_ps, gen[2]]

        def tables(e, eng):
            if e == "pool":
                done(eng.iota(slot_n[:, :, :], [[1, NSLOT], [0, NE]], base=0, channel_multiplier=0), "slot_n")
            if e == "dve":
                k = 0

                def step(ins):
                    nonlocal k
                    k += 1
                    done(ins, "table")
                    need(eng, "table", k)
                step(eng.tensor_scalar(tiles_i[:, :], cnt_keep[:, :], float(P - 1), None, ALU.add))
                step(eng.tensor_scalar(tiles_i[:, :], tiles_i[:, :], 7, None, ALU.logical_shift_right))
                step(eng.tensor_copy(tiles[:, :], tiles_i[:, :]))
                step(eng.memset(unit[:, :], 1.0))
                step(eng.tensor_tensor_scan(ends[:, :], unit[:, :], tiles[:, :], 0.0, ALU.mult, ALU.add))
                need(eng, "slot_n", 1)
                step(eng.tensor_copy(slot_f[:, :, :], slot_n[:, :, :]))
                each = lambda t: t[0:1, :].unsqueeze(1).to_broadcast([1, NSLOT, NE])
                step(eng.tensor_tensor(past[:, :, :], slot_f[:, :, :], each(ends), ALU.is_ge))
                step(eng.tensor_tensor(before[:, :, :], past[:, :, :], each(tiles), ALU.mult))
                step(eng.tensor_reduce(n_past[:, :], past[:, :, :], AX.X, ALU.add))
                step(eng.tensor_reduce(start[:, :], before[:, :, :], AX.X, ALU.add))
                step(eng.tensor_tensor(start[:, :], slot_f[:, :, 0], start[:, :], ALU.subtract))
                step(eng.tensor_scalar(start[:, :], start[:, :], float(P), None, ALU.mult))
                step(eng.scalar_tensor_tensor(rowf[:, :], n_past[:, :], float(REGION), start[:, :], ALU.mult, ALU.add))
                step(eng.tensor_scalar(slot_row[:, :], rowf[:, :], float(NE * REGION), None, ALU.min))
                step(eng.tensor_scalar(slot_e[:, :], n_past[:, :], float(NE - 1), None, ALU.min))
                step(eng.tensor_scalar(mk[:, :], k1[:, :], 4.0, None, ALU.add))
                step(eng.tensor_tensor(mk[:, :], mk[:, :], kb[:, :], ALU.max))
                step(eng.tensor_scalar(mk[:, :], mk[:, :], 1.0, None, ALU.add))
                step(eng.tensor_scalar(hsc[:, :], mk[:, :], -float(ONE), 268.0 * ONE, ALU.mult, ALU.add))
                step(eng.tensor_scalar(inv1[:, :], k1[:, :], 25.0, float(ONE), ALU.subtract, ALU.mult))
                step(eng.tensor_tensor(inv2[:, :], mk[:, :], k2[:, :], ALU.add))
                step(eng.tensor_scalar(inv2[:, :], inv2[:, :], 155.0, float(ONE), ALU.subtract, ALU.mult))
                eng.sem_inc(sem("tables"), 1)
            else:
                need(eng, "tables", 1)
            if e == "act":
                landed(eng.dma_start(b2s[:, :, :], b2.partition_broadcast(P)), "ldb2")

        def expert_of(eng, s):
            return eng.value_load(slot_e[0:1, bass.ds(s, 1)], min_val=0, max_val=NE - 1)

        def slot(i, j):
            i, j = i + j // U, j % U
            return U * i + j, i, j

        def load_records(e, eng, i, j):
            if e == "sp":
                s, i, j = slot(i, j)
                need_dma(eng, f"add{j}", i)
                row = eng.value_load(slot_row[0:1, bass.ds(s, 1)], min_val=0, max_val=NE * REGION)
                landed(eng.dma_start(rb[j][:, :], xrec_d[bass.ds(row, P), :]), f"ldrec{j}")

        def turn_records(e, eng, i, j):
            s, i, j = slot(i, j)
            if e == "pe":
                need_dma(eng, f"ldrec{j}", i + 1)
                need(eng, "xte", s - 1)
                g = gen[j % 2][:, :].bitcast(F16)
                for k in range(2 * DC):
                    ins = eng.transpose(g[:, k * P:(k + 1) * P], rb[j][:, :].bitcast(F16)[:, k * P:(k + 1) * P],
                                        id16[:, :])
                done(ins, "xtp")
            if e == "dve":
                need(eng, "xtp", s + 1)
                need(eng, "mm1", 2 * (s - 1))
                done(eng.tensor_copy(xt[j % 2][:, :, :, :].rearrange("p s k t -> p (s k t)"),
                                     gen[j % 2][:, :].bitcast(F16)[:, 0:2 * DC * P]), "xte")

        def first_product(e, eng, i, j):
            s, i, j = slot(i, j)
            ex = expert_of(eng, s) if e in ("pe", "act", "dve") else None
            for half in range(2):
                hb = hbank[2 * (j % 2) + half]
                blocks = range(half * HC // 2, (half + 1) * HC // 2)
                if e == "pe":
                    need(eng, "xte", s + 1)
                    need(eng, "gel", 2 * (s - 2) + half + 1)
                    for m in blocks:
                        o = (m % (HC // 2)) * P
                        terms = [(k, wp, xp) for k in range(DC) for wp, xp in ((0, 0), (0, 1), (1, 0))]
                        for t, (k, wp, xp) in enumerate(terms):
                            w = w1s[:, bass.ds(ex, 1), wp, k, m * P:(m + 1) * P].rearrange("p o h -> p (o h)")
                            ins = eng.matmul(hb[:, o:o + P], w, xt[j % 2][:, xp, k, :],
                                             start=(t == 0), stop=(t == len(terms) - 1))
                    done(ins, "mm1")
                if e == "act":
                    need(eng, "mm1", 2 * s + half + 1)
                    need(eng, "lo", 2 * (s - 1) + half + 1)
                    for m in blocks:
                        o = (m % (HC // 2)) * P
                        ins = eng.activation(h32[half][:, m % (HC // 2), :], hb[:, o:o + P], ACT.Gelu,
                                             scale=inv1[:, bass.ds(ex, 1)].bitcast(F32),
                                             bias=b1t[:, bass.ds(ex, 1), m])
                    done(ins, "gel")
                if e == "dve":
                    need(eng, "gel", 2 * s + half + 1)
                    need(eng, "mm2", s - 1)
                    hi = hs[j % 2][:, 0, blocks[0]:blocks[-1] + 1, :].rearrange("p m t -> p (m t)")
                    lo = hs[j % 2][:, 1, blocks[0]:blocks[-1] + 1, :].rearrange("p m t -> p (m t)")
                    h = h32[half][:, :, :].rearrange("p m t -> p (m t)")
                    scale = hsc[:, bass.ds(ex, 1)].bitcast(F32)
                    done(eng.tensor_scalar(hi, h, scale, None, ALU.mult), "hi")
                    need(eng, "hi", 2 * s + half + 1)
                    done(eng.scalar_tensor_tensor(lo, h, scale, hi, ALU.mult, ALU.subtract), "lo")

        def second_product(e, eng, i, j):
            s, i, j = slot(i, j)
            ex = expert_of(eng, s) if e in ("pe", "dve") else None
            y = ybank[j % 2][:, 0:D]
            if e == "pe":
                need(eng, "w2_ready", ex + 1)
                need(eng, "yb", s - 1)
                for half in range(2):
                    need(eng, "lo", 2 * s + half + 1)
                    for m in range(half * HC // 2, (half + 1) * HC // 2):
                        for t, (hp, wp) in enumerate(((0, 0), (0, 1), (1, 0))):
                            w = w2s[:, bass.ds(ex, 1), wp, m, :].rearrange("p o d -> p (o d)")
                            ins = eng.matmul(y, hs[j % 2][:, hp, m, :], w, start=(m == 0 and t == 0),
                                             stop=(m == HC - 1 and t == 2))
                done(ins, "mm2")
            if e == "dve":
                need(eng, "mm2", s + 1)
                need_dma(eng, "ldb2", 1)
                need(eng, "yw", s)
                done(eng.scalar_tensor_tensor(yb[:, :], y, inv2[:, bass.ds(ex, 1)].bitcast(F32),
                                              b2s[:, bass.ds(ex, 1), :].rearrange("p o d -> p (o d)"),
                                              ALU.mult, ALU.add), "yb")
                need(eng, "yb", s + 1)
                need_dma(eng, f"add{(j - 2) % U}", i + (1 if j >= 2 else 0))
                done(eng.tensor_scalar(yw[j % 2][:, :], yb[:, :],
                                       rb[j][:, D:D + NE].bitcast(F32)[:, bass.ds(ex, 1)], None, ALU.mult), "yw")
            if e == "pool":
                need(eng, "yw", s + 1)
                need_dma(eng, f"add{(j - 1) % U}", i + (1 if j >= 1 else 0))
                settle(eng)
                landed(eng.indirect_dma_start(
                    acc_d[:, :], bass.IndirectOffsetOnAxis(ap=rb[j][:, D + NE:D + NE + 1], axis=0),
                    yw[j % 2][:, :], None, compute_op=ALU.add), f"add{j}")

        def load_w2(e, eng):
            for i in range(NE):
                if e == "sp":
                    landed(eng.dma_start(w2s[:, i, :, :, :].rearrange("q s k d -> q (s k d)"), w2s_d[i, :, :]),
                           f"ldw2_{i}")
            for i in range(NE):
                if e == "pool":
                    need_dma(eng, f"ldw2_{i}", 1)
                    eng.sem_inc(sem("w2_ready"), 1)

        def slots(e, eng):
            tables(e, eng)
            for j in range(AHEAD):
                load_records(e, eng, 0, j)
            load_w2(e, eng)
            turn_records(e, eng, 0, 0)
            turn_records(e, eng, 0, 1)
            first_product(e, eng, 0, 0)

            def one(i, j, rest):
                if rest >= AHEAD:
                    load_records(e, eng, i, j + AHEAD)
                if rest >= 2:
                    turn_records(e, eng, i, j + 2)
                if rest >= 1:
                    first_product(e, eng, i, j + 1)
                second_product(e, eng, i, j)

            for j in range(U):
                one(0, j, NSLOT)
            with eng.Fori(1, SLOOP // U) as i:
                for j in range(U):
                    one(i, j, NSLOT)
            for s in range(SLOOP, NSLOT):
                one(s // U, s % U, NSLOT - 1 - s)
            if e == "sp" or e == "act":
                for j in range(U):
                    need_dma(eng, f"add{j}", (NSLOT - 1 - j) // U + 1)
                half = slice(0, T // 2) if e == "sp" else slice(T // 2, T)
                landed(eng.dma_start(out[half, :], acc_d[half, :]), f"out_{e}")
                need_dma(eng, f"out_{e}", 1)

        with nc.Block() as block:
            @block.tensor
            def _(eng): slots("pe", eng)
            @block.scalar
            def _(eng): slots("act", eng)
            @block.vector
            def _(eng): slots("dve", eng)
            @block.gpsimd
            def _(eng): slots("pool", eng)
            @block.sync
            def _(eng): slots("sp", eng)


INPUTS = ["x", "ctx_1024", "L0_xattn_Wq", "L0_xattn_bq", "L0_xattn_Wk", "L0_xattn_bk", "L0_xattn_Wv", "L0_xattn_bv",
          "L0_xattn_Wo", "L0_xattn_bo", "L0_xattn_alpha", "L0_ffn_Wr", "L0_ffn_W1", "L0_ffn_b1", "L0_ffn_W2",
          "L0_ffn_b2"]


def kernel(**inputs):
    from concourse import bacc
    from concourse.bass_utils import run_bass_kernel_spmd

    nc = bacc.Bacc("TRN2", target_bir_lowering=False, num_devices=1)
    arrays, args = {}, []
    for name in INPUTS:
        a = np.asarray(inputs[name])
        shape = (T, D) if name in ("x", "ctx_1024") else (NH,) if name == "L0_xattn_alpha" else a.shape
        arrays[name] = np.ascontiguousarray(a.reshape(shape))
        args.append(nc.dram_tensor(name, shape, F32, kind="ExternalInput").ap())
    args.append(nc.dram_tensor("out", (T, D), F32, kind="ExternalOutput").ap())
    with ExitStack() as ctx:
        build(nc, ctx, args)
    result = run_bass_kernel_spmd(nc, [arrays], core_ids=[0])
    return result.results[0]["out"].reshape(NB, P, D)
```

```python
from contextlib import ExitStack

import numpy as np

import concourse.bass as bass
from concourse import mybir

F32, BF16, F16, I32 = mybir.dt.float32, mybir.dt.bfloat16, mybir.dt.float16, mybir.dt.int32
ALU, ACT, AX = mybir.AluOpType, mybir.ActivationFunctionType, mybir.AxisListType

P = 128
NB, D, NH, DK = 32, 256, 16, 16
NP = NB // 2
T = NB * P
DC = D // P
NE, H = 8, 1024
HC = H // P
EPS = 1e-5
TWO = 2
SLOT = TWO * P
NSLOT = 2 * T // SLOT + NE - 1
REGION = T + SLOT
REC = D + NE + 1
NSPLIT = 3
STRIP = 32
RROWS = NSPLIT * STRIP
QW = 4 * (P // 2 + 4)
VM = P // 2 + 4
X_SCALE = 2.0 ** 11
QK_SCALE = 2.0 ** 12
ONE = 1 << 23
LN2 = float(np.log(2.0))


def build(nc, ctx, io):
    (x, c, wq, bq, wk, bk, wv, bv, wo, bo, alpha, wr, w1, b1, w2, b2, out) = io

    sems = {}

    def sem(name):
        if name not in sems:
            sems[name] = ctx.enter_context(nc.semaphore(name))
        return sems[name]

    chains = {
        "dve_norms": ["mant", "ex", "exf", "ah", "signed", "p0", "r2", "p1", "r3", "parts", "y2", "n2y2",
                  "rn", "coef"],
        "dve_route": ["rmx", "rd", "rs", "rrs", "rp", "b_mx1", "b_eq1", "b_v1", "b_vm1", "b_oh1", "rq",
                  "b_mx2", "b_eq2", "b_v2", "b_vm2", "b_oh2", "rsm", "rrm", "rv1", "rv2", "rw1", "rw2", "rw",
                  "rtok", "rtk", "rhot", "ra0", "ra1", "racc", "rpos", "rm1", "rm2", "rp1", "rp2", "ridx"],
        "dve_split": ["wcl", "wexa", "wexb", "wex", "wsc"],
    }
    halves = range(4)
    chains["pe_scores"] = [f"{s}{n}" for n in halves for s in ("u", "su")]
    chains["act_tanh"] = [f"{s}{n}" for n in halves for s in ("th", "t2")]
    chains["dve_max"] = [f"{s}{n}" for n in halves for s in ("tw", "tm")]
    chains["pool_parts"] = ["unit", "lo0", "lo1"]
    chains["pool_less_max"] = [f"sb{n}" for n in halves]
    chains["pe_turn"] = [f"{s}{n}" for n in halves for s in ("ta", "tt")]
    chains["act_exp"] = [f"ex{n}{i}" for n in halves for i in range(2)]
    chains["pe_values"] = [f"pv{n}" for n in halves]
    for b_ in range(2):
        chains[f"pe_first{b_}"] = [f"xct{b_}", f"qk{b_}", f"v{b_}"]
        chains[f"pe_stack{b_}"] = [f"stq{b_}", f"stk{b_}"]
        chains[f"dve_first{b_}"] = [f"ln{b_}st", f"ln{b_}mv", f"ln{b_}ve", f"xn{b_}", f"qke{b_}", f"ve{b_}", f"n2{b_}"]
        chains[f"dve_second{b_}"] = [f"x1{b_}", f"lm{b_}st", f"lm{b_}mv", f"lm{b_}ve", f"lm{b_}rx", f"y{b_}",
                                 f"rh{b_}", f"rl{b_}"]
    owner = lambda chain: chain.split("_")[0]
    place = {name: (chain, i, len(names)) for chain, names in chains.items() for i, name in enumerate(names)}

    def done(ins, name):
        ins.then_inc(sem(place[name][0] if name in place else name), 1)

    def landed(ins, name):
        ins.then_inc(sem(name), 16)

    def need(eng, name, count):
        if isinstance(count, int) and count <= 0 or isinstance(eng, Rehearsal):
            return
        if name in place:
            name, i, m = place[name]
            count = count * m + i + 1
        eng.wait_ge(sem(name), count)
        if eng is nc.sync and not isinstance(count, int):
            settle(eng)

    def settle(eng):
        eng.sem_inc(sem("settled"), 1)

    def need_dma(eng, name, count):
        if isinstance(count, int) and count <= 0 or isinstance(eng, Rehearsal):
            return
        eng.wait_ge(sem(name), count * 16)
        if eng is nc.sync and not isinstance(count, int):
            settle(eng)

    xrec_d = nc.dram_tensor("xrec", [NE * REGION + SLOT, REC], I32).ap()
    w2s_d = nc.dram_tensor("w2s", [NE, P, 2 * HC * D], F16).ap()

    def alloc(stack, name, shape, dt):
        return stack.enter_context(nc.sbuf_tensor(name, shape, dt))

    def bank(name, shape, dt):
        return ctx.enter_context(nc.psum_tensor(name, shape, dt))

    w1s = alloc(ctx, "w1s", [P, NE, 2, DC, H], F16)
    id16 = alloc(ctx, "id16", [P, P], F16)
    ones_f = alloc(ctx, "ones_f", [P, P], F32)
    k1 = alloc(ctx, "k1", [P, NE], I32)
    k2 = alloc(ctx, "k2", [P, NE], I32)
    kb = alloc(ctx, "kb", [P, NE], I32)
    b1t = alloc(ctx, "b1t", [P, NE, HC], F32)
    acc_cnt = alloc(ctx, "acc_cnt", [P, NE], BF16)
    ebase = alloc(ctx, "ebase", [P, 2, NE], F32)
    cnt_f = alloc(ctx, "cnt_f", [P, NE], F32)
    ones_b = alloc(ctx, "ones_b", [P, P], BF16)

    tiles_i = alloc(ctx, "tiles_i", [P, NE], I32)
    tiles = alloc(ctx, "tiles", [P, NE], F32)
    ends = alloc(ctx, "ends", [P, NE], F32)
    unit = alloc(ctx, "unit_row", [P, NE], F32)
    slot_n = alloc(ctx, "slot_n", [1, NSLOT, NE], I32)
    slot_f = alloc(ctx, "slot_f", [1, NSLOT, NE], F32)
    past = alloc(ctx, "past", [1, NSLOT, NE], F32)
    before = alloc(ctx, "before", [1, NSLOT, NE], F32)
    n_past = alloc(ctx, "n_past", [1, NSLOT], F32)
    start = alloc(ctx, "start", [1, NSLOT], F32)
    rowf = alloc(ctx, "rowf", [1, NSLOT], F32)
    slot_e = alloc(ctx, "slot_e", [1, NSLOT], I32)
    slot_row = alloc(ctx, "slot_row", [1, NSLOT], I32)
    mk = alloc(ctx, "mk", [P, NE], I32)
    hsc = alloc(ctx, "hsc", [P, NE], I32)
    inv1 = alloc(ctx, "inv1", [P, NE], I32)
    inv2 = alloc(ctx, "inv2", [P, NE], I32)
    cnt_i = alloc(ctx, "cnt_i", [P, NE], I32)

    s_ps = bank("s_ps", [P, 2, 512], F32)
    u_ps = bank("u_ps", [P, 1024], F32)
    pv_ps = bank("pv_ps", [P, 512], F32)
    gen = [bank(f"gen{i}", [P, 512], F32) for i in range(3)]

    class Turns:
        section, n, freed, given = 0, 0, [None] * 3, {}

    class Rehearsal:
        def __getattr__(self, _):
            return lambda *args, **kw: self

    def start_section(k, freed=(None,) * 3):
        Turns.section, Turns.n, Turns.freed = k, 0, list(freed)

    def turn(pe, what, name, count):
        i = Turns.n % 3
        Turns.n += 1
        if Turns.freed[i]:
            need(pe, *Turns.freed[i])
        Turns.freed[i] = (name, count)
        Turns.given[Turns.section, what] = gen[i]
        return gen[i]

    def given(what):
        return Turns.given[Turns.section, what]

    with ExitStack() as a:
        wq_sb = alloc(a, "wq_sb", [P, DC, D], F32)
        wk_sb = alloc(a, "wk_sb", [P, DC, D], F32)
        wv_sb = alloc(a, "wv_sb", [P, DC, D], F32)
        wo_sb = alloc(a, "wo_sb", [P, DC, D], F32)
        wr_sb = alloc(a, "wr_sb", [P, DC, NE], F32)
        bqk = alloc(a, "bqk", [P, 2 * D], F32)
        bv_sb = alloc(a, "bv_sb", [P, D], F32)
        bo_sb = alloc(a, "bo_sb", [P, D], F32)
        al = alloc(a, "al", [P, NH], F32)
        amax = alloc(a, "amax", [P, 1], F32)
        abig = alloc(a, "abig", [P, 1], I32)
        arec = alloc(a, "arec", [P, 1], I32)
        escale = alloc(a, "escale", [P, 1], F32)
        colscale = alloc(a, "colscale", [P, 2 * NH], F32)
        signs = alloc(a, "signs", [P, 2 * NH], F32)
        idf = alloc(a, "idf", [P, P], F32)
        idb = alloc(a, "idb", [P, P], BF16)
        lstrict = alloc(a, "lstrict", [P, P], BF16)
        rank8 = alloc(a, "rank8", [P, 2, NE], F32)
        padrec = alloc(a, "padrec", [P, REC], I32)
        zrow = alloc(a, "zrow", [P, D], F32)
        mhalf = alloc(a, "mhalf", [P, 1], F32)
        io8 = alloc(a, "io8", [P, 2, NE], I32)
        tok = alloc(a, "tok", [P, 1], I32)
        wl = alloc(a, "wl", [P, 2048], F32)
        wst = alloc(a, "wst", [P, 2, 2048], F16)
        wss = alloc(a, "wss", [P, 1], F32)
        wkk = alloc(a, "wkk", [P, 1], I32)
        wsc = alloc(a, "wsc", [P, 1], I32)
        wcl = alloc(a, "wcl", [P, 1], F32)
        pair = lambda name, shape, dt: [alloc(a, f"{name}{b}", shape, dt) for b in range(2)]
        xin, cin, xn = pair("xin", [P, D], F32), pair("cin", [P, D], F32), pair("xn", [P, D], F32)
        xct = pair("xct", [P, 2 * DC, P], F32)
        norm_bufs = {name: [[alloc(a, f"{name}{b}_{k}", [P, w], F32) for k, w in (("st6", 6), ("mv", 2), ("var", 1), ("rstd", 1))]
                            for b in range(2)] for name in ("ln", "lm")}
        qk = alloc(a, "qk", [P, 2, 2 * NH, DK], F32)
        qks = alloc(a, "qks", [P, 2, 2 * NH, DK], F32)
        vn = pair("vn", [P, D], F32)
        n2 = alloc(a, "n2", [P, 2, 2 * NH], F32)
        na = {k: alloc(a, f"na_{k}", [P, 2, 2 * NH], I32 if k in ("mant", "ex") else F32)
              for k in ("mant", "ex", "exf", "ln", "ah", "y", "y2", "n2y2", "rn", "coef", "r1", "r2")}
        ar = alloc(a, "ar", [P, 2, 2, RROWS], BF16)
        qks16 = pair("qks16", [P, 2 * NH, 4, DK], F16)
        qt, kt = pair("qt", [P, NH // 2, P], F16), pair("kt", [P, NH // 2, P], F16)
        aq = pair("aq", [RROWS + NSPLIT, P], BF16)
        kbr = pair("kbr", [RROWS, P], BF16)
        uk = pair("uk", [RROWS + NSPLIT, NH * P], BF16)
        vz = pair("vz", [P, 4, 4, VM + 16], F32)
        th, tw = pair("th", [P, 1024], F32), pair("tw", [P, 2, 4, P], F32)
        tm = pair("tm", [P, 8], F32)
        pt = pair("pt", [P, 2, 512], F32)
        osb = alloc(a, "osb", [VM, 512], F32)
        rz = alloc(a, "rz", [P, 4, 4], F32)
        on = alloc(a, "on", [P, D], F32)
        ot = alloc(a, "ot", [P, DC, P], F32)
        xres, xb = pair("xres", [P, D], F32), pair("xb", [P, D], F32)
        x1 = pair("x1", [P, D], F32)
        xn2 = pair("xn2", [P, D], F32)
        xn2t = alloc(a, "xn2t", [P, DC, P], F32)
        rec = alloc(a, "rec", [P, 2, REC], I32)
        r = {k: alloc(a, f"r_{k}", [P, 2, NE], F32)
             for k in ("l", "d", "e", "p", "q", "eq", "v", "oh1", "oh2", "w1", "w2", "pos", "m1", "m2")}
        rs = {k: alloc(a, f"rs_{k}", [P, 2], F32)
              for k in ("mx", "s", "rs", "p1", "vm", "p2", "sm", "rsm", "v1", "v2", "pos1", "pos2")}
        hot = alloc(a, "hot", [P, 2, NE], BF16)
        acc2 = alloc(a, "acc2", [P, 2, NE], BF16)
        idx = alloc(a, "idx", [P, 2, 2], I32)
        b1r = alloc(a, "b1r", [NE * HC, P], F32)
        b1q = alloc(a, "b1q", [P, NE, HC], F32)
        b1ss = alloc(a, "b1ss", [P, NE], F32)

        def load_stage(b):
            def go(e, eng, p):
                if e != "sp":
                    return
                row = (2 * p + b) * P
                need(eng, f"xn{b}", p)
                landed(eng.dma_start(xin[b][:, :], x[bass.ds(row, P), :]), f"ldx{b}")
                need(eng, f"xct{b}", p)
                landed(eng.dma_start(cin[b][:, :], c[bass.ds(row, P), :]), f"ldc{b}")
            return go

        def statistics(e, eng, src, b, name, count):
            st6, mv, var, rstd = norm_bufs[name][b]
            name = f"{name}{b}"
            if e == "dve":
                done(eng.bn_stats(st6[:, :], src), name + "st")
                need(eng, name + "st", count)
                settle(eng)
                done(eng.bn_aggr(mv[:, :], st6[:, :]), name + "mv")
                need(eng, name + "mv", count)
                done(eng.tensor_scalar(var[:, :], mv[:, 1:2], EPS, None, ALU.add), name + "ve")
            if e == "pool":
                need(eng, name + "ve", count)
                done(eng.tensor_tensor(rstd[:, :], var[:, :], mhalf[:, :], ALU.pow), name + "rs")

        def normalised(eng, src, b, name, count, dst, scale=1.0):
            _, mv, _, rstd = norm_bufs[name][b]
            name = f"{name}{b}"
            need(eng, name + "rs", count)
            if scale != 1.0:
                done(eng.tensor_scalar(rstd[:, :], rstd[:, :], scale, None, ALU.mult), name + "rx")
                need(eng, name + "rx", count)
            return eng.tensor_scalar(dst, src, mv[:, 0:1], rstd[:, :], ALU.subtract, ALU.mult)

        def means_in(b):
            def go(e, eng, p):
                if e == "dve":
                    need_dma(eng, f"ldx{b}", p + 1)
                    need(eng, f"xn{b}", p)
                statistics(e, eng, xin[b][:, :], b, "ln", p + 1)
            return go

        def norm_in(b):
            def go(e, eng, p):
                if e == "dve":
                    need(eng, f"xct{b}", p)
                    done(normalised(eng, xin[b][:, :], b, "ln", p + 1, xn[b][:, :]), f"xn{b}")
                if e == "pe":
                    g = turn(eng, f"xct{b}", f"xce{b}", p + 1)
                    need(eng, f"xn{b}", p + 1)
                    need_dma(eng, f"ldc{b}", p + 1)
                    for i, src in enumerate((xn[b], cin[b])):
                        for k in range(DC):
                            o = (DC * i + k) * P
                            ins = eng.transpose(g[:, o:o + P], src[:, k * P:(k + 1) * P], idf[:, :])
                    done(ins, f"xct{b}")
                if e == "act":
                    need(eng, f"xct{b}", p + 1)
                    need(eng, f"v{b}", p)
                    done(eng.activation(xct[b][:, :, :], given(f"xct{b}")[:, :].rearrange("p (a t) -> p a t", t=P),
                                        ACT.Copy), f"xce{b}")
            return go

        def project(b):
            def go(e, eng, p):
                if e == "pe":
                    need(eng, f"xce{b}", p + 1)
                    g = turn(eng, f"qk{b}", f"qke{b}", p + 1)
                    for i, w in ((0, wq_sb), (1, wk_sb)):
                        for k in range(DC):
                            ins = eng.matmul(g[:, i * D:(i + 1) * D], xct[b][:, DC * i + k, :], w[:, k, :],
                                             start=(k == 0), stop=(k == DC - 1))
                    done(ins, f"qk{b}")
                    g = turn(eng, f"v{b}", f"ve{b}", p + 1)
                    for k in range(DC):
                        ins = eng.matmul(g[:, 0:D], xct[b][:, DC + k, :], wv_sb[:, k, :],
                                         start=(k == 0), stop=(k == DC - 1))
                    done(ins, f"v{b}")
                if e == "dve":
                    need(eng, f"qk{b}", p + 1)
                    need(eng, "unit", p)
                    done(eng.tensor_tensor(qk[:, b, :, :].rearrange("p h d -> p (h d)"),
                                           given(f"qk{b}")[:, :], bqk[:, :], ALU.add), f"qke{b}")
                    need(eng, f"v{b}", p + 1)
                    need(eng, f"vz{b}", p)
                    done(eng.tensor_tensor(vn[b][:, :], given(f"v{b}")[:, 0:D], bv_sb[:, :], ALU.add), f"ve{b}")
            return go

        def squares(b):
            def go(e, eng, p):
                if e == "act":
                    need(eng, f"qke{b}", p + 1)
                    need(eng, "lo1", p)
                    done(eng.activation(qks[:, b, :, :], qk[:, b, :, :], ACT.Square), f"sq{b}")
                if e == "dve":
                    need(eng, f"sq{b}", p + 1)
                    need(eng, "n2y2", p)
                    done(eng.tensor_reduce(n2[:, b, :], qks[:, b, :, :], AX.X, ALU.add), f"n2{b}")
            return go

        def norms(piece):
            def go(e, eng, p):
                n = p + 1
                def step(ins, name):
                    done(ins, name)
                    need(eng, name, n)
                if piece == 1:
                    if e == "dve":
                        need(eng, "n20", n)
                        need(eng, "n21", n)
                        need(eng, "nln", p)
                        step(eng.tensor_scalar(na["mant"][:, :, :], n2[:, :, :].bitcast(I32), ONE - 1, 127 * ONE,
                                               ALU.bitwise_and, ALU.bitwise_or), "mant")
                        step(eng.tensor_scalar(na["ex"][:, :, :], n2[:, :, :].bitcast(I32), 23, None,
                                               ALU.logical_shift_right), "ex")
                        step(eng.tensor_scalar(na["exf"][:, :, :], na["ex"][:, :, :], -127.0, 0.5 * LN2,
                                               ALU.add, ALU.mult), "exf")
                    if e == "act":
                        need(eng, "mant", n)
                        done(eng.activation(na["ln"][:, :, :], na["mant"][:, :, :].bitcast(F32), ACT.Ln), "nln")
                if piece == 2:
                    if e == "dve":
                        need(eng, "nln", n)
                        need(eng, "ny", p)
                        step(eng.scalar_tensor_tensor(na["ah"][:, :, :], na["ln"][:, :, :], 0.5, na["exf"][:, :, :],
                                                      ALU.mult, ALU.add), "ah")
                    if e == "act":
                        need(eng, "ah", n)
                        need(eng, "rn", p)
                        done(eng.activation(na["y"][:, :, :], na["ah"][:, :, :], ACT.Exp, scale=-1.0), "ny")
                if piece == 3:
                    if e == "dve":
                        sgn = na["r1"]
                        need(eng, "rows_t", p)
                        step(eng.tensor_tensor(sgn[:, :, :], na["ah"][:, :, :],
                                               signs[:, :].unsqueeze(1).to_broadcast([P, 2, 2 * NH]), ALU.mult),
                             "signed")
                        part = lambda i: ar[:, :, :, i * STRIP:i * STRIP + NH]
                        v4 = lambda t: t[:, :, :].rearrange("p b (i h) -> p b i h", h=NH)
                        step(eng.tensor_copy(part(0), v4(sgn)), "p0")
                        step(eng.tensor_tensor(v4(na["r2"]), v4(sgn), part(0), ALU.subtract), "r2")
                        step(eng.tensor_copy(part(1), v4(na["r2"])), "p1")
                        step(eng.tensor_tensor(v4(sgn), v4(na["r2"]), part(1), ALU.subtract), "r3")
                        step(eng.tensor_copy(part(2), v4(sgn)), "parts")
                if piece == 4:
                    if e == "dve":
                        need(eng, "ny", n)
                        step(eng.tensor_tensor(na["y2"][:, :, :], na["y"][:, :, :], na["y"][:, :, :], ALU.mult), "y2")
                        step(eng.tensor_tensor(na["n2y2"][:, :, :], na["y2"][:, :, :], n2[:, :, :], ALU.mult), "n2y2")
                        step(eng.scalar_tensor_tensor(na["rn"][:, :, :], na["n2y2"][:, :, :], -3.0, na["y"][:, :, :],
                                                      ALU.add, ALU.mult), "rn")
                        need(eng, "unit", p)
                        step(eng.tensor_tensor(na["coef"][:, :, :], na["rn"][:, :, :],
                                               colscale[:, :].unsqueeze(1).to_broadcast([P, 2, 2 * NH]), ALU.mult),
                             "coef")
                    if e == "pool":
                        need(eng, "coef", n)
                        for b in range(2):
                            ins = eng.tensor_tensor(qks[:, b, :, :], qk[:, b, :, :],
                                                    na["coef"][:, b, :].unsqueeze(2).to_broadcast([P, 2 * NH, DK]),
                                                    ALU.mult)
                        done(ins, "unit")
            return go

        def parts_of(b):
            def go(e, eng, p):
                n = p + 1
                part = lambda i, s0, ds: qks16[b][:, NH * i:NH * (i + 1), s0:s0 + ds + 1:ds, :]
                both = lambda t, i: t[:, NH * i:NH * (i + 1), :].unsqueeze(2).to_broadcast([P, NH, 2, DK])
                if e == "act":
                    need(eng, "unit", n)
                    need(eng, f"stk{b}", p)
                    eng.activation(part(0, 0, 1), both(qks[:, b, :, :], 0), ACT.Copy)
                    done(eng.activation(part(1, 0, 2), both(qks[:, b, :, :], 1), ACT.Copy), f"hi{b}")
                if e == "pool":
                    need(eng, f"hi{b}", n)
                    need(eng, "unit", n)
                    for i, s0, ds in ((0, 2, 1), (1, 1, 2)):
                        ins = eng.tensor_tensor(part(i, s0, ds), both(qks[:, b, :, :], i),
                                                both(qks16[b][:, :, 0, :], i), ALU.subtract)
                    done(ins, f"lo{b}")
            return go

        def rows(e, eng, p):
            n = p + 1
            if e == "pe":
                need(eng, "parts", n)
                g = turn(eng, "rows_t", "rowk1", n)
                gb = g[:, :].bitcast(BF16)
                for b in range(2):
                    for i in range(2):
                        o = (2 * b + i) * P
                        ins = eng.transpose(gb[0:RROWS, o:o + P], ar[:, b, i, :], idb[:, :])
                done(ins, "rows_t")
            if e == "dve":
                gb = given("rows_t")[:, :].bitcast(BF16)
                need(eng, "rows_t", n)
                for b in range(2):
                    need(eng, f"su{2 * b + 1}", p)
                    done(eng.tensor_copy(aq[b][0:RROWS, :], gb[0:RROWS, 2 * b * P:(2 * b + 1) * P]), f"rowq{b}")
                    need_dma(eng, f"flat{b}", 2 * NSPLIT * p)
                    done(eng.tensor_copy(kbr[b][:, :], gb[0:RROWS, (2 * b + 1) * P:(2 * b + 2) * P]), f"rowk{b}")
            if e == "sp":
                for b in range(2):
                    need(eng, f"rowk{b}", n)
                    need(eng, f"su{2 * b + 1}", p)
                    for s in range(NSPLIT):
                        for par in range(2):
                            dst = uk[b][RROWS + s:RROWS + s + 1, par * 1024:(par + 1) * 1024]
                            src = kbr[b][s * STRIP + par:s * STRIP + NH:2, :]
                            landed(eng.dma_start(dst.rearrange("o (j k) -> o j k", k=P), src), f"flat{b}")

        def stack(b):
            def go(e, eng, p):
                n = p + 1
                if e == "pe":
                    need(eng, f"lo{b}", n)
                    for i, to in ((0, "qte"), (1, "kte")):
                        g = turn(eng, f"{to}{b}", f"{to}{b}", n)
                        gh = g[:, :].bitcast(F16)
                        for j in range(NH // 2):
                            h = NH * i + 2 * j
                            src = qks16[b][:, h:h + 2, :, :].rearrange("p h s d -> p (h s d)")
                            ins = eng.transpose(gh[:, j * P:(j + 1) * P], src, id16[:, :])
                        done(ins, f"stk{b}" if i else f"stq{b}")
                if e == "act":
                    need(eng, f"stq{b}", n)
                    need(eng, f"su{2 * b + 1}", p)
                    done(eng.activation(qt[b][:, :, :], given(f"qte{b}")[:, :].bitcast(F16)
                                        .rearrange("p (j t) -> p j t", t=P), ACT.Copy), f"qte{b}")
                if e == "dve":
                    need(eng, f"stk{b}", n)
                    need(eng, f"su{2 * b + 1}", p)
                    done(eng.tensor_copy(kt[b][:, :, :], given(f"kte{b}")[:, :].bitcast(F16)
                                         .rearrange("p (j t) -> p j t", t=P)), f"kte{b}")
                if e == "pool":
                    need(eng, f"ve{b}", n)
                    need(eng, f"pv{2 * b + 1}", p)
                    settle(eng)
                    for h in range(2):
                        ins = eng.tensor_copy(
                            vz[b][:, 2 * h:2 * h + 2, :, 0:DK],
                            vn[b][:, h * P:(h + 1) * P].rearrange("p (j a d) -> p a j d", a=2, d=DK))
                    done(ins, f"vz{b}")
            return go

        def factors(n_):
            b, h = divmod(n_, 2)
            def go(e, eng, p):
                n = p + 1
                prev = (n_ - 1) % 4
                pc = n if n_ else p
                if e == "pe":
                    need(eng, f"rowq{b}", n)
                    need_dma(eng, f"flat{b}", 2 * NSPLIT * n)
                    need(eng, f"th{prev}", pc)
                    for i in range(2):
                        o = i * 1024 + h * 512
                        ins = eng.matmul(u_ps[:, i * 512:(i + 1) * 512], aq[b][:, :], uk[b][:, o:o + 512],
                                         start=True, stop=True)
                    done(ins, f"u{n_}")
                if e == "act":
                    need(eng, f"u{n_}", n)
                    need(eng, f"tw{n_ ^ 2}", n if n_ >= 2 else p)
                    done(eng.activation(th[h][:, :], u_ps[:, :], ACT.Tanh, scale=0.5), f"th{n_}")
                    need(eng, f"th{n_}", n)
                    done(eng.activation(th[h][:, :], th[h][:, :], ACT.Square), f"t2{n_}")
            return go

        def scores(n_):
            b, h = divmod(n_, 2)
            def go(e, eng, p):
                n = p + 1
                prev = (n_ - 1) % 4
                pc = n if n_ else p
                if e == "pe":
                    need(eng, f"qte{b}", n)
                    need(eng, f"kte{b}", n)
                    need(eng, f"tw{prev}", pc)
                    for j in range(4):
                        for i in range(2):
                            rws = slice(64 * i, 64 * i + 64)
                            ins = eng.matmul(s_ps[:, i, j * P:(j + 1) * P], qt[b][rws, 4 * h + j, :],
                                             kt[b][rws, 4 * h + j, :], start=True, stop=True)
                    done(ins, f"su{n_}")
                if e == "dve":
                    need(eng, f"t2{n_}", n)
                    need(eng, f"su{n_}", n)
                    need(eng, f"tt{n_ ^ 2}", n if n_ >= 2 else p)
                    twf = tw[h][:, :, :, :].rearrange("p i j k -> p (i j k)")
                    done(eng.scalar_tensor_tensor(twf, th[h][:, :], -1.0,
                                                  s_ps[:, :, :].rearrange("p i k -> p (i k)"),
                                                  ALU.add, ALU.mult), f"tw{n_}")
                    need(eng, f"tw{n_}", n)
                    need(eng, f"sb{n_ ^ 2}", n if n_ >= 2 else p)
                    done(eng.tensor_reduce(tm[h][:, :], tw[h][:, :, :, :].rearrange("p i j k -> p (i j) k"),
                                           AX.X, ALU.max), f"tm{n_}")
                if e == "pool":
                    need(eng, f"tm{n_}", n)
                    v = tw[h][:, :, :, :].rearrange("p i j k -> p (i j) k")
                    done(eng.tensor_tensor(v, v, tm[h][:, :].unsqueeze(2).to_broadcast([P, 8, P]),
                                           ALU.subtract), f"sb{n_}")
            return go

        def turned(n_, i):
            b, h = divmod(n_, 2)
            def go(e, eng, p):
                n = p + 1
                if e == "pe":
                    if i == 0:
                        need(eng, f"sb{n_}", n)
                    g = turn(eng, f"ex{n_}{i}", f"ex{n_}{i}", n)
                    for j in range(4):
                        ins = eng.transpose(g[:, j * P:(j + 1) * P], tw[h][:, i, j, :], idf[:, :])
                    done(ins, f"tt{n_}" if i else f"ta{n_}")
                if e == "act":
                    need(eng, f"tt{n_}" if i else f"ta{n_}", n)
                    need(eng, f"pv{n_ ^ 2}", n if n_ >= 2 else p)
                    done(eng.activation(pt[h][:, i, :], given(f"ex{n_}{i}")[:, :], ACT.Exp,
                                        scale=escale[:, :]), f"ex{n_}{i}")
            return go

        def values(n_):
            b, h = divmod(n_, 2)
            def go(e, eng, p):
                n = p + 1
                if e == "pe":
                    need(eng, f"vz{b}", n)
                    if h == 0:
                        need(eng, "osb", 2 * p + b)
                    for i in range(2):
                        need(eng, f"ex{n_}{i}", n)
                        q = 2 * h + i
                        for j in range(4):
                            vq = vz[b][:, q, :, :].rearrange("p j m -> p (j m)")
                            ins = eng.matmul(pv_ps[0:VM, q * P:(q + 1) * P], vq[:, j * VM:(j + 1) * VM],
                                             pt[h][:, i, j * P:(j + 1) * P], start=(j == 0), stop=(j == 3))
                    done(ins, f"pv{n_}")
            return go

        def back(b, part):
            def go(e, eng, p):
                n, m = p + 1, 2 * p + b + 1
                if part == 0:
                    if e == "sp":
                        need(eng, f"xb{b}", p)
                        landed(eng.dma_start(xres[b][:, :], x[bass.ds((2 * p + b) * P, P), :]), f"ldr{b}")
                    if e == "pool":
                        need_dma(eng, f"ldr{b}", n)
                        need(eng, f"x1{b}", p)
                        done(eng.tensor_tensor(xb[b][:, :], xres[b][:, :], bo_sb[:, :], ALU.add), f"xb{b}")
                if part == 1:
                    if e == "act":
                        need(eng, f"pv{2 * b + 1}", n)
                        need(eng, "ob", m - 1)
                        done(eng.activation(osb[:, :], pv_ps[0:VM, :], ACT.Copy), "osb")
                    if e == "pe":
                        g = turn(eng, f"ob{b}", "on", m)
                        need(eng, "osb", m)
                        for q in range(4):
                            ins = eng.transpose(g[:, q * P:q * P + VM], osb[:, q * P:(q + 1) * P],
                                                idf[0:VM, 0:VM])
                        done(ins, "ob")
                    if e == "dve":
                        g = given(f"ob{b}")[:, :].rearrange("p (q c) -> p q c", q=4)
                        need(eng, "ob", m)
                        done(eng.reciprocal(rz[:, :, :], g[:, :, 4 * DK:4 * DK + 4]), "rz")
                        need(eng, "rz", m)
                        need(eng, "oc", m - 1)
                        for h in range(2):
                            ins = eng.tensor_tensor(
                                on[:, h * P:(h + 1) * P].rearrange("p (j a d) -> p a j d", a=2, d=DK),
                                g[:, 2 * h:2 * h + 2, 0:4 * DK].rearrange("p a (j d) -> p a j d", d=DK),
                                rz[:, 2 * h:2 * h + 2, :].unsqueeze(3).to_broadcast([P, 2, 4, DK]), ALU.mult)
                        done(ins, "on")
                if part == 2:
                    if e == "pe":
                        g = turn(eng, f"oc{b}", "ote", m)
                        need(eng, "on", m)
                        for k in range(DC):
                            ins = eng.transpose(g[:, k * P:(k + 1) * P], on[:, k * P:(k + 1) * P], idf[:, :])
                        done(ins, "oc")
                    if e == "act":
                        need(eng, "oc", m)
                        need(eng, "wo", m - 1)
                        done(eng.activation(ot[:, :, :], given(f"oc{b}")[:, 0:D]
                                            .rearrange("p (k t) -> p k t", t=P), ACT.Copy), "ote")
                if part == 3:
                    if e == "pe":
                        g = turn(eng, f"wo{b}", f"x1{b}", n)
                        need(eng, "ote", m)
                        for k in range(DC):
                            ins = eng.matmul(g[:, 0:D], ot[:, k, :], wo_sb[:, k, :], start=(k == 0),
                                             stop=(k == DC - 1))
                        done(ins, "wo")
                    if e == "dve":
                        need(eng, "wo", m)
                        need(eng, f"xb{b}", n)
                        need_dma(eng, f"stx{b}", p)
                        done(eng.tensor_tensor(x1[b][:, :], given(f"wo{b}")[:, 0:D], xb[b][:, :], ALU.add), f"x1{b}")
                        need(eng, f"x1{b}", n)
                        need(eng, f"y{b}", p)
                    statistics(e, eng, x1[b][:, :], b, "lm", n)
                    if e == "sp":
                        need(eng, f"x1{b}", n)
                        landed(eng.dma_start(out[bass.ds((2 * p + b) * P, P), :], x1[b][:, :]), f"stx{b}")
                if part == 4:
                    if e == "dve":
                        need(eng, f"xu{b}", p)
                        done(normalised(eng, x1[b][:, :], b, "lm", n, xn2[b][:, :], X_SCALE), f"y{b}")
                        need_dma(eng, "scat", 4 * p)
                        need(eng, f"y{b}", n)
                        done(eng.tensor_copy(rec[:, b, :].bitcast(F16)[:, 0:D], xn2[b][:, :]), f"rh{b}")
                        need(eng, f"rh{b}", n)
                        done(eng.tensor_tensor(rec[:, b, :].bitcast(F16)[:, D:2 * D], xn2[b][:, :],
                                               rec[:, b, :].bitcast(F16)[:, 0:D], ALU.subtract), f"rl{b}")
                    if e == "pe":
                        g = turn(eng, f"xu{b}", "xue", m)
                        need(eng, f"y{b}", n)
                        for k in range(DC):
                            ins = eng.transpose(g[:, k * P:(k + 1) * P], xn2[b][:, k * P:(k + 1) * P], idf[:, :])
                        done(ins, f"xu{b}")
                    if e == "act":
                        need(eng, f"xu{b}", n)
                        need(eng, "lg", m - 1)
                        done(eng.activation(xn2t[:, :, :], given(f"xu{b}")[:, 0:D]
                                            .rearrange("p (k t) -> p k t", t=P), ACT.Copy), "xue")
                if part == 5:
                    if e == "pe":
                        g = turn(eng, f"lg{b}", f"rl_{b}", n)
                        need(eng, "xue", m)
                        for k in range(DC):
                            ins = eng.matmul(g[:, 0:NE], xn2t[:, k, :], wr_sb[:, k, :], start=(k == 0),
                                             stop=(k == DC - 1))
                        done(ins, "lg")
                    if e == "dve":
                        need(eng, "lg", m)
                        need(eng, "rd", p)
                        done(eng.tensor_scalar(r["l"][:, b, :], given(f"lg{b}")[:, 0:NE], 1.0 / X_SCALE, None,
                                               ALU.mult), f"rl_{b}")
            return go

        def route(piece):
            def go(e, eng, p):
                n = p + 1
                wide = lambda t: rs[t][:, :].unsqueeze(2).to_broadcast([P, 2, NE])
                f = lambda t: r[t][:, :, :]
                def step(ins, name):
                    done(ins, name)
                    need(eng, name, n)

                def best(src, i):
                    top, oh = f"p{i}", f"oh{i}"
                    step(eng.tensor_reduce(rs[top][:, :], f(src), AX.X, ALU.max), f"b_mx{i}")
                    step(eng.tensor_tensor(f("eq"), f(src), wide(top), ALU.is_equal), f"b_eq{i}")
                    step(eng.tensor_tensor(f("v"), f("eq"), rank8[:, :, :], ALU.mult), f"b_v{i}")
                    step(eng.tensor_reduce(rs["vm"][:, :], f("v"), AX.X, ALU.max), f"b_vm{i}")
                    step(eng.tensor_tensor(f(oh), f("v"), wide("vm"), ALU.is_equal), f"b_oh{i}")

                if piece == 1:
                    if e == "dve":
                        need(eng, "rl_0", n)
                        need(eng, "rl_1", n)
                        step(eng.tensor_reduce(rs["mx"][:, :], f("l"), AX.X, ALU.max), "rmx")
                        need(eng, "re", p)
                        step(eng.tensor_tensor(f("d"), f("l"), wide("mx"), ALU.subtract), "rd")
                    if e == "act":
                        need(eng, "rd", n)
                        need(eng, "rp", p)
                        done(eng.activation(f("e"), f("d"), ACT.Exp), "re")
                if piece == 2:
                    if e == "dve":
                        need(eng, "re", n)
                        step(eng.tensor_reduce(rs["s"][:, :], f("e"), AX.X, ALU.add), "rs")
                        step(eng.reciprocal(rs["rs"][:, :], rs["s"][:, :]), "rrs")
                        step(eng.tensor_tensor(f("p"), f("e"), wide("rs"), ALU.mult), "rp")

                        best("p", 1)
                        step(eng.scalar_tensor_tensor(f("q"), f("oh1"), -2.0, f("p"), ALU.mult, ALU.add), "rq")
                        best("q", 2)
                if piece == 3:
                    if e == "dve":
                        step(eng.tensor_tensor(rs["sm"][:, :], rs["p1"][:, :], rs["p2"][:, :], ALU.add), "rsm")
                        step(eng.reciprocal(rs["rsm"][:, :], rs["sm"][:, :]), "rrm")
                        step(eng.tensor_tensor(rs["v1"][:, :], rs["p1"][:, :], rs["rsm"][:, :], ALU.mult), "rv1")
                        step(eng.tensor_tensor(rs["v2"][:, :], rs["p2"][:, :], rs["rsm"][:, :], ALU.mult), "rv2")
                        step(eng.tensor_tensor(f("w1"), f("oh1"), wide("v1"), ALU.mult), "rw1")
                        step(eng.tensor_tensor(f("w2"), f("oh2"), wide("v2"), ALU.mult), "rw2")
                if piece == 4:
                    if e == "dve":
                        recf = rec[:, :, :].bitcast(F32)
                        done(eng.tensor_tensor(recf[:, :, D:D + NE], f("w1"), f("w2"), ALU.add), "rw")
                        reci = rec[:, :, :]
                        for b in range(2):
                            ins = eng.tensor_scalar(reci[:, b, D + NE:D + NE + 1], tok[:, :], float(b * P), None, ALU.add)
                        step(ins, "rtok")
                        step(eng.tensor_scalar(tok[:, :], tok[:, :], float(2 * P), None, ALU.add), "rtk")
                        need(eng, "rank", p)
                        step(eng.tensor_tensor(hot[:, :, :], f("oh1"), f("oh2"), ALU.add), "rhot")
                        step(eng.tensor_copy(acc2[:, 0, :], acc_cnt[:, :]), "ra0")
                        step(eng.tensor_tensor(acc2[:, 1, :], acc_cnt[:, :], hot[:, 0, :], ALU.add), "ra1")
                        step(eng.tensor_tensor(acc_cnt[:, :], acc2[:, 1, :], hot[:, 1, :], ALU.add), "racc")
                    if e == "pe":
                        g = turn(eng, "rank", "rpos", n)
                        need(eng, "racc", n)
                        eng.matmul(g[:, 0:2 * NE], lstrict[:, :], hot[:, :, :].rearrange("p b e -> p (b e)"),
                                   start=True, stop=False)
                        done(eng.matmul(g[:, 0:2 * NE], ones_b[:, :], acc2[:, :, :].rearrange("p b e -> p (b e)"),
                                        start=False, stop=True), "rank")
                if piece == 5:
                    if e == "dve":
                        need(eng, "rank", n)
                        step(eng.tensor_tensor(f("pos"), given("rank")[:, 0:2 * NE].rearrange("p (b e) -> p b e", e=NE),
                                               ebase[:, :, :], ALU.add), "rpos")
                        step(eng.tensor_tensor(f("m1"), f("oh1"), f("pos"), ALU.mult), "rm1")
                        step(eng.tensor_tensor(f("m2"), f("oh2"), f("pos"), ALU.mult), "rm2")
                        step(eng.tensor_reduce(rs["pos1"][:, :], f("m1"), AX.X, ALU.add), "rp1")
                        step(eng.tensor_reduce(rs["pos2"][:, :], f("m2"), AX.X, ALU.add), "rp2")
                        need_dma(eng, "scat", 4 * p)
                        eng.tensor_copy(idx[:, 0, :], rs["pos1"][:, :])
                        done(eng.tensor_copy(idx[:, 1, :], rs["pos2"][:, :]), "ridx")
                    if e == "pool":
                        need(eng, "ridx", n)
                        need(eng, "rtok", n)
                        for b in range(2):
                            need(eng, f"rl{b}", n)
                            settle(eng)
                            for i in range(2):
                                landed(eng.indirect_dma_start(
                                    xrec_d[:, :], bass.IndirectOffsetOnAxis(ap=idx[:, i, b:b + 1], axis=0),
                                    rec[:, b, :], None), "scat")
            return go

        def weights(which, piece):
            def go(e, eng, p):
                n = p + 1
                ex = p if which == 1 else p - NE
                if piece == 1:
                    if e == "sp":
                        need(eng, "wlo", p)
                        src = (w1[bass.ds(ex, 1), :, :].rearrange("o (k q) h -> q (o k) h", q=P) if which == 1
                               else w2[bass.ds(ex, 1), :, :].rearrange("o (k q) h -> q (o k) h", q=P))
                        landed(eng.dma_start(wl[:, :].rearrange("q (k h) -> q k h", k=DC if which == 1 else HC), src), "ldw")
                    if e == "act":
                        need_dma(eng, "ldw", n)
                        if which == 2:
                            need_dma(eng, "stw", ex + 1)
                        done(eng.activation(wst[:, 0, :], wl[:, :], ACT.Square, accum_out=wss[:, :]), "wss")
                    if e == "pe":
                        g = turn(eng, "wsum", "wcl", n)
                        need(eng, "wss", n)
                        done(eng.matmul(g[:, 0:1], ones_f[:, :], wss[:, :], start=True, stop=True), "wsum")
                    if e == "dve":
                        dst = (k1 if which == 1 else k2)
                        need(eng, "wsum", n)
                        done(eng.tensor_scalar(wcl[:, :], given("wsum")[:, 0:1], 2.0 ** -60, None, ALU.max), "wcl")
                        need(eng, "wcl", n)
                        exponent(eng, wcl[:, :], wkk[:, :], "wex", n)
                        eng.tensor_copy(dst[:, bass.ds(ex, 1)], wkk[:, :])
                        done(eng.tensor_scalar(wsc[:, :], wkk[:, :], -float(ONE), 268.0 * ONE, ALU.mult, ALU.add), "wsc")
                hi = (w1s[:, bass.ds(ex, 1), 0, :, :].rearrange("p o k h -> p (o k h)") if which == 1 else wst[:, 0, :])
                lo = (w1s[:, bass.ds(ex, 1), 1, :, :].rearrange("p o k h -> p (o k h)") if which == 1 else wst[:, 1, :])
                if piece == 2:
                    if e == "act":
                        need(eng, "wsc", n)
                        need(eng, "wss", n)
                        done(eng.activation(wl[:, :], wl[:, :], ACT.Identity, scale=wsc[:, :].bitcast(F32)), "wscaled")
                        need(eng, "wscaled", n)
                        done(eng.activation(hi, wl[:, :], ACT.Copy), "whi")
                    if e == "pool":
                        need(eng, "whi", n)
                        if which == 2:
                            need_dma(eng, "stw", ex + 1)
                        done(eng.tensor_tensor(lo, wl[:, :], hi, ALU.subtract), "wlo")
                    if e == "sp" and which == 2:
                        need(eng, "wlo", n)
                        landed(eng.dma_start(w2s_d[bass.ds(ex, 1), :, :].rearrange("o q h -> q (o h)"),
                                             wst[:, :, :].rearrange("q s h -> q (s h)")), "stw")
            return go

        def exponent(eng, src, dst, name, count):
            done(eng.tensor_scalar(dst, src.bitcast(I32), 23, None, ALU.logical_shift_right), name + "a")
            need(eng, name + "a", count)
            done(eng.tensor_scalar(dst, dst, 129.0, None, ALU.add), name + "b")
            need(eng, name + "b", count)
            done(eng.tensor_scalar(dst, dst, 1, None, ALU.logical_shift_right), name)
            need(eng, name, count)

        def setup(e, eng, _):
            if e == "sp":
                for dst, src in ((wq_sb, wq), (wk_sb, wk), (wv_sb, wv), (wo_sb, wo), (wr_sb, wr)):
                    landed(eng.dma_start(dst[:, :, :], src.rearrange("(k q) n -> q k n", q=P)), "set_w")
                landed(eng.dma_start(b1r[:, :], b1.rearrange("e (m q) -> (e m) q", q=P)), "set_w")
            if e == "act":
                for dst, src in (((bqk[:, 0:D], bq), (bqk[:, D:2 * D], bk), (bv_sb[:, :], bv),
                                                (bo_sb[:, :], bo), (al[:, :], alpha))):
                    landed(eng.dma_start(dst, src.partition_broadcast(P)), "set_v")
            if e == "pe":
                need(eng, "set_pool", 2)
                need_dma(eng, "set_w", 6)
                done(eng.transpose(gen[0][:, 0:NE * HC], b1r[:, :], idf[0:NE * HC, 0:NE * HC]), "set_bt")
            if e == "dve":
                eng.memset(ones_f[:, :], 1.0)
                eng.memset(ones_b[:, :], 1.0)
                eng.memset(zrow[:, :], 0.0)
                eng.memset(acc_cnt[:, :], 0.0)
                eng.memset(mhalf[:, :], -0.5)
                eng.memset(ar[:, :, :, :], 0.0)
                eng.memset(padrec[:, :], 0)
                for b in range(2):
                    eng.memset(aq[b][RROWS:RROWS + NSPLIT, :], 1.0)
                    ins = eng.memset(vz[b][:, :, :, :], 0.0)
                done(ins, "set_dve")
                need(eng, "set_dve", 1)
                for b in range(2):
                    for j in range(4):
                        vq = vz[b][:, :, :, :].rearrange("p q j m -> p q (j m)")
                        ins = eng.memset(vq[:, :, j * VM + 4 * DK + j:j * VM + 4 * DK + j + 1], 1.0)
                done(ins, "set_dve")
                need_dma(eng, "set_v", 5)
                done(eng.tensor_reduce(amax[:, :], al[:, :], AX.X, ALU.max, apply_absolute_value=True), "set_a")
                need(eng, "set_a", 1)
                done(eng.tensor_scalar(amax[:, :], amax[:, :], 2.0 ** -60, None, ALU.max), "set_a")
                need(eng, "set_a", 2)
                done(eng.tensor_scalar(abig[:, :], amax[:, :].bitcast(I32), 255 * ONE, None, ALU.bitwise_and), "set_a")
                need(eng, "set_a", 3)
                done(eng.tensor_scalar(abig[:, :], abig[:, :], float(ONE), None, ALU.add), "set_a")
                need(eng, "set_a", 4)
                eng.tensor_scalar(arec[:, :], abig[:, :], -1.0, 254.0 * ONE, ALU.mult, ALU.add)
                done(eng.tensor_scalar(escale[:, :], abig[:, :].bitcast(F32), QK_SCALE ** -2, None, ALU.mult), "set_a")
                need(eng, "set_a", 5)
                eng.memset(signs[:, 0:NH], 1.0)
                eng.memset(signs[:, NH:2 * NH], -1.0)
                eng.memset(colscale[:, NH:2 * NH], -0.5 * QK_SCALE)
                done(eng.tensor_scalar(colscale[:, 0:NH], al[:, :], arec[:, :].bitcast(F32), 0.5 * QK_SCALE,
                                       ALU.mult, ALU.mult), "set_a")
                need(eng, "set_bt", 1)
                done(eng.tensor_copy(b1t[:, :, :].rearrange("p e m -> p (e m)"), gen[0][:, 0:NE * HC]), "set_b1t")
                need(eng, "set_b1t", 1)
                done(eng.tensor_tensor(b1q[:, :, :], b1t[:, :, :], b1t[:, :, :], ALU.mult), "set_b")
                need(eng, "set_b", 1)
                done(eng.tensor_reduce(b1ss[:, :], b1q[:, :, :], AX.X, ALU.add), "set_b")
                need(eng, "set_a", 6)
            if e == "pe":
                need(eng, "set_dve", 2)
                need(eng, "set_b", 2)
                done(eng.matmul(pv_ps[:, 0:NE], ones_f[:, :], b1ss[:, :], start=True, stop=True), "set_bs")
            if e == "dve":
                need(eng, "set_bs", 1)
                done(eng.tensor_scalar(b1ss[:, :], pv_ps[:, 0:NE], 2.0 ** -60, None, ALU.max), "set_b")
                need(eng, "set_b", 3)
                exponent(eng, b1ss[:, :], kb[:, :], "set_kb", 1)
            if e == "pool":
                for m in (idf, idb, id16, lstrict):
                    eng.memset(m[:, :], 0.0)
                for b in range(2):
                    eng.memset(uk[b][:, :], 0.0)
                eng.iota(io8[:, :, :], [[0, 2], [REGION, NE]], base=0, channel_multiplier=0)
                eng.iota(slot_n[:, :, :], [[1, NSLOT], [0, NE]], base=0, channel_multiplier=0)
                done(eng.iota(tok[:, :], [[0, 1]], base=T, channel_multiplier=1), "set_pool")
                need(eng, "set_pool", 1)
                made = 0

                def one(ins):
                    nonlocal made
                    made += 1
                    done(ins, "set_select")
                    need(eng, "set_select", made)
                for m in (idf, idb, id16):
                    one(eng.affine_select(out=m[:, :], in_=m[:, :], compare_op=ALU.not_equal, fill=1.0, base=0,
                                          pattern=[[-1, P]], channel_multiplier=1))
                one(eng.affine_select(out=lstrict[:, :], in_=lstrict[:, :], compare_op=ALU.is_ge, fill=1.0, base=0,
                                      pattern=[[-1, P]], channel_multiplier=1))
                for b in range(2):
                    for i in range(NSPLIT):
                        for par in range(2):
                            w = uk[b][i * STRIP:(i + 1) * STRIP, par * 1024:(par + 1) * 1024]\
                                .rearrange("r (j k) -> r j k", k=P)
                            one(eng.affine_select(out=w, in_=w, compare_op=ALU.not_equal, fill=1.0, base=-par,
                                                  pattern=[[-2, NH // 2], [0, P]], channel_multiplier=1))
                eng.sem_inc(sem("set_pool"), 1)
                need(eng, "set_pool", 2)
                need(eng, "set_dve", 1)
                done(eng.tensor_copy(padrec[:, D + NE:D + NE + 1], tok[:, :]), "set_pool")
                need(eng, "set_pool", 3)
                done(eng.iota(tok[:, :], [[0, 1]], base=0, channel_multiplier=1), "set_pool")
            if e == "dve":
                need(eng, "set_pool", 4)
                done(eng.tensor_copy(ebase[:, :, :], io8[:, :, :]), "set_e")
                for i in range(NE):
                    ins = eng.memset(rank8[:, :, i:i + 1], float(NE - i))
                done(ins, "set_e")
                need(eng, "set_e", 2)
            if e == "sp":
                need(eng, "set_pool", 4)
                for i in range(TWO):
                    spare = NE * REGION + i * P
                    landed(eng.dma_start(xrec_d[spare:spare + P, :], padrec[:, :]), "set_pad")
                need(eng, "set_dve", 1)
                landed(eng.dma_start(out[T:T + P, :], zrow[:, :]), "set_pad")
            if e == "pe":
                need(eng, "set_pool", 2)
                need_dma(eng, "set_w", 6)
                need(eng, "set_b", 3)
            if e == "act":
                need(eng, "set_a", 6)
            if e == "pool":
                need_dma(eng, "set_v", 5)

        stages = {"rows": rows}
        for b_ in range(2):
            stages.update({f"load{b_}": load_stage(b_), f"means{b_}": means_in(b_), f"norm{b_}": norm_in(b_),
                           f"project{b_}": project(b_), f"squares{b_}": squares(b_), f"parts{b_}": parts_of(b_),
                           f"stack{b_}": stack(b_)})
            stages.update({f"back{b_}.{i}": back(b_, i) for i in range(6)})
        for n_ in halves:
            stages.update({f"factors{n_}": factors(n_), f"scores{n_}": scores(n_), f"values{n_}": values(n_)})
            stages.update({f"turned{n_}.{i}": turned(n_, i) for i in range(2)})
        stages.update({f"norms.{i}": norms(i) for i in range(1, 5)})
        stages.update({f"route.{i}": route(i) for i in range(1, 6)})

        order = {
            "pe": """
                factors0 turned3.0- scores0 back0.2- turned3.1- factors1 back0.3- values3- weights.1
                norm0+ scores1 back1.1- project0+ norm1+ factors2 back1.2- turned0.0 project1+
                back1.3- turned0.1 stack1 back0.4- scores2 values0 factors3 scores3 rows+ turned1.0
                back0.5- turned1.1 back1.4- back1.5- values1 turned2.0 turned2.1 stack0+ back0.1
                values2 route.4-""",
            "act": """
                parts1 factors0 turned3.0- back0.2- turned3.1- weights.1 back1.1- norm0+ factors1
                squares0+ norm1+ back1.2- turned0.0 factors2 squares1+ turned0.1 stack1 norms.1+
                norms.2+ weights.2 back0.4- factors3 turned1.0 parts0+ turned1.1 back1.4- route.1-
                turned2.0 back0.1 turned2.1 stack0+""",
            "dve": """
                means0+ scores0 norm0+ back0.3- weights.1 means1+ back1.1- norm1+ project0+ back0.4-
                scores1 project1+ squares0+ back1.3- squares1+ stack1 norms.1+ norms.2+ parts1
                norms.3+ norms.4+ scores2 rows+ parts0+ back0.5- back1.4- scores3 back1.5- route.1-
                route.2- route.3- weights.2 route.4- route.5- stack0+ back0.1""",
            "pool": """
                means0+ scores0 stack1 means1+ back0.3- back0.0 scores1 back1.3- norms.4+ weights.2
                scores2 parts0+ scores3 back1.0 stack0+ parts1+ route.5-""",
            "sp": """
                weights.1 load0+ load1+ back0.3- back0.0 back1.3- back1.0 rows+ weights.2""",
        }
        deltas = {"+": 1, "-": -1}
        steps = {e: [(w.rstrip("+-"), deltas.get(w[-1], 0)) for w in text.split()] for e, text in order.items()}

        def tables(e, eng):
            if e == "dve":
                k = 0

                def step(ins):
                    nonlocal k
                    k += 1
                    done(ins, "table")
                    need(eng, "table", k)
                step(eng.tensor_scalar(tiles_i[:, :], cnt_f[:, :], float(SLOT - 1), None, ALU.add))
                step(eng.tensor_scalar(tiles_i[:, :], tiles_i[:, :], SLOT.bit_length() - 1, None, ALU.logical_shift_right))
                step(eng.tensor_copy(tiles[:, :], tiles_i[:, :]))
                step(eng.memset(unit[:, :], 1.0))
                step(eng.tensor_tensor_scan(ends[:, :], unit[:, :], tiles[:, :], 0.0, ALU.mult, ALU.add))
                step(eng.tensor_copy(slot_f[:, :, :], slot_n[:, :, :]))
                each = lambda t: t[0:1, :].unsqueeze(1).to_broadcast([1, NSLOT, NE])
                step(eng.tensor_tensor(past[:, :, :], slot_f[:, :, :], each(ends), ALU.is_ge))
                step(eng.tensor_tensor(before[:, :, :], past[:, :, :], each(tiles), ALU.mult))
                step(eng.tensor_reduce(n_past[:, :], past[:, :, :], AX.X, ALU.add))
                step(eng.tensor_reduce(start[:, :], before[:, :, :], AX.X, ALU.add))
                step(eng.tensor_tensor(start[:, :], slot_f[:, :, 0], start[:, :], ALU.subtract))
                step(eng.tensor_scalar(start[:, :], start[:, :], float(SLOT), None, ALU.mult))
                step(eng.scalar_tensor_tensor(rowf[:, :], n_past[:, :], float(REGION), start[:, :], ALU.mult, ALU.add))
                step(eng.tensor_scalar(slot_row[:, :], rowf[:, :], float(NE * REGION), None, ALU.min))
                step(eng.tensor_scalar(slot_e[:, :], n_past[:, :], float(NE - 1), None, ALU.min))
                eng.sem_inc(sem("tables"), 1)
                step(eng.tensor_scalar(mk[:, :], k1[:, :], 4.0, None, ALU.add))
                step(eng.tensor_tensor(mk[:, :], mk[:, :], kb[:, :], ALU.max))
                step(eng.tensor_scalar(mk[:, :], mk[:, :], 1.0, None, ALU.add))
                step(eng.tensor_scalar(hsc[:, :], mk[:, :], -float(ONE), 268.0 * ONE, ALU.mult, ALU.add))
                step(eng.tensor_scalar(inv1[:, :], k1[:, :], 25.0, float(ONE), ALU.subtract, ALU.mult))
                step(eng.tensor_tensor(inv2[:, :], mk[:, :], k2[:, :], ALU.add))
                step(eng.tensor_scalar(inv2[:, :], inv2[:, :], 155.0, float(ONE), ALU.subtract, ALU.mult))
                eng.sem_inc(sem("scales"), 1)

        def finish_attention(e, eng, _):
            if e == "pe":
                g = turn(eng, "cnt", "cnt", 1)
                need(eng, "racc", NP)
                done(eng.matmul(g[:, 0:NE], ones_b[:, :], acc_cnt[:, :], start=True, stop=True), "cnt_ps")
            if e == "dve":
                need(eng, "cnt_ps", 1)
                done(eng.tensor_copy(cnt_f[:, :], given("cnt")[:, 0:NE]), "cnt")
                need(eng, "cnt", 1)
                done(eng.tensor_copy(cnt_i[:, :], cnt_f[:, :]), "cnt_i")
            if e == "sp" or e == "act":
                need(eng, "cnt_i", 1)
                for x_ in range(e == "act", NE, 2):
                    row = eng.value_load(cnt_i[0:1, x_:x_ + 1], min_val=0, max_val=T)
                    landed(eng.dma_start(xrec_d[bass.ds(row + x_ * REGION, SLOT), :].rearrange("(i q) w -> q i w", q=P),
                                         padrec[:, :].unsqueeze(1).to_broadcast([P, TWO, REC])), f"pad_{e}")
                need_dma(eng, f"pad_{e}", NE // 2)
            tables(e, eng)
            if e == "pool":
                need_dma(eng, "scat", 4 * NP)
            if e == "sp":
                for b in range(2):
                    need_dma(eng, f"stx{b}", NP)
                need_dma(eng, "stw", NE + 1)
                need_dma(eng, "set_pad", TWO + 1)

        def run(e, eng, k, p, which=1, kept=(-1, 0, 1), freed=(None,) * 3):
            start_section(k, freed)
            for name, d in steps[e]:
                if d in kept:
                    (weights(which, int(name[-1])) if name.startswith("weights") else stages[name])(e, eng, p + d)

        def readers(p):
            seen = []
            for q in range(2, 4):
                run("pe", Rehearsal(), None, q)
                seen.append(Turns.freed)
            return [(name, (n1 - n0) * (p - 2) + n0) for (name, n0), (_, n1) in zip(*seen)]

        def program(e, eng):
            for chain, names in chains.items():
                if e == owner(chain):
                    eng.sem_inc(sem(chain), len(names))
            if e == "sp":
                eng.sem_inc(sem("stw"), 16)
            setup(e, eng, 0)
            run(e, eng, 0, -1, kept=(1,))
            run(e, eng, 1, 0, kept=(0, 1), freed=Turns.freed)
            if e == "pe":
                for reader in Turns.freed:
                    need(eng, *reader)
            run(e, eng, 2, 1)
            with eng.Fori(2, NE) as p:
                run(e, eng, 3, p, freed=readers(p - 1))
            with eng.Fori(0, NP - 1 - NE) as q:
                run(e, eng, 4, q + NE, which=2, freed=readers(q + (NE - 1)))
            run(e, eng, 5, NP - 1, which=2, kept=(-1, 0), freed=readers(NP - 2))
            run(e, eng, 6, NP, kept=(-1,), freed=Turns.freed)
            finish_attention(e, eng, 0)

        with nc.Block() as block:
            @block.tensor
            def _(eng): program("pe", eng)
            @block.scalar
            def _(eng): program("act", eng)
            @block.vector
            def _(eng): program("dve", eng)
            @block.gpsimd
            def _(eng): program("pool", eng)
            @block.sync
            def _(eng): program("sp", eng)

    U = 4
    AHEAD = 3
    HB = 2
    QS = HC // HB
    SLOOP = (NSLOT - AHEAD - 1) // U * U
    with ExitStack() as f:
        w2s = alloc(f, "w2s_sb", [P, NE, 2, HC, D], F16)
        b2s = alloc(f, "b2s", [P, NE, D], F32)
        rb = [alloc(f, f"rb{i}", [P, TWO, REC], I32) for i in range(U)]
        xt = [alloc(f, f"xt{i}", [P, 2, DC, SLOT], F16) for i in range(2)]
        h32 = [alloc(f, f"h32_{i}", [P, HB, SLOT], F32) for i in range(HC // HB)]
        hs = [alloc(f, f"hs{i}", [P, 2, HC, SLOT], F16) for i in range(2)]
        yw = [alloc(f, f"yw{i}", [P, TWO, D], F32) for i in range(2)]
        yb = alloc(f, "yb", [P, TWO, D], F32)
        hbank = [s_ps[:, 0, :], s_ps[:, 1, :], u_ps[:, 0:512], u_ps[:, 512:1024]]
        ybank = [pv_ps, gen[2]]

        def expert_of(eng, s):
            return eng.value_load(slot_e[0:1, bass.ds(s, 1)], min_val=0, max_val=NE - 1)

        def slot(i, j):
            i, j = i + j // U, j % U
            return U * i + j, i, j

        def load_records(e, eng, i, j):
            if e == "sp":
                s, i, j = slot(i, j)
                need_dma(eng, f"add{j}", TWO * i)
                row = eng.value_load(slot_row[0:1, bass.ds(s, 1)], min_val=0, max_val=NE * REGION)
                landed(eng.dma_start(rb[j][:, :, :], xrec_d[bass.ds(row, SLOT), :].rearrange("(i q) w -> q i w", q=P)),
                       f"ldrec{j}")

        def turn_records(e, eng, i, j):
            s, i, j = slot(i, j)
            g = gen[j % 2][:, :].bitcast(F16).rearrange("p (a i t) -> p a i t", i=TWO, t=P)
            if e == "pe":
                need_dma(eng, f"ldrec{j}", i + 1)
                need(eng, "xte", s - 1)
                for a_ in range(2 * DC):
                    for i_ in range(TWO):
                        ins = eng.transpose(g[:, a_, i_, :], rb[j][:, i_, :].bitcast(F16)[:, a_ * P:(a_ + 1) * P],
                                            id16[:, :])
                done(ins, "xtp")
            if e == "dve":
                need(eng, "xtp", s + 1)
                need(eng, "mm1", QS * (s - 1))
                done(eng.tensor_copy(xt[j % 2][:, :, :, :].rearrange("p s k t -> p (s k t)"),
                                     gen[j % 2][:, :].bitcast(F16)), "xte")

        def first_product(e, eng, i, j):
            s, i, j = slot(i, j)
            ex = expert_of(eng, s) if e in ("pe", "act", "dve") else None
            for q in range(QS):
                hb = hbank[q]
                n = QS * s + q + 1
                blocks = range(q * HB, (q + 1) * HB)
                if e == "pe":
                    need(eng, "xte", s + 1)
                    need(eng, "gel", n - QS)
                    for m in blocks:
                        o = (m % HB) * SLOT
                        terms = [(k, wp, xp) for k in range(DC) for wp, xp in ((0, 0), (0, 1), (1, 0))]
                        for t, (k, wp, xp) in enumerate(terms):
                            w = w1s[:, bass.ds(ex, 1), wp, k, m * P:(m + 1) * P].rearrange("p o h -> p (o h)")
                            ins = eng.matmul(hb[:, o:o + SLOT], w, xt[j % 2][:, xp, k, :],
                                             start=(t == 0), stop=(t == len(terms) - 1))
                    done(ins, "mm1")
                if e == "act":
                    need(eng, "mm1", n)
                    need(eng, "lo", n - QS)
                    for m in blocks:
                        o = (m % HB) * SLOT
                        ins = eng.activation(h32[q][:, m % HB, :], hb[:, o:o + SLOT], ACT.Gelu,
                                             scale=inv1[:, bass.ds(ex, 1)].bitcast(F32),
                                             bias=b1t[:, bass.ds(ex, 1), m])
                    done(ins, "gel")
                if e == "dve":
                    need(eng, "gel", n)
                    need(eng, "mm2", s - 1)
                    hi = hs[j % 2][:, 0, blocks[0]:blocks[-1] + 1, :].rearrange("p m t -> p (m t)")
                    lo = hs[j % 2][:, 1, blocks[0]:blocks[-1] + 1, :].rearrange("p m t -> p (m t)")
                    h = h32[q][:, :, :].rearrange("p m t -> p (m t)")
                    scale = hsc[:, bass.ds(ex, 1)].bitcast(F32)
                    done(eng.tensor_scalar(hi, h, scale, None, ALU.mult), "hi")
                    need(eng, "hi", n)
                    done(eng.scalar_tensor_tensor(lo, h, scale, hi, ALU.mult, ALU.subtract), "lo")

        def second_product(e, eng, i, j):
            s, i, j = slot(i, j)
            ex = expert_of(eng, s) if e in ("pe", "dve") else None
            y = ybank[j % 2][:, :].rearrange("p (i d) -> p i d", i=TWO)
            if e == "pe":
                need(eng, "w2_ready", ex + 1)
                need(eng, "yb", s - 1)
                for i_ in range(TWO):
                    for m in range(HC):
                        if m % HB == 0:
                            need(eng, "lo", QS * s + m // HB + 1)
                        for t, (wp, hp) in enumerate(((0, 0), (0, 1), (1, 0))):
                            w = w2s[:, bass.ds(ex, 1), wp, m, :].rearrange("p o d -> p (o d)")
                            ins = eng.matmul(y[:, i_, :], hs[j % 2][:, hp, m, i_ * P:(i_ + 1) * P], w,
                                             start=(m == 0 and t == 0), stop=(m == HC - 1 and t == 2))
                done(ins, "mm2")
            if e == "dve":
                need(eng, "mm2", s + 1)
                need_dma(eng, "ldb2", 1)
                need(eng, "yw", s)
                done(eng.scalar_tensor_tensor(yb[:, :, :], y, inv2[:, bass.ds(ex, 1)].bitcast(F32),
                                              b2s[:, bass.ds(ex, 1), :].to_broadcast([P, TWO, D]),
                                              ALU.mult, ALU.add), "yb")
                need(eng, "yb", s + 1)
                need_dma(eng, f"add{(j - 2) % U}", TWO * (i + (1 if j >= 2 else 0)))
                for i_ in range(TWO):
                    ins = eng.tensor_scalar(yw[j % 2][:, i_, :], yb[:, i_, :],
                                            rb[j][:, i_, D:D + NE].bitcast(F32)[:, bass.ds(ex, 1)], None, ALU.mult)
                done(ins, "yw")
            if e == "pool":
                need(eng, "yw", s + 1)
                need_dma(eng, f"add{(j - 1) % U}", TWO * (i + (1 if j >= 1 else 0)))
                for i_ in range(TWO):
                    need_dma(eng, f"add{j}", TWO * i + i_)
                    settle(eng)
                    landed(eng.indirect_dma_start(
                        out[:, :], bass.IndirectOffsetOnAxis(ap=rb[j][:, i_, D + NE:D + NE + 1], axis=0),
                        yw[j % 2][:, i_, :], None, compute_op=ALU.add), f"add{j}")

        def load_w2(e, eng):
            for i in range(NE):
                if e == "sp":
                    landed(eng.dma_start(w2s[:, i, :, :, :].rearrange("q s k d -> q (s k d)"), w2s_d[i, :, :]),
                           f"ldw2_{i}")
            for i in range(NE):
                if e == "pool":
                    need_dma(eng, f"ldw2_{i}", 1)
                    eng.sem_inc(sem("w2_ready"), 1)

        def slots(e, eng):
            need(eng, "tables", 1)
            need(eng, "scales", 1)
            for j in range(AHEAD):
                load_records(e, eng, 0, j)
            if e == "act":
                landed(eng.dma_start(b2s[:, :, :], b2.partition_broadcast(P)), "ldb2")
            load_w2(e, eng)
            turn_records(e, eng, 0, 0)
            turn_records(e, eng, 0, 1)
            first_product(e, eng, 0, 0)

            def one(i, j, rest):
                if rest >= AHEAD:
                    load_records(e, eng, i, j + AHEAD)
                if rest >= 2:
                    turn_records(e, eng, i, j + 2)
                if rest >= 1:
                    first_product(e, eng, i, j + 1)
                second_product(e, eng, i, j)

            for j in range(U):
                one(0, j, NSLOT)
            with eng.Fori(1, SLOOP // U) as i:
                for j in range(U):
                    one(i, j, NSLOT)
            for s in range(SLOOP, NSLOT):
                one(s // U, s % U, NSLOT - 1 - s)
            if e == "pool":
                for j in range(U):
                    need_dma(eng, f"add{j}", TWO * ((NSLOT - 1 - j) // U + 1))

        with nc.Block() as block:
            @block.tensor
            def _(eng): slots("pe", eng)
            @block.scalar
            def _(eng): slots("act", eng)
            @block.vector
            def _(eng): slots("dve", eng)
            @block.gpsimd
            def _(eng): slots("pool", eng)
            @block.sync
            def _(eng): slots("sp", eng)


INPUTS = ["x", "ctx_1024", "L0_xattn_Wq", "L0_xattn_bq", "L0_xattn_Wk", "L0_xattn_bk", "L0_xattn_Wv", "L0_xattn_bv",
          "L0_xattn_Wo", "L0_xattn_bo", "L0_xattn_alpha", "L0_ffn_Wr", "L0_ffn_W1", "L0_ffn_b1", "L0_ffn_W2",
          "L0_ffn_b2"]


def kernel(**inputs):
    from concourse import bacc
    from concourse.bass_utils import run_bass_kernel_spmd

    nc = bacc.Bacc("TRN2", target_bir_lowering=False, num_devices=1)
    arrays, args = {}, []
    for name in INPUTS:
        a = np.asarray(inputs[name])
        shape = (T, D) if name in ("x", "ctx_1024") else (NH,) if name == "L0_xattn_alpha" else a.shape
        arrays[name] = np.ascontiguousarray(a.reshape(shape))
        args.append(nc.dram_tensor(name, shape, F32, kind="ExternalInput").ap())
    args.append(nc.dram_tensor("out", (T + P, D), F32, kind="ExternalOutput").ap())
    with ExitStack() as ctx:
        build(nc, ctx, args)
    result = run_bass_kernel_spmd(nc, [arrays], core_ids=[0])
    return result.results[0]["out"][:T].reshape(NB, P, D)
```

```python
from contextlib import ExitStack

import numpy as np

import concourse.bass as bass
from concourse import mybir

F32, BF16, F16, I32 = mybir.dt.float32, mybir.dt.bfloat16, mybir.dt.float16, mybir.dt.int32
ALU, ACT, AX = mybir.AluOpType, mybir.ActivationFunctionType, mybir.AxisListType

P = 128
NB, D, NH, DK = 32, 256, 16, 16
NP = NB // 2
T = NB * P
DC = D // P
NE, H = 8, 1024
HC = H // P
EPS = 1e-5
TWO = 2
SLOT = TWO * P
NSLOT = 2 * T // SLOT + NE - 1
REGION = T + SLOT
REC = D + NE + 1
NSPLIT = 3
STRIP = 32
RROWS = NSPLIT * STRIP
QW = 4 * (P // 2 + 4)
VM = P // 2 + 4
X_SCALE = 2.0 ** 11
QK_SCALE = 2.0 ** 12
ONE = 1 << 23
LN2 = float(np.log(2.0))


def build(nc, ctx, io):
    (x, c, wq, bq, wk, bk, wv, bv, wo, bo, alpha, wr, w1, b1, w2, b2, out) = io

    sems = {}

    def sem(name):
        if name not in sems:
            sems[name] = ctx.enter_context(nc.semaphore(name))
        return sems[name]

    chains = {
        "dve_norms": ["mant", "ah", "parts", "coef"],
        "dve_route": ["rd", "rtok", "racc", "rpos", "ridx"],
        "dve_split": ["wcl", "wsc"],
    }
    halves = range(4)
    chains["pe_scores"] = [f"{s}{n}" for n in halves for s in ("u", "su")]
    chains["act_tanh"] = [f"{s}{n}" for n in halves for s in ("th", "t2")]
    chains["dve_max"] = [f"{s}{n}" for n in halves for s in ("tw", "tm")]
    chains["pool_parts"] = ["unit", "lo0", "lo1"]
    chains["pool_less_max"] = [f"sb{n}" for n in halves]
    chains["pe_turn"] = [f"{s}{n}" for n in halves for s in ("ta", "tt")]
    chains["act_exp"] = [f"ex{n}{i}" for n in halves for i in range(2)]
    chains["pe_values"] = [f"pv{n}" for n in halves]
    for b_ in range(2):
        chains[f"pe_first{b_}"] = [f"xct{b_}", f"qk{b_}", f"v{b_}"]
        chains[f"pe_stack{b_}"] = [f"stq{b_}", f"stk{b_}"]
        chains[f"dve_first{b_}"] = [f"ln{b_}ve", f"xn{b_}", f"qke{b_}", f"n2{b_}"]
        chains[f"dve_second{b_}"] = [f"x1{b_}", f"lm{b_}ve", f"y{b_}"]
    owner = lambda chain: chain.split("_")[0]
    place = {name: (chain, i, len(names)) for chain, names in chains.items() for i, name in enumerate(names)}

    def done(ins, name):
        ins.then_inc(sem(place[name][0] if name in place else name), 1)

    def landed(ins, name):
        ins.then_inc(sem(name), 16)

    def need(eng, name, count):
        if isinstance(count, int) and count <= 0 or isinstance(eng, Rehearsal):
            return
        if name in place:
            name, i, m = place[name]
            count = count * m + i + 1
        eng.wait_ge(sem(name), count)
        if eng is nc.sync and not isinstance(count, int):
            settle(eng)

    class Own:
        made = 0

    def clear_own(eng):
        settle(eng)
        eng.sem_clear(sem("own"))
        Own.made = 0

    def own_steps(eng):
        def step(ins):
            Own.made += 1
            done(ins, "own")
            eng.wait_ge(sem("own"), Own.made)
        return step

    def settle(eng):
        eng.sem_inc(sem("settled"), 1)

    def need_dma(eng, name, count):
        if isinstance(count, int) and count <= 0 or isinstance(eng, Rehearsal):
            return
        eng.wait_ge(sem(name), count * 16)
        if eng is nc.sync and not isinstance(count, int):
            settle(eng)

    xrec_d = nc.dram_tensor("xrec", [NE * REGION + SLOT, REC], I32).ap()
    w2s_d = nc.dram_tensor("w2s", [NE, P, 2 * HC * D], F16).ap()

    def alloc(stack, name, shape, dt):
        return stack.enter_context(nc.sbuf_tensor(name, shape, dt))

    def bank(name, shape, dt):
        return ctx.enter_context(nc.psum_tensor(name, shape, dt))

    w1s = alloc(ctx, "w1s", [P, NE, 2, DC, H], F16)
    id16 = alloc(ctx, "id16", [P, P], F16)
    ones_f = alloc(ctx, "ones_f", [P, P], F32)
    k1 = alloc(ctx, "k1", [P, NE], I32)
    k2 = alloc(ctx, "k2", [P, NE], I32)
    kb = alloc(ctx, "kb", [P, NE], I32)
    b1t = alloc(ctx, "b1t", [P, NE, HC], F32)
    acc_cnt = alloc(ctx, "acc_cnt", [P, NE], BF16)
    ebase = alloc(ctx, "ebase", [P, 2, NE], F32)
    cnt_f = alloc(ctx, "cnt_f", [P, NE], F32)
    ones_b = alloc(ctx, "ones_b", [P, P], BF16)

    tiles_i = alloc(ctx, "tiles_i", [P, NE], I32)
    tiles = alloc(ctx, "tiles", [P, NE], F32)
    ends = alloc(ctx, "ends", [P, NE], F32)
    unit = alloc(ctx, "unit_row", [P, NE], F32)
    slot_n = alloc(ctx, "slot_n", [1, NSLOT, NE], I32)
    slot_f = alloc(ctx, "slot_f", [1, NSLOT, NE], F32)
    past = alloc(ctx, "past", [1, NSLOT, NE], F32)
    before = alloc(ctx, "before", [1, NSLOT, NE], F32)
    n_past = alloc(ctx, "n_past", [1, NSLOT], F32)
    start = alloc(ctx, "start", [1, NSLOT], F32)
    rowf = alloc(ctx, "rowf", [1, NSLOT], F32)
    slot_e = alloc(ctx, "slot_e", [1, NSLOT], I32)
    slot_row = alloc(ctx, "slot_row", [1, NSLOT], I32)
    mk = alloc(ctx, "mk", [P, NE], I32)
    hsc = alloc(ctx, "hsc", [P, NE], I32)
    inv1 = alloc(ctx, "inv1", [P, NE], I32)
    inv2 = alloc(ctx, "inv2", [P, NE], I32)
    cnt_i = alloc(ctx, "cnt_i", [P, NE], I32)

    s_ps = bank("s_ps", [P, 2, 512], F32)
    u_ps = bank("u_ps", [P, 1024], F32)
    pv_ps = bank("pv_ps", [P, 512], F32)
    gen = [bank(f"gen{i}", [P, 512], F32) for i in range(3)]

    class Turns:
        section, n, freed, given = 0, 0, [None] * 3, {}

    class Rehearsal:
        def __getattr__(self, _):
            return lambda *args, **kw: self

    def start_section(k, freed=(None,) * 3):
        Turns.section, Turns.n, Turns.freed = k, 0, list(freed)

    def turn(pe, what, name, count):
        i = Turns.n % 3
        Turns.n += 1
        if Turns.freed[i]:
            need(pe, *Turns.freed[i])
        Turns.freed[i] = (name, count)
        Turns.given[Turns.section, what] = gen[i]
        return gen[i]

    def given(what):
        return Turns.given[Turns.section, what]

    with ExitStack() as a:
        wq_sb = alloc(a, "wq_sb", [P, DC, D], F32)
        wk_sb = alloc(a, "wk_sb", [P, DC, D], F32)
        wv_sb = alloc(a, "wv_sb", [P, DC, D], F32)
        wo_sb = alloc(a, "wo_sb", [P, DC, D], F32)
        wr_sb = alloc(a, "wr_sb", [P, DC, NE], F32)
        bqk = alloc(a, "bqk", [P, 2 * D], F32)
        bv_sb = alloc(a, "bv_sb", [P, D], F32)
        bv_wide = alloc(a, "bv_wide", [P, DC, P], F32)
        bo_sb = alloc(a, "bo_sb", [P, D], F32)
        al = alloc(a, "al", [P, NH], F32)
        amax = alloc(a, "amax", [P, 1], F32)
        abig = alloc(a, "abig", [P, 1], I32)
        arec = alloc(a, "arec", [P, 1], I32)
        escale = alloc(a, "escale", [P, 1], F32)
        colscale = alloc(a, "colscale", [P, 2 * NH], F32)
        signs = alloc(a, "signs", [P, 2 * NH], F32)
        idf = alloc(a, "idf", [P, P], F32)
        idb = alloc(a, "idb", [P, P], BF16)
        lstrict = alloc(a, "lstrict", [P, P], BF16)
        rank8 = alloc(a, "rank8", [P, 2, NE], F32)
        padrec = alloc(a, "padrec", [P, REC], I32)
        zrow = alloc(a, "zrow", [P, D], F32)
        mhalf = alloc(a, "mhalf", [P, 1], F32)
        io8 = alloc(a, "io8", [P, 2, NE], I32)
        tok = alloc(a, "tok", [P, 1], I32)
        wl = alloc(a, "wl", [P, 2048], F32)
        wst = alloc(a, "wst", [P, 2, 2048], F16)
        wss = alloc(a, "wss", [P, 1], F32)
        wkk = alloc(a, "wkk", [P, 1], I32)
        wsc = alloc(a, "wsc", [P, 1], I32)
        wcl = alloc(a, "wcl", [P, 1], F32)
        pair = lambda name, shape, dt: [alloc(a, f"{name}{b}", shape, dt) for b in range(2)]
        xin, cin, xn = pair("xin", [P, D], F32), pair("cin", [P, D], F32), pair("xn", [P, D], F32)
        xct = pair("xct", [P, 2 * DC, P], F32)
        norm_bufs = {name: [[alloc(a, f"{name}{b}_{k}", [P, w], F32)
                             for k, w in (("st6", 6), ("mv", 2), ("var", 1), ("rstd", 1))]
                            for b in range(2)] for name in ("ln", "lm")}
        qk = alloc(a, "qk", [P, 2, 2 * NH, DK], F32)
        qks = alloc(a, "qks", [P, 2, 2 * NH, DK], F32)
        vn = pair("vn", [P, D], F32)
        n2 = alloc(a, "n2", [P, 2, 2 * NH], F32)
        na = {k: alloc(a, f"na_{k}", [P, 2, 2 * NH], I32 if k in ("mant", "ex") else F32)
              for k in ("mant", "ex", "exf", "ln", "ah", "y", "y2", "n2y2", "rn", "coef", "r1", "r2")}
        ar = alloc(a, "ar", [P, 2, 2, RROWS], BF16)
        qks16 = pair("qks16", [P, 2 * NH, 4, DK], F16)
        qt, kt = pair("qt", [P, NH // 2, P], F16), pair("kt", [P, NH // 2, P], F16)
        aq = pair("aq", [RROWS + NSPLIT, P], BF16)
        kbr = pair("kbr", [RROWS, P], BF16)
        uk = pair("uk", [RROWS + NSPLIT, NH * P], BF16)
        vz = pair("vz", [P, 4, 4, VM + 16], F32)
        th, tw = pair("th", [P, 1024], F32), pair("tw", [P, 2, 4, P], F32)
        tm = pair("tm", [P, 8], F32)
        pt = pair("pt", [P, 2, 512], F32)
        osb = alloc(a, "osb", [VM, 512], F32)
        rz = alloc(a, "rz", [P, 4, 4], F32)
        on = alloc(a, "on", [P, D], F32)
        ot = alloc(a, "ot", [P, DC, P], F32)
        xres, xb = pair("xres", [P, D], F32), pair("xb", [P, D], F32)
        x1 = pair("x1", [P, D], F32)
        xn2 = pair("xn2", [P, D], F32)
        xn2t = alloc(a, "xn2t", [P, DC, P], F32)
        rec = alloc(a, "rec", [P, 2, REC], I32)
        r = {k: alloc(a, f"r_{k}", [P, 2, NE], F32)
             for k in ("l", "q", "eq", "v", "oh1", "oh2", "w1", "w2", "pos", "m1", "m2")}
        rs = {k: alloc(a, f"rs_{k}", [P, 2], F32)
              for k in ("l1", "l2", "d", "e", "vm", "sm", "v1", "v2", "pos1", "pos2")}
        hot = alloc(a, "hot", [P, 2, NE], BF16)
        acc2 = alloc(a, "acc2", [P, 2, NE], BF16)
        idx = alloc(a, "idx", [P, 2, 2], I32)
        b1r = alloc(a, "b1r", [NE * HC, P], F32)
        b1q = alloc(a, "b1q", [P, NE, HC], F32)
        b1ss = alloc(a, "b1ss", [P, NE], F32)

        def load_stage(b):
            def go(e, eng, p):
                if e != "sp":
                    return
                row = (2 * p + b) * P
                need(eng, f"xn{b}", p)
                landed(eng.dma_start(xin[b][:, :], x[bass.ds(row, P), :]), f"ldx{b}")
                need(eng, f"xct{b}", p)
                landed(eng.dma_start(cin[b][:, :], c[bass.ds(row, P), :]), f"ldc{b}")
            return go

        def statistics(e, eng, src, b, name, count):
            st6, mv, var, rstd = norm_bufs[name][b]
            name = f"{name}{b}"
            if e == "dve":
                step = own_steps(eng)
                step(eng.bn_stats(st6[:, :], src))
                step(eng.bn_aggr(mv[:, :], st6[:, :]))
                done(eng.tensor_scalar(var[:, :], mv[:, 1:2], EPS, None, ALU.add), name + "ve")
            if e == "pool":
                need(eng, name + "ve", count)
                done(eng.tensor_tensor(rstd[:, :], var[:, :], mhalf[:, :], ALU.pow), name + "rs")

        def normalised(eng, src, b, name, count, dst, scale=1.0):
            _, mv, _, rstd = norm_bufs[name][b]
            name = f"{name}{b}"
            need(eng, name + "rs", count)
            if scale != 1.0:
                own_steps(eng)(eng.tensor_scalar(rstd[:, :], rstd[:, :], scale, None, ALU.mult))
            return eng.tensor_scalar(dst, src, mv[:, 0:1], rstd[:, :], ALU.subtract, ALU.mult)

        def means_in(b):
            def go(e, eng, p):
                if e == "dve":
                    need_dma(eng, f"ldx{b}", p + 1)
                    need(eng, f"xn{b}", p)
                statistics(e, eng, xin[b][:, :], b, "ln", p + 1)
            return go

        def norm_in(b):
            def go(e, eng, p):
                if e == "dve":
                    need(eng, f"xct{b}", p)
                    done(normalised(eng, xin[b][:, :], b, "ln", p + 1, xn[b][:, :]), f"xn{b}")
                if e == "pe":
                    g = turn(eng, f"xct{b}", f"xce{b}", p + 1)
                    need(eng, f"xn{b}", p + 1)
                    need_dma(eng, f"ldc{b}", p + 1)
                    for i, src in enumerate((xn[b], cin[b])):
                        for k in range(DC):
                            o = (DC * i + k) * P
                            ins = eng.transpose(g[:, o:o + P], src[:, k * P:(k + 1) * P], idf[:, :])
                    done(ins, f"xct{b}")
                if e == "act":
                    need(eng, f"xct{b}", p + 1)
                    need(eng, f"v{b}", p)
                    done(eng.activation(xct[b][:, :, :], given(f"xct{b}")[:, :].rearrange("p (a t) -> p a t", t=P),
                                        ACT.Copy), f"xce{b}")
            return go

        def project(b):
            def go(e, eng, p):
                if e == "pe":
                    need(eng, f"xce{b}", p + 1)
                    g = turn(eng, f"qk{b}", f"qke{b}", p + 1)
                    for i, w in ((0, wq_sb), (1, wk_sb)):
                        for k in range(DC):
                            ins = eng.matmul(g[:, i * D:(i + 1) * D], xct[b][:, DC * i + k, :], w[:, k, :],
                                             start=(k == 0), stop=(k == DC - 1))
                    done(ins, f"qk{b}")
                    g = turn(eng, f"v{b}", f"ve{b}", p + 1)
                    for k in range(DC):
                        ins = eng.matmul(g[:, 0:D], xct[b][:, DC + k, :], wv_sb[:, k, :],
                                         start=(k == 0), stop=(k == DC - 1))
                    done(ins, f"v{b}")
                if e == "dve":
                    need(eng, f"qk{b}", p + 1)
                    need(eng, "unit", p)
                    done(eng.tensor_tensor(qk[:, b, :, :].rearrange("p h d -> p (h d)"),
                                           given(f"qk{b}")[:, :], bqk[:, :], ALU.add), f"qke{b}")
                if e == "act":
                    need(eng, f"v{b}", p + 1)
                    need(eng, f"vz{b}", p)
                    done(eng.activation(vn[b][:, :], given(f"v{b}")[:, 0:D], ACT.Copy), f"ve{b}")
            return go

        def squares(b):
            def go(e, eng, p):
                if e == "act":
                    need(eng, f"qke{b}", p + 1)
                    need(eng, "lo1", p)
                    done(eng.activation(qks[:, b, :, :], qk[:, b, :, :], ACT.Square), f"sq{b}")
                if e == "dve":
                    need(eng, f"sq{b}", p + 1)
                    need(eng, "coef", p)
                    done(eng.tensor_reduce(n2[:, b, :], qks[:, b, :, :], AX.X, ALU.add), f"n2{b}")
            return go

        def norms(piece):
            def go(e, eng, p):
                n = p + 1
                step = own_steps(eng) if e == "dve" else None
                if piece == 1:
                    if e == "dve":
                        need(eng, "n20", n)
                        need(eng, "n21", n)
                        need(eng, "nln", p)
                        done(eng.tensor_scalar(na["mant"][:, :, :], n2[:, :, :].bitcast(I32), ONE - 1, 127 * ONE,
                                               ALU.bitwise_and, ALU.bitwise_or), "mant")
                        step(eng.tensor_scalar(na["ex"][:, :, :], n2[:, :, :].bitcast(I32), 23, None,
                                               ALU.logical_shift_right))
                        step(eng.tensor_scalar(na["exf"][:, :, :], na["ex"][:, :, :], -127.0, 0.5 * LN2,
                                               ALU.add, ALU.mult))
                    if e == "act":
                        need(eng, "mant", n)
                        done(eng.activation(na["ln"][:, :, :], na["mant"][:, :, :].bitcast(F32), ACT.Ln), "nln")
                if piece == 2:
                    if e == "dve":
                        need(eng, "nln", n)
                        need(eng, "ny", p)
                        done(eng.scalar_tensor_tensor(na["ah"][:, :, :], na["ln"][:, :, :], 0.5, na["exf"][:, :, :],
                                                      ALU.mult, ALU.add), "ah")
                    if e == "act":
                        need(eng, "ah", n)
                        done(eng.activation(na["y"][:, :, :], na["ah"][:, :, :], ACT.Exp, scale=-1.0), "ny")
                if piece == 3:
                    if e == "dve":
                        sgn = na["r1"]
                        need(eng, "ah", n)
                        need(eng, "rows_t", p)
                        step(eng.tensor_tensor(sgn[:, :, :], na["ah"][:, :, :],
                                               signs[:, :].unsqueeze(1).to_broadcast([P, 2, 2 * NH]), ALU.mult))
                        part = lambda i: ar[:, :, :, i * STRIP:i * STRIP + NH]
                        v4 = lambda t: t[:, :, :].rearrange("p b (i h) -> p b i h", h=NH)
                        step(eng.tensor_copy(part(0), v4(sgn)))
                        step(eng.tensor_tensor(v4(na["r2"]), v4(sgn), part(0), ALU.subtract))
                        step(eng.tensor_copy(part(1), v4(na["r2"])))
                        step(eng.tensor_tensor(v4(sgn), v4(na["r2"]), part(1), ALU.subtract))
                        done(eng.tensor_copy(part(2), v4(sgn)), "parts")
                if piece == 4:
                    if e == "dve":
                        need(eng, "ny", n)
                        step(eng.tensor_tensor(na["y2"][:, :, :], na["y"][:, :, :], na["y"][:, :, :], ALU.mult))
                        step(eng.tensor_tensor(na["n2y2"][:, :, :], na["y2"][:, :, :], n2[:, :, :], ALU.mult))
                        step(eng.scalar_tensor_tensor(na["rn"][:, :, :], na["n2y2"][:, :, :], -3.0, na["y"][:, :, :],
                                                      ALU.add, ALU.mult))
                        need(eng, "unit", p)
                        done(eng.tensor_tensor(na["coef"][:, :, :], na["rn"][:, :, :],
                                               colscale[:, :].unsqueeze(1).to_broadcast([P, 2, 2 * NH]), ALU.mult),
                             "coef")
                    if e == "pool":
                        need(eng, "coef", n)
                        for b in range(2):
                            ins = eng.tensor_tensor(qks[:, b, :, :], qk[:, b, :, :],
                                                    na["coef"][:, b, :].unsqueeze(2).to_broadcast([P, 2 * NH, DK]),
                                                    ALU.mult)
                        done(ins, "unit")
            return go

        def parts_of(b):
            def go(e, eng, p):
                n = p + 1
                part = lambda i, s0, ds: qks16[b][:, NH * i:NH * (i + 1), s0:s0 + ds + 1:ds, :]
                both = lambda t, i: t[:, NH * i:NH * (i + 1), :].unsqueeze(2).to_broadcast([P, NH, 2, DK])
                if e == "act":
                    need(eng, "unit", n)
                    need(eng, f"stk{b}", p)
                    eng.activation(part(0, 0, 1), both(qks[:, b, :, :], 0), ACT.Copy)
                    done(eng.activation(part(1, 0, 2), both(qks[:, b, :, :], 1), ACT.Copy), f"hi{b}")
                if e == "pool":
                    need(eng, f"hi{b}", n)
                    need(eng, "unit", n)
                    for i, s0, ds in ((0, 2, 1), (1, 1, 2)):
                        ins = eng.tensor_tensor(part(i, s0, ds), both(qks[:, b, :, :], i),
                                                both(qks16[b][:, :, 0, :], i), ALU.subtract)
                    done(ins, f"lo{b}")
            return go

        def rows(e, eng, p):
            n = p + 1
            if e == "pe":
                need(eng, "parts", n)
                g = turn(eng, "rows_t", "rowk1", n)
                gb = g[:, :].bitcast(BF16)
                for b in range(2):
                    for i in range(2):
                        o = (2 * b + i) * P
                        ins = eng.transpose(gb[0:RROWS, o:o + P], ar[:, b, i, :], idb[:, :])
                done(ins, "rows_t")
            if e == "dve":
                gb = given("rows_t")[:, :].bitcast(BF16)
                need(eng, "rows_t", n)
                for b in range(2):
                    need(eng, f"su{2 * b + 1}", p)
                    done(eng.tensor_copy(aq[b][0:RROWS, :], gb[0:RROWS, 2 * b * P:(2 * b + 1) * P]), f"rowq{b}")
                    need_dma(eng, f"flat{b}", 2 * NSPLIT * p)
                    done(eng.tensor_copy(kbr[b][:, :], gb[0:RROWS, (2 * b + 1) * P:(2 * b + 2) * P]), f"rowk{b}")
            if e == "sp":
                for b in range(2):
                    need(eng, f"rowk{b}", n)
                    need(eng, f"su{2 * b + 1}", p)
                    for s in range(NSPLIT):
                        for par in range(2):
                            dst = uk[b][RROWS + s:RROWS + s + 1, par * 1024:(par + 1) * 1024]
                            src = kbr[b][s * STRIP + par:s * STRIP + NH:2, :]
                            landed(eng.dma_start(dst.rearrange("o (j k) -> o j k", k=P), src), f"flat{b}")

        def stack(b):
            def go(e, eng, p):
                n = p + 1
                if e == "pe":
                    need(eng, f"lo{b}", n)
                    for i, to in ((0, "qte"), (1, "kte")):
                        g = turn(eng, f"{to}{b}", f"{to}{b}", n)
                        gh = g[:, :].bitcast(F16)
                        for j in range(NH // 2):
                            h = NH * i + 2 * j
                            src = qks16[b][:, h:h + 2, :, :].rearrange("p h s d -> p (h s d)")
                            ins = eng.transpose(gh[:, j * P:(j + 1) * P], src, id16[:, :])
                        done(ins, f"stk{b}" if i else f"stq{b}")
                if e == "act":
                    for to, stacked, name in ((qt, f"stq{b}", f"qte{b}"), (kt, f"stk{b}", f"kte{b}")):
                        need(eng, stacked, n)
                        need(eng, f"su{2 * b + 1}", p)
                        done(eng.activation(to[b][:, :, :], given(name)[:, :].bitcast(F16)
                                            .rearrange("p (j t) -> p j t", t=P), ACT.Copy), name)
                if e == "pool":
                    need(eng, f"ve{b}", n)
                    need(eng, f"pv{2 * b + 1}", p)
                    settle(eng)
                    for h in range(2):
                        ins = eng.tensor_copy(
                            vz[b][:, 2 * h:2 * h + 2, :, 0:DK],
                            vn[b][:, h * P:(h + 1) * P].rearrange("p (j a d) -> p a j d", a=2, d=DK))
                    done(ins, f"vz{b}")
            return go

        def factors(n_):
            b, h = divmod(n_, 2)
            def go(e, eng, p):
                n = p + 1
                prev = (n_ - 1) % 4
                pc = n if n_ else p
                if e == "pe":
                    need(eng, f"rowq{b}", n)
                    need_dma(eng, f"flat{b}", 2 * NSPLIT * n)
                    need(eng, f"th{prev}", pc)
                    for i in range(2):
                        o = i * 1024 + h * 512
                        ins = eng.matmul(u_ps[:, i * 512:(i + 1) * 512], aq[b][:, :], uk[b][:, o:o + 512],
                                         start=True, stop=True)
                    done(ins, f"u{n_}")
                if e == "act":
                    need(eng, f"u{n_}", n)
                    need(eng, f"tw{n_ ^ 2}", n if n_ >= 2 else p)
                    done(eng.activation(th[h][:, :], u_ps[:, :], ACT.Tanh, scale=0.5), f"th{n_}")
                    need(eng, f"th{n_}", n)
                    done(eng.activation(th[h][:, :], th[h][:, :], ACT.Square), f"t2{n_}")
            return go

        def scores(n_):
            b, h = divmod(n_, 2)
            def go(e, eng, p):
                n = p + 1
                prev = (n_ - 1) % 4
                pc = n if n_ else p
                if e == "pe":
                    need(eng, f"qte{b}", n)
                    need(eng, f"kte{b}", n)
                    need(eng, f"tw{prev}", pc)
                    for j in range(4):
                        for i in range(2):
                            rws = slice(64 * i, 64 * i + 64)
                            ins = eng.matmul(s_ps[:, i, j * P:(j + 1) * P], qt[b][rws, 4 * h + j, :],
                                             kt[b][rws, 4 * h + j, :], start=True, stop=True)
                    done(ins, f"su{n_}")
                if e == "dve":
                    need(eng, f"t2{n_}", n)
                    need(eng, f"su{n_}", n)
                    need(eng, f"tt{n_ ^ 2}", n if n_ >= 2 else p)
                    twf = tw[h][:, :, :, :].rearrange("p i j k -> p (i j k)")
                    done(eng.scalar_tensor_tensor(twf, th[h][:, :], -1.0,
                                                  s_ps[:, :, :].rearrange("p i k -> p (i k)"),
                                                  ALU.add, ALU.mult), f"tw{n_}")
                    need(eng, f"tw{n_}", n)
                    need(eng, f"sb{n_ ^ 2}", n if n_ >= 2 else p)
                    done(eng.tensor_reduce(tm[h][:, :], tw[h][:, :, :, :].rearrange("p i j k -> p (i j) k"),
                                           AX.X, ALU.max), f"tm{n_}")
                if e == "pool":
                    need(eng, f"tm{n_}", n)
                    v = tw[h][:, :, :, :].rearrange("p i j k -> p (i j) k")
                    done(eng.tensor_tensor(v, v, tm[h][:, :].unsqueeze(2).to_broadcast([P, 8, P]),
                                           ALU.subtract), f"sb{n_}")
            return go

        def turned(n_, i):
            b, h = divmod(n_, 2)
            def go(e, eng, p):
                n = p + 1
                if e == "pe":
                    if i == 0:
                        need(eng, f"sb{n_}", n)
                    g = turn(eng, f"ex{n_}{i}", f"ex{n_}{i}", n)
                    for j in range(4):
                        ins = eng.transpose(g[:, j * P:(j + 1) * P], tw[h][:, i, j, :], idf[:, :])
                    done(ins, f"tt{n_}" if i else f"ta{n_}")
                if e == "act":
                    need(eng, f"tt{n_}" if i else f"ta{n_}", n)
                    need(eng, f"pv{n_ ^ 2}", n if n_ >= 2 else p)
                    done(eng.activation(pt[h][:, i, :], given(f"ex{n_}{i}")[:, :], ACT.Exp,
                                        scale=escale[:, :]), f"ex{n_}{i}")
            return go

        def values(n_):
            b, h = divmod(n_, 2)
            def go(e, eng, p):
                n = p + 1
                if e == "pe":
                    need(eng, f"vz{b}", n)
                    if h == 0:
                        need(eng, "osb", 2 * p + b)
                    for i in range(2):
                        need(eng, f"ex{n_}{i}", n)
                        q = 2 * h + i
                        for j in range(4):
                            vq = vz[b][:, q, :, :].rearrange("p j m -> p (j m)")
                            ins = eng.matmul(pv_ps[0:VM, q * P:(q + 1) * P], vq[:, j * VM:(j + 1) * VM],
                                             pt[h][:, i, j * P:(j + 1) * P], start=(j == 0), stop=(j == 3))
                    done(ins, f"pv{n_}")
            return go

        def back(b, part):
            def go(e, eng, p):
                n, m = p + 1, 2 * p + b + 1
                if part == 0:
                    if e == "sp":
                        need(eng, f"xb{b}", p)
                        landed(eng.dma_start(xres[b][:, :], x[bass.ds((2 * p + b) * P, P), :]), f"ldr{b}")
                    if e == "pool":
                        need_dma(eng, f"ldr{b}", n)
                        need(eng, f"x1{b}", p)
                        done(eng.tensor_tensor(xb[b][:, :], xres[b][:, :], bo_sb[:, :], ALU.add), f"xb{b}")
                if part == 1:
                    if e == "act":
                        need(eng, f"pv{2 * b + 1}", n)
                        need(eng, "ob", m - 1)
                        done(eng.activation(osb[:, :], pv_ps[0:VM, :], ACT.Copy), "osb")
                    if e == "pe":
                        g = turn(eng, f"ob{b}", "on", m)
                        need(eng, "osb", m)
                        for q in range(4):
                            ins = eng.transpose(g[:, q * P:q * P + VM], osb[:, q * P:(q + 1) * P],
                                                idf[0:VM, 0:VM])
                        done(ins, "ob")
                    if e == "dve":
                        g = given(f"ob{b}")[:, :].rearrange("p (q c) -> p q c", q=4)
                        need(eng, "ob", m)
                        done(eng.reciprocal(rz[:, :, :], g[:, :, 4 * DK:4 * DK + 4]), "rz")
                        need(eng, "rz", m)
                        need(eng, "oc", m - 1)
                        for h in range(2):
                            ins = eng.tensor_tensor(
                                on[:, h * P:(h + 1) * P].rearrange("p (j a d) -> p a j d", a=2, d=DK),
                                g[:, 2 * h:2 * h + 2, 0:4 * DK].rearrange("p a (j d) -> p a j d", d=DK),
                                rz[:, 2 * h:2 * h + 2, :].unsqueeze(3).to_broadcast([P, 2, 4, DK]), ALU.mult)
                        done(ins, "on")
                if part == 2:
                    if e == "pe":
                        g = turn(eng, f"oc{b}", "ote", m)
                        need(eng, "on", m)
                        for k in range(DC):
                            ins = eng.transpose(g[:, k * P:(k + 1) * P], on[:, k * P:(k + 1) * P], idf[:, :])
                        done(ins, "oc")
                    if e == "act":
                        need(eng, "oc", m)
                        need(eng, "wo", m - 1)
                        done(eng.activation(ot[:, :, :], given(f"oc{b}")[:, 0:D]
                                            .rearrange("p (k t) -> p k t", t=P), ACT.Copy), "ote")
                if part == 3:
                    if e == "pe":
                        g = turn(eng, f"wo{b}", f"x1{b}", n)
                        need(eng, "ote", m)
                        for k in range(DC):
                            ins = eng.matmul(g[:, 0:D], ot[:, k, :], wo_sb[:, k, :], start=(k == 0),
                                             stop=(k == DC - 1))
                        done(ins, "wo")
                    if e == "dve":
                        need(eng, "wo", m)
                        need(eng, f"xb{b}", n)
                        need_dma(eng, f"stx{b}", p)
                        done(eng.tensor_tensor(x1[b][:, :], given(f"wo{b}")[:, 0:D], xb[b][:, :], ALU.add), f"x1{b}")
                        need(eng, f"x1{b}", n)
                    statistics(e, eng, x1[b][:, :], b, "lm", n)
                    if e == "sp":
                        need(eng, f"x1{b}", n)
                        landed(eng.dma_start(out[bass.ds((2 * p + b) * P, P), :], x1[b][:, :]), f"stx{b}")
                if part == 4:
                    if e == "dve":
                        need(eng, f"xu{b}", p)
                        need(eng, f"rl{b}", p)
                        done(normalised(eng, x1[b][:, :], b, "lm", n, xn2[b][:, :], X_SCALE), f"y{b}")
                    if e == "act":
                        need_dma(eng, "scat", 4 * p)
                        need(eng, f"y{b}", n)
                        done(eng.activation(rec[:, b, :].bitcast(F16)[:, 0:D], xn2[b][:, :], ACT.Copy), f"rh{b}")
                    if e == "pool":
                        need(eng, f"rh{b}", n)
                        done(eng.tensor_tensor(rec[:, b, :].bitcast(F16)[:, D:2 * D], xn2[b][:, :],
                                               rec[:, b, :].bitcast(F16)[:, 0:D], ALU.subtract), f"rl{b}")
                    if e == "pe":
                        g = turn(eng, f"xu{b}", "xue", m)
                        need(eng, f"y{b}", n)
                        for k in range(DC):
                            ins = eng.transpose(g[:, k * P:(k + 1) * P], xn2[b][:, k * P:(k + 1) * P], idf[:, :])
                        done(ins, f"xu{b}")
                    if e == "act":
                        need(eng, f"xu{b}", n)
                        need(eng, "lg", m - 1)
                        done(eng.activation(xn2t[:, :, :], given(f"xu{b}")[:, 0:D]
                                            .rearrange("p (k t) -> p k t", t=P), ACT.Copy), "xue")
                if part == 5:
                    if e == "pe":
                        g = turn(eng, f"lg{b}", f"rl_{b}", n)
                        need(eng, "xue", m)
                        for k in range(DC):
                            ins = eng.matmul(g[:, 0:NE], xn2t[:, k, :], wr_sb[:, k, :], start=(k == 0),
                                             stop=(k == DC - 1))
                        done(ins, "lg")
                    if e == "dve":
                        need(eng, "lg", m)
                        need(eng, "racc", p)
                        done(eng.tensor_scalar(r["l"][:, b, :], given(f"lg{b}")[:, 0:NE], 1.0 / X_SCALE, None,
                                               ALU.mult), f"rl_{b}")
            return go

        def route(piece):
            def go(e, eng, p):
                n = p + 1
                wide = lambda t: rs[t][:, :].unsqueeze(2).to_broadcast([P, 2, NE])
                f = lambda t: r[t][:, :, :]
                step = own_steps(eng) if e == "dve" else None

                def best(src, i):
                    top, oh = f"l{i}", f"oh{i}"
                    step(eng.tensor_reduce(rs[top][:, :], f(src), AX.X, ALU.max))
                    step(eng.tensor_tensor(f("eq"), f(src), wide(top), ALU.is_equal))
                    step(eng.tensor_tensor(f("v"), f("eq"), rank8[:, :, :], ALU.mult))
                    step(eng.tensor_reduce(rs["vm"][:, :], f("v"), AX.X, ALU.max))
                    step(eng.tensor_tensor(f(oh), f("v"), wide("vm"), ALU.is_equal))

                if piece == 1:
                    if e == "dve":
                        need(eng, "rl_0", n)
                        need(eng, "rl_1", n)
                        best("l", 1)
                        step(eng.scalar_tensor_tensor(f("q"), f("oh1"), -2.0 ** 100, f("l"), ALU.mult, ALU.add))
                if piece == 2:
                    if e == "dve":
                        best("q", 2)
                        done(eng.tensor_tensor(rs["d"][:, :], rs["l2"][:, :], rs["l1"][:, :], ALU.subtract), "rd")
                    if e == "act":
                        need(eng, "rd", n)
                        done(eng.activation(rs["e"][:, :], rs["d"][:, :], ACT.Exp), "re")
                if piece == 3:
                    if e == "dve":
                        need(eng, "re", n)
                        step(eng.tensor_scalar(rs["sm"][:, :], rs["e"][:, :], 1.0, None, ALU.add))
                        step(eng.reciprocal(rs["v1"][:, :], rs["sm"][:, :]))
                        step(eng.tensor_tensor(rs["v2"][:, :], rs["e"][:, :], rs["v1"][:, :], ALU.mult))
                        step(eng.tensor_tensor(f("w1"), f("oh1"), wide("v1"), ALU.mult))
                        step(eng.tensor_tensor(f("w2"), f("oh2"), wide("v2"), ALU.mult))
                if piece == 4:
                    if e == "dve":
                        recf = rec[:, :, :].bitcast(F32)
                        eng.tensor_tensor(recf[:, :, D:D + NE], f("w1"), f("w2"), ALU.add)
                        reci = rec[:, :, :]
                        for b in range(2):
                            ins = eng.tensor_scalar(reci[:, b, D + NE:D + NE + 1], tok[:, :], float(b * P), None,
                                                    ALU.add)
                        done(ins, "rtok")
                        need(eng, "rtok", n)
                        step(eng.tensor_scalar(tok[:, :], tok[:, :], float(2 * P), None, ALU.add))
                        need(eng, "rank", p)
                        step(eng.tensor_tensor(hot[:, :, :], f("oh1"), f("oh2"), ALU.add))
                        step(eng.tensor_copy(acc2[:, 0, :], acc_cnt[:, :]))
                        step(eng.tensor_tensor(acc2[:, 1, :], acc_cnt[:, :], hot[:, 0, :], ALU.add))
                        done(eng.tensor_tensor(acc_cnt[:, :], acc2[:, 1, :], hot[:, 1, :], ALU.add), "racc")
                    if e == "pe":
                        g = turn(eng, "rank", "rpos", n)
                        need(eng, "racc", n)
                        eng.matmul(g[:, 0:2 * NE], lstrict[:, :], hot[:, :, :].rearrange("p b e -> p (b e)"),
                                   start=True, stop=False)
                        done(eng.matmul(g[:, 0:2 * NE], ones_b[:, :], acc2[:, :, :].rearrange("p b e -> p (b e)"),
                                        start=False, stop=True), "rank")
                if piece == 5:
                    if e == "dve":
                        need(eng, "rank", n)
                        done(eng.tensor_tensor(f("pos"), given("rank")[:, 0:2 * NE].rearrange("p (b e) -> p b e", e=NE),
                                               ebase[:, :, :], ALU.add), "rpos")
                        need(eng, "rpos", n)
                        step(eng.tensor_tensor(f("m1"), f("oh1"), f("pos"), ALU.mult))
                        step(eng.tensor_tensor(f("m2"), f("oh2"), f("pos"), ALU.mult))
                        step(eng.tensor_reduce(rs["pos1"][:, :], f("m1"), AX.X, ALU.add))
                        step(eng.tensor_reduce(rs["pos2"][:, :], f("m2"), AX.X, ALU.add))
                        need_dma(eng, "scat", 4 * p)
                        eng.tensor_copy(idx[:, 0, :], rs["pos1"][:, :])
                        done(eng.tensor_copy(idx[:, 1, :], rs["pos2"][:, :]), "ridx")
                    if e == "pool":
                        need(eng, "ridx", n)
                        for b in range(2):
                            need(eng, f"rl{b}", n)
                            settle(eng)
                            for i in range(2):
                                landed(eng.indirect_dma_start(
                                    xrec_d[:, :], bass.IndirectOffsetOnAxis(ap=idx[:, i, b:b + 1], axis=0),
                                    rec[:, b, :], None), "scat")
            return go

        def weights(which, piece):
            def go(e, eng, p):
                n = p + 1
                ex = p if which == 1 else p - NE
                if piece == 1:
                    if e == "sp":
                        need(eng, "wlo", p)
                        src = (w1[bass.ds(ex, 1), :, :].rearrange("o (k q) h -> q (o k) h", q=P) if which == 1
                               else w2[bass.ds(ex, 1), :, :].rearrange("o (k q) h -> q (o k) h", q=P))
                        dst = wl[:, :].rearrange("q (k h) -> q k h", k=DC if which == 1 else HC)
                        landed(eng.dma_start(dst, src), "ldw")
                    if e == "act":
                        need_dma(eng, "ldw", n)
                        if which == 2:
                            need_dma(eng, "stw", ex + 1)
                        done(eng.activation(wst[:, 0, :], wl[:, :], ACT.Square, accum_out=wss[:, :]), "wss")
                    if e == "pe":
                        g = turn(eng, "wsum", "wcl", n)
                        need(eng, "wss", n)
                        done(eng.matmul(g[:, 0:1], ones_f[:, :], wss[:, :], start=True, stop=True), "wsum")
                    if e == "dve":
                        dst = (k1 if which == 1 else k2)
                        need(eng, "wsum", n)
                        done(eng.tensor_scalar(wcl[:, :], given("wsum")[:, 0:1], 2.0 ** -60, None, ALU.max), "wcl")
                        need(eng, "wcl", n)
                        exponent(eng, wcl[:, :], wkk[:, :])
                        eng.tensor_copy(dst[:, bass.ds(ex, 1)], wkk[:, :])
                        done(eng.tensor_scalar(wsc[:, :], wkk[:, :], -float(ONE), 268.0 * ONE, ALU.mult, ALU.add), "wsc")
                hi = (w1s[:, bass.ds(ex, 1), 0, :, :].rearrange("p o k h -> p (o k h)") if which == 1 else wst[:, 0, :])
                lo = (w1s[:, bass.ds(ex, 1), 1, :, :].rearrange("p o k h -> p (o k h)") if which == 1 else wst[:, 1, :])
                if piece == 2:
                    if e == "act":
                        need(eng, "wsc", n)
                        need(eng, "wss", n)
                        done(eng.activation(wl[:, :], wl[:, :], ACT.Identity, scale=wsc[:, :].bitcast(F32)), "wscaled")
                        need(eng, "wscaled", n)
                        done(eng.activation(hi, wl[:, :], ACT.Copy), "whi")
                    if e == "pool":
                        need(eng, "whi", n)
                        if which == 2:
                            need_dma(eng, "stw", ex + 1)
                        done(eng.tensor_tensor(lo, wl[:, :], hi, ALU.subtract), "wlo")
                    if e == "sp" and which == 2:
                        need(eng, "wlo", n)
                        landed(eng.dma_start(w2s_d[bass.ds(ex, 1), :, :].rearrange("o q h -> q (o h)"),
                                             wst[:, :, :].rearrange("q s h -> q (s h)")), "stw")
            return go

        def exponent(eng, src, dst):
            step = own_steps(eng)
            step(eng.tensor_scalar(dst, src.bitcast(I32), 23, None, ALU.logical_shift_right))
            step(eng.tensor_scalar(dst, dst, 129.0, None, ALU.add))
            step(eng.tensor_scalar(dst, dst, 1, None, ALU.logical_shift_right))

        def setup(e, eng, _):
            if e == "sp":
                for dst, src in ((wq_sb, wq), (wk_sb, wk), (wv_sb, wv), (wo_sb, wo), (wr_sb, wr)):
                    landed(eng.dma_start(dst[:, :, :], src.rearrange("(k q) n -> q k n", q=P)), "set_w")
                landed(eng.dma_start(b1r[:, :], b1.rearrange("e (m q) -> (e m) q", q=P)), "set_w")
            if e == "act":
                for dst, src in (((bqk[:, 0:D], bq), (bqk[:, D:2 * D], bk), 
                                                (bv_sb[:, :], bv), (bo_sb[:, :], bo), (al[:, :], alpha))):
                    landed(eng.dma_start(dst, src.partition_broadcast(P)), "set_v")
            if e == "pe":
                need(eng, "set_pool", 2)
                need_dma(eng, "set_w", 6)
                done(eng.transpose(gen[0][:, 0:NE * HC], b1r[:, :], idf[0:NE * HC, 0:NE * HC]), "set_bt")
                need_dma(eng, "set_v", 5)
                for k in range(DC):
                    ins = eng.transpose(gen[2][:, k * P:(k + 1) * P], bv_sb[:, k * P:(k + 1) * P], idf[:, :])
                done(ins, "set_bvt")
            if e == "dve":
                eng.memset(ones_f[:, :], 1.0)
                eng.memset(ones_b[:, :], 1.0)
                eng.memset(zrow[:, :], 0.0)
                eng.memset(acc_cnt[:, :], 0.0)
                eng.memset(mhalf[:, :], -0.5)
                eng.memset(ar[:, :, :, :], 0.0)
                eng.memset(padrec[:, :], 0)
                for b in range(2):
                    eng.memset(aq[b][RROWS:RROWS + NSPLIT, :], 1.0)
                    ins = eng.memset(vz[b][:, :, :, :], 0.0)
                done(ins, "set_dve")
                need(eng, "set_dve", 1)
                for b in range(2):
                    for j in range(4):
                        vq = vz[b][:, :, :, :].rearrange("p q j m -> p q (j m)")
                        ins = eng.memset(vq[:, :, j * VM + 4 * DK + j:j * VM + 4 * DK + j + 1], 1.0)
                done(ins, "set_dve")
                need_dma(eng, "set_v", 5)
                done(eng.tensor_reduce(amax[:, :], al[:, :], AX.X, ALU.max, apply_absolute_value=True), "set_a")
                need(eng, "set_a", 1)
                done(eng.tensor_scalar(amax[:, :], amax[:, :], 2.0 ** -60, None, ALU.max), "set_a")
                need(eng, "set_a", 2)
                done(eng.tensor_scalar(abig[:, :], amax[:, :].bitcast(I32), 255 * ONE, None, ALU.bitwise_and), "set_a")
                need(eng, "set_a", 3)
                done(eng.tensor_scalar(abig[:, :], abig[:, :], float(ONE), None, ALU.add), "set_a")
                need(eng, "set_a", 4)
                eng.tensor_scalar(arec[:, :], abig[:, :], -1.0, 254.0 * ONE, ALU.mult, ALU.add)
                done(eng.tensor_scalar(escale[:, :], abig[:, :].bitcast(F32), QK_SCALE ** -2, None, ALU.mult), "set_a")
                need(eng, "set_a", 5)
                eng.memset(signs[:, 0:NH], 1.0)
                eng.memset(signs[:, NH:2 * NH], -1.0)
                eng.memset(colscale[:, NH:2 * NH], -0.5 * QK_SCALE)
                done(eng.tensor_scalar(colscale[:, 0:NH], al[:, :], arec[:, :].bitcast(F32), 0.5 * QK_SCALE,
                                       ALU.mult, ALU.mult), "set_a")
                need(eng, "set_bvt", 1)
                done(eng.tensor_copy(bv_wide[:, :, :].rearrange("p k t -> p (k t)"), gen[2][:, 0:D]), "set_bv")
                need(eng, "set_bt", 1)
                done(eng.tensor_copy(b1t[:, :, :].rearrange("p e m -> p (e m)"), gen[0][:, 0:NE * HC]), "set_b1t")
                need(eng, "set_b1t", 1)
                done(eng.tensor_tensor(b1q[:, :, :], b1t[:, :, :], b1t[:, :, :], ALU.mult), "set_b")
                need(eng, "set_b", 1)
                done(eng.tensor_reduce(b1ss[:, :], b1q[:, :, :], AX.X, ALU.add), "set_b")
                need(eng, "set_a", 6)
            if e == "pe":
                need(eng, "set_dve", 2)
                need(eng, "set_b", 2)
                done(eng.matmul(pv_ps[:, 0:NE], ones_f[:, :], b1ss[:, :], start=True, stop=True), "set_bs")
                need(eng, "set_bv", 1)
                for k in range(DC):
                    ins = eng.matmul(gen[1][:, 0:D], bv_wide[:, k, :], wo_sb[:, k, :], start=(k == 0),
                                     stop=(k == DC - 1))
                done(ins, "set_bvo")
            if e == "dve":
                need(eng, "set_bvo", 1)
                done(eng.tensor_tensor(bo_sb[:, :], gen[1][:, 0:D], bo_sb[:, :], ALU.add), "set_bo")
                need(eng, "set_bs", 1)
                done(eng.tensor_scalar(b1ss[:, :], pv_ps[:, 0:NE], 2.0 ** -60, None, ALU.max), "set_b")
                need(eng, "set_b", 3)
                exponent(eng, b1ss[:, :], kb[:, :])
            if e == "pool":
                for m in (idf, idb, id16, lstrict):
                    eng.memset(m[:, :], 0.0)
                eng.memset(uk[0][0:STRIP, :], 0.0)
                eng.iota(io8[:, :, :], [[0, 2], [REGION, NE]], base=0, channel_multiplier=0)
                eng.iota(slot_n[:, :, :], [[1, NSLOT], [0, NE]], base=0, channel_multiplier=0)
                done(eng.iota(tok[:, :], [[0, 1]], base=T, channel_multiplier=1), "set_pool")
                need(eng, "set_pool", 1)
                made = 0

                def one(ins):
                    nonlocal made
                    made += 1
                    done(ins, "set_select")
                    need(eng, "set_select", made)
                for m in (idf, idb, id16):
                    one(eng.affine_select(out=m[:, :], in_=m[:, :], compare_op=ALU.not_equal, fill=1.0, base=0,
                                          pattern=[[-1, P]], channel_multiplier=1))
                one(eng.affine_select(out=lstrict[:, :], in_=lstrict[:, :], compare_op=ALU.is_ge, fill=1.0, base=0,
                                      pattern=[[-1, P]], channel_multiplier=1))
                w = uk[0][0:STRIP, :].rearrange("r (par j k) -> r par j k", par=2, k=P)
                one(eng.affine_select(out=w, in_=w, compare_op=ALU.not_equal, fill=1.0, base=0,
                                      pattern=[[-1, 2], [-2, NH // 2], [0, P]], channel_multiplier=1))
                eng.sem_inc(sem("set_pool"), 1)
                need(eng, "set_pool", 2)
                need(eng, "set_dve", 1)
                done(eng.tensor_copy(padrec[:, D + NE:D + NE + 1], tok[:, :]), "set_pool")
                need(eng, "set_pool", 3)
                done(eng.iota(tok[:, :], [[0, 1]], base=0, channel_multiplier=1), "set_pool")
            if e == "dve":
                need(eng, "set_pool", 4)
                done(eng.tensor_copy(ebase[:, :, :], io8[:, :, :]), "set_e")
                for i in range(NE):
                    ins = eng.memset(rank8[:, :, i:i + 1], float(NE - i))
                done(ins, "set_e")
                need(eng, "set_e", 2)
            if e == "pe":
                need(eng, "set_pool", 2)
                need_dma(eng, "set_w", 6)
                need_dma(eng, "set_uk", 2 * NSPLIT - 1)
                need(eng, "set_b", 3)
                need(eng, "set_bo", 1)
            if e == "act":
                need(eng, "set_pool", 2)
                for b in range(2):
                    for i in range(b == 0, NSPLIT):
                        landed(eng.dma_start(uk[b][i * STRIP:(i + 1) * STRIP, :], uk[0][0:STRIP, :]), "set_uk")
                need(eng, "set_a", 6)
            if e == "pool":
                need(eng, "set_bo", 1)

        def spare(e, eng, _):
            if e == "sp":
                need(eng, "set_pool", 4)
                for i in range(TWO):
                    spare = NE * REGION + i * P
                    landed(eng.dma_start(xrec_d[spare:spare + P, :], padrec[:, :]), "set_pad")
                need(eng, "set_dve", 1)
                landed(eng.dma_start(out[T:T + P, :], zrow[:, :]), "set_pad")

        stages = {"rows": rows}
        for b_ in range(2):
            stages.update({f"load{b_}": load_stage(b_), f"means{b_}": means_in(b_), f"norm{b_}": norm_in(b_),
                           f"project{b_}": project(b_), f"squares{b_}": squares(b_), f"parts{b_}": parts_of(b_),
                           f"stack{b_}": stack(b_)})
            stages.update({f"back{b_}.{i}": back(b_, i) for i in range(6)})
        for n_ in halves:
            stages.update({f"factors{n_}": factors(n_), f"scores{n_}": scores(n_), f"values{n_}": values(n_)})
            stages.update({f"turned{n_}.{i}": turned(n_, i) for i in range(2)})
        stages.update({f"norms.{i}": norms(i) for i in range(1, 5)})
        stages.update({f"route.{i}": route(i) for i in range(1, 6)})

        order = {
            "pe": """
                factors0 turned3.0- turned3.1- scores0 factors1 stack1 values3- back0.2- scores1
                back1.1- back0.3- factors2 back1.2- norm1+ norm0+ turned0.0 project1+ scores2
                turned0.1 project0+ back1.3- turned1.0 back0.4- values0 turned1.1 back0.5- factors3
                back1.4- values1 weights.1 scores3 turned2.0 rows+ back1.5- turned2.1 stack0+ values2
                back0.1 route.4-""",
            "act": """
                parts1 factors0 turned3.0- turned3.1- stack1 back1.1- back0.2- factors1 back1.2-
                norm1+ norm0+ turned0.0 factors2 project1+ squares1+ turned0.1 weights.1 project0+
                squares0+ turned1.0 back0.4- norms.1+ norms.2+ turned1.1 back1.4- factors3 turned2.0
                parts0+ weights.2 back0.1 route.2- turned2.1 stack0+""",
            "dve": """
                scores0 means0+ means1+ back1.1- norm1+ norm0+ back0.3- parts1 scores1 project1+
                back0.4- scores2 project0+ squares1+ back1.3- squares0+ back1.4- norms.1+ parts0+
                norms.2+ norms.3+ norms.4+ back0.5- weights.1 rows+ scores3 back1.5- route.1- route.2-
                weights.2 route.3- route.4- route.5- back0.1""",
            "pool": """
                means0+ means1+ scores0 back0.3- back0.0 stack1 scores1 back1.0 back1.3- scores2
                back0.4- back1.4- norms.4+ stack0+ parts0+ scores3 weights.2 parts1+ route.5-""",
            "sp": """
                load0+ load1+ back1.0 back0.0 weights.1 back1.3- back0.3- rows+ weights.2""",
        }
        deltas = {"+": 1, "-": -1}
        steps = {e: [(w.rstrip("+-"), deltas.get(w[-1], 0)) for w in text.split()] for e, text in order.items()}

        def tables(e, eng):
            if e == "dve":
                k = 0

                def step(ins):
                    nonlocal k
                    k += 1
                    done(ins, "table")
                    need(eng, "table", k)
                step(eng.tensor_scalar(tiles_i[:, :], cnt_f[:, :], float(SLOT - 1), None, ALU.add))
                step(eng.tensor_scalar(tiles_i[:, :], tiles_i[:, :], SLOT.bit_length() - 1, None, ALU.logical_shift_right))
                step(eng.tensor_copy(tiles[:, :], tiles_i[:, :]))
                step(eng.memset(unit[:, :], 1.0))
                step(eng.tensor_tensor_scan(ends[:, :], unit[:, :], tiles[:, :], 0.0, ALU.mult, ALU.add))
                step(eng.tensor_copy(slot_f[:, :, :], slot_n[:, :, :]))
                each = lambda t: t[0:1, :].unsqueeze(1).to_broadcast([1, NSLOT, NE])
                step(eng.tensor_tensor(past[:, :, :], slot_f[:, :, :], each(ends), ALU.is_ge))
                step(eng.tensor_tensor(before[:, :, :], past[:, :, :], each(tiles), ALU.mult))
                step(eng.tensor_reduce(n_past[:, :], past[:, :, :], AX.X, ALU.add))
                step(eng.tensor_reduce(start[:, :], before[:, :, :], AX.X, ALU.add))
                step(eng.tensor_tensor(start[:, :], slot_f[:, :, 0], start[:, :], ALU.subtract))
                step(eng.tensor_scalar(start[:, :], start[:, :], float(SLOT), None, ALU.mult))
                step(eng.scalar_tensor_tensor(rowf[:, :], n_past[:, :], float(REGION), start[:, :], ALU.mult, ALU.add))
                step(eng.tensor_scalar(slot_row[:, :], rowf[:, :], float(NE * REGION), None, ALU.min))
                step(eng.tensor_scalar(slot_e[:, :], n_past[:, :], float(NE - 1), None, ALU.min))
                eng.sem_inc(sem("tables"), 1)
                step(eng.tensor_scalar(mk[:, :], k1[:, :], 4.0, None, ALU.add))
                step(eng.tensor_tensor(mk[:, :], mk[:, :], kb[:, :], ALU.max))
                step(eng.tensor_scalar(mk[:, :], mk[:, :], 1.0, None, ALU.add))
                step(eng.tensor_scalar(hsc[:, :], mk[:, :], -float(ONE), 268.0 * ONE, ALU.mult, ALU.add))
                step(eng.tensor_scalar(inv1[:, :], k1[:, :], 25.0, float(ONE), ALU.subtract, ALU.mult))
                step(eng.tensor_tensor(inv2[:, :], mk[:, :], k2[:, :], ALU.add))
                step(eng.tensor_scalar(inv2[:, :], inv2[:, :], 155.0, float(ONE), ALU.subtract, ALU.mult))
                eng.sem_inc(sem("scales"), 1)

        def finish_attention(e, eng, _):
            if e == "pe":
                g = turn(eng, "cnt", "cnt", 1)
                need(eng, "racc", NP)
                done(eng.matmul(g[:, 0:NE], ones_b[:, :], acc_cnt[:, :], start=True, stop=True), "cnt_ps")
            if e == "dve":
                need(eng, "cnt_ps", 1)
                done(eng.tensor_copy(cnt_f[:, :], given("cnt")[:, 0:NE]), "cnt")
                need(eng, "cnt", 1)
                done(eng.tensor_copy(cnt_i[:, :], cnt_f[:, :]), "cnt_i")
            if e == "sp" or e == "act":
                need(eng, "cnt_i", 1)
                for x_ in range(e == "act", NE, 2):
                    row = eng.value_load(cnt_i[0:1, x_:x_ + 1], min_val=0, max_val=T)
                    landed(eng.dma_start(xrec_d[bass.ds(row + x_ * REGION, SLOT), :].rearrange("(i q) w -> q i w", q=P),
                                         padrec[:, :].unsqueeze(1).to_broadcast([P, TWO, REC])), f"pad_{e}")
                need_dma(eng, f"pad_{e}", NE // 2)
            tables(e, eng)
            if e == "pool":
                need_dma(eng, "scat", 4 * NP)
            if e == "sp":
                for b in range(2):
                    need_dma(eng, f"stx{b}", NP)
                need_dma(eng, "stw", NE + 1)
                need_dma(eng, "set_pad", TWO + 1)

        def run(e, eng, k, p, which=1, kept=(-1, 0, 1), freed=(None,) * 3):
            start_section(k, freed)
            if e == "dve":
                clear_own(eng)
            for name, d in steps[e]:
                if d in kept:
                    (weights(which, int(name[-1])) if name.startswith("weights") else stages[name])(e, eng, p + d)

        def readers(p):
            seen = []
            for q in range(2, 4):
                run("pe", Rehearsal(), None, q)
                seen.append(Turns.freed)
            return [(name, (n1 - n0) * (p - 2) + n0) for (name, n0), (_, n1) in zip(*seen)]

        def program(e, eng):
            for chain, names in chains.items():
                if e == owner(chain):
                    eng.sem_inc(sem(chain), len(names))
            if e == "sp":
                eng.sem_inc(sem("stw"), 16)
            setup(e, eng, 0)
            run(e, eng, 0, -1, kept=(1,))
            spare(e, eng, 0)
            run(e, eng, 1, 0, kept=(0, 1), freed=Turns.freed)
            if e == "pe":
                for reader in Turns.freed:
                    need(eng, *reader)
            run(e, eng, 2, 1)
            with eng.Fori(2, NE) as p:
                run(e, eng, 3, p, freed=readers(p - 1))
            with eng.Fori(0, NP - 1 - NE) as q:
                run(e, eng, 4, q + NE, which=2, freed=readers(q + (NE - 1)))
            run(e, eng, 5, NP - 1, which=2, kept=(-1, 0), freed=readers(NP - 2))
            run(e, eng, 6, NP, kept=(-1,), freed=Turns.freed)
            finish_attention(e, eng, 0)

        with nc.Block() as block:
            @block.tensor
            def _(eng): program("pe", eng)
            @block.scalar
            def _(eng): program("act", eng)
            @block.vector
            def _(eng): program("dve", eng)
            @block.gpsimd
            def _(eng): program("pool", eng)
            @block.sync
            def _(eng): program("sp", eng)

    U = 4
    AHEAD = 3
    HB = 2
    QS = HC // HB
    SLOOP = (NSLOT - AHEAD - 1) // U * U
    with ExitStack() as f:
        w2s = alloc(f, "w2s_sb", [P, NE, 2, HC, D], F16)
        b2s = alloc(f, "b2s", [P, NE, D], F32)
        rb = [alloc(f, f"rb{i}", [P, TWO, REC], I32) for i in range(U)]
        xt = [alloc(f, f"xt{i}", [P, 2, DC, SLOT], F16) for i in range(2)]
        h32 = [alloc(f, f"h32_{i}", [P, HB, SLOT], F32) for i in range(HC // HB)]
        hs = [alloc(f, f"hs{i}", [P, 2, HC, SLOT], F16) for i in range(2)]
        yw = [alloc(f, f"yw{i}", [P, TWO, D], F32) for i in range(2)]
        yb = alloc(f, "yb", [P, TWO, D], F32)
        hbank = [s_ps[:, 0, :], s_ps[:, 1, :], u_ps[:, 0:512], u_ps[:, 512:1024]]
        ybank = [pv_ps, gen[2]]

        def expert_of(eng, s):
            return eng.value_load(slot_e[0:1, bass.ds(s, 1)], min_val=0, max_val=NE - 1)

        def slot(i, j):
            i, j = i + j // U, j % U
            return U * i + j, i, j

        def load_records(e, eng, i, j):
            if e == "sp":
                s, i, j = slot(i, j)
                need_dma(eng, f"add{j}", TWO * i)
                row = eng.value_load(slot_row[0:1, bass.ds(s, 1)], min_val=0, max_val=NE * REGION)
                landed(eng.dma_start(rb[j][:, :, :], xrec_d[bass.ds(row, SLOT), :].rearrange("(i q) w -> q i w", q=P)),
                       f"ldrec{j}")

        def turn_records(e, eng, i, j):
            s, i, j = slot(i, j)
            g = gen[j % 2][:, :].bitcast(F16).rearrange("p (a i t) -> p a i t", i=TWO, t=P)
            if e == "pe":
                need_dma(eng, f"ldrec{j}", i + 1)
                need(eng, "xte", s - 1)
                for a_ in range(2 * DC):
                    for i_ in range(TWO):
                        ins = eng.transpose(g[:, a_, i_, :], rb[j][:, i_, :].bitcast(F16)[:, a_ * P:(a_ + 1) * P],
                                            id16[:, :])
                done(ins, "xtp")
            if e == "dve":
                need(eng, "xtp", s + 1)
                need(eng, "mm1", QS * (s - 1))
                done(eng.tensor_copy(xt[j % 2][:, :, :, :].rearrange("p s k t -> p (s k t)"),
                                     gen[j % 2][:, :].bitcast(F16)), "xte")

        def first_product(e, eng, i, j):
            s, i, j = slot(i, j)
            ex = expert_of(eng, s) if e in ("pe", "act", "dve") else None
            for q in range(QS):
                hb = hbank[q]
                n = QS * s + q + 1
                blocks = range(q * HB, (q + 1) * HB)
                if e == "pe":
                    need(eng, "xte", s + 1)
                    need(eng, "gel", n - QS)
                    for m in blocks:
                        o = (m % HB) * SLOT
                        terms = [(k, wp, xp) for k in range(DC) for wp, xp in ((0, 0), (0, 1), (1, 0))]
                        for t, (k, wp, xp) in enumerate(terms):
                            w = w1s[:, bass.ds(ex, 1), wp, k, m * P:(m + 1) * P].rearrange("p o h -> p (o h)")
                            ins = eng.matmul(hb[:, o:o + SLOT], w, xt[j % 2][:, xp, k, :],
                                             start=(t == 0), stop=(t == len(terms) - 1))
                    done(ins, "mm1")
                if e == "act":
                    need(eng, "mm1", n)
                    need(eng, "lo", n - QS)
                    for m in blocks:
                        o = (m % HB) * SLOT
                        ins = eng.activation(h32[q][:, m % HB, :], hb[:, o:o + SLOT], ACT.Gelu,
                                             scale=inv1[:, bass.ds(ex, 1)].bitcast(F32),
                                             bias=b1t[:, bass.ds(ex, 1), m])
                    done(ins, "gel")
                if e == "dve":
                    need(eng, "gel", n)
                    need(eng, "mm2", s - 1)
                    hi = hs[j % 2][:, 0, blocks[0]:blocks[-1] + 1, :].rearrange("p m t -> p (m t)")
                    lo = hs[j % 2][:, 1, blocks[0]:blocks[-1] + 1, :].rearrange("p m t -> p (m t)")
                    h = h32[q][:, :, :].rearrange("p m t -> p (m t)")
                    scale = hsc[:, bass.ds(ex, 1)].bitcast(F32)
                    done(eng.tensor_scalar(hi, h, scale, None, ALU.mult), "hi")
                    need(eng, "hi", n)
                    done(eng.scalar_tensor_tensor(lo, h, scale, hi, ALU.mult, ALU.subtract), "lo")

        def second_product(e, eng, i, j):
            s, i, j = slot(i, j)
            ex = expert_of(eng, s) if e in ("pe", "dve") else None
            y = ybank[j % 2][:, :].rearrange("p (i d) -> p i d", i=TWO)
            if e == "pe":
                need(eng, "w2_ready", ex + 1)
                need(eng, "yb", s - 1)
                for i_ in range(TWO):
                    for m in range(HC):
                        if m % HB == 0:
                            need(eng, "lo", QS * s + m // HB + 1)
                        for t, (wp, hp) in enumerate(((0, 0), (0, 1), (1, 0))):
                            w = w2s[:, bass.ds(ex, 1), wp, m, :].rearrange("p o d -> p (o d)")
                            ins = eng.matmul(y[:, i_, :], hs[j % 2][:, hp, m, i_ * P:(i_ + 1) * P], w,
                                             start=(m == 0 and t == 0), stop=(m == HC - 1 and t == 2))
                done(ins, "mm2")
            if e == "dve":
                need(eng, "mm2", s + 1)
                need_dma(eng, "ldb2", 1)
                need(eng, "yw", s)
                done(eng.scalar_tensor_tensor(yb[:, :, :], y, inv2[:, bass.ds(ex, 1)].bitcast(F32),
                                              b2s[:, bass.ds(ex, 1), :].to_broadcast([P, TWO, D]),
                                              ALU.mult, ALU.add), "yb")
                need(eng, "yb", s + 1)
                need_dma(eng, f"add{(j - 2) % U}", TWO * (i + (1 if j >= 2 else 0)))
                for i_ in range(TWO):
                    ins = eng.tensor_scalar(yw[j % 2][:, i_, :], yb[:, i_, :],
                                            rb[j][:, i_, D:D + NE].bitcast(F32)[:, bass.ds(ex, 1)], None, ALU.mult)
                done(ins, "yw")
            if e == "pool":
                need(eng, "yw", s + 1)
                need_dma(eng, f"add{(j - 1) % U}", TWO * (i + (1 if j >= 1 else 0)))
                for i_ in range(TWO):
                    need_dma(eng, f"add{j}", TWO * i + i_)
                    settle(eng)
                    landed(eng.indirect_dma_start(
                        out[:, :], bass.IndirectOffsetOnAxis(ap=rb[j][:, i_, D + NE:D + NE + 1], axis=0),
                        yw[j % 2][:, i_, :], None, compute_op=ALU.add), f"add{j}")

        def load_w2(e, eng):
            for i in range(NE):
                if e == "sp":
                    landed(eng.dma_start(w2s[:, i, :, :, :].rearrange("q s k d -> q (s k d)"), w2s_d[i, :, :]),
                           f"ldw2_{i}")
                    if i == 0:
                        landed(eng.dma_start(b2s[:, :, :], b2.partition_broadcast(P)), "ldb2")
            for i in range(NE):
                if e == "pool":
                    need_dma(eng, f"ldw2_{i}", 1)
                    eng.sem_inc(sem("w2_ready"), 1)

        def slots(e, eng):
            need(eng, "tables", 1)
            need(eng, "scales", 1)
            for j in range(AHEAD):
                load_records(e, eng, 0, j)
            load_w2(e, eng)
            turn_records(e, eng, 0, 0)
            turn_records(e, eng, 0, 1)
            first_product(e, eng, 0, 0)

            def one(i, j, rest):
                if rest >= AHEAD:
                    load_records(e, eng, i, j + AHEAD)
                if rest >= 2:
                    turn_records(e, eng, i, j + 2)
                if rest >= 1:
                    first_product(e, eng, i, j + 1)
                second_product(e, eng, i, j)

            for j in range(U):
                one(0, j, NSLOT)
            with eng.Fori(1, SLOOP // U) as i:
                for j in range(U):
                    one(i, j, NSLOT)
            for s in range(SLOOP, NSLOT):
                one(s // U, s % U, NSLOT - 1 - s)
            if e == "pool":
                for j in range(U):
                    need_dma(eng, f"add{j}", TWO * ((NSLOT - 1 - j) // U + 1))

        with nc.Block() as block:
            @block.tensor
            def _(eng): slots("pe", eng)
            @block.scalar
            def _(eng): slots("act", eng)
            @block.vector
            def _(eng): slots("dve", eng)
            @block.gpsimd
            def _(eng): slots("pool", eng)
            @block.sync
            def _(eng): slots("sp", eng)


INPUTS = ["x", "ctx_1024", "L0_xattn_Wq", "L0_xattn_bq", "L0_xattn_Wk", "L0_xattn_bk", "L0_xattn_Wv", "L0_xattn_bv",
          "L0_xattn_Wo", "L0_xattn_bo", "L0_xattn_alpha", "L0_ffn_Wr", "L0_ffn_W1", "L0_ffn_b1", "L0_ffn_W2",
          "L0_ffn_b2"]


def kernel(**inputs):
    from concourse import bacc
    from concourse.bass_utils import run_bass_kernel_spmd

    nc = bacc.Bacc("TRN2", target_bir_lowering=False, num_devices=1)
    arrays, args = {}, []
    for name in INPUTS:
        a = np.asarray(inputs[name])
        shape = (T, D) if name in ("x", "ctx_1024") else (NH,) if name == "L0_xattn_alpha" else a.shape
        arrays[name] = np.ascontiguousarray(a.reshape(shape))
        args.append(nc.dram_tensor(name, shape, F32, kind="ExternalInput").ap())
    args.append(nc.dram_tensor("out", (T + P, D), F32, kind="ExternalOutput").ap())
    with ExitStack() as ctx:
        build(nc, ctx, args)
    result = run_bass_kernel_spmd(nc, [arrays], core_ids=[0])
    return result.results[0]["out"][:T].reshape(NB, P, D)
```
